# Optimizing a Trainium2 kernel written in Bass

```python
import numpy as np
import jax
import jax.numpy as jnp

def _softmax(x, axis=-1):
    return jax.nn.softmax(x, axis=axis)

def _gelu(x):
    return jax.nn.gelu(x, approximate=True)

def _silu(x):
    return jax.nn.silu(x)

def _sigmoid(x):
    return jax.nn.sigmoid(x)

def _layernorm(x, axis=-1, eps=1e-05):
    m = jnp.mean(x, axis=axis, keepdims=True)
    v = jnp.var(x, axis=axis, keepdims=True)
    return (x - m) / jnp.sqrt(v + eps)

def _scatter_add(tgt, idx, src, axis=0):
    return tgt.at[idx].add(src)

def _segment_sum(src, seg, n):
    return jax.ops.segment_sum(src, seg, n)
kernel_name = 'mk_gnn_preln_d2_gnn_r32_42a811'

def setup_inputs(seed: int=0):
    np.random.seed(seed)
    _w = jnp.asarray

    def _rec_inputs():
        import jax
        import jax.numpy as jnp
        _gk = jax.random.key(seed)
        x = -0.0006008 + 1.001 * jax.random.normal(jax.random.fold_in(_gk, 1), (3125, 256), jnp.float32)
        src = jax.random.randint(jax.random.fold_in(_gk, 2), (50000,), 0, 3125, jnp.int32)
        dst = jnp.minimum((3125 * jax.random.uniform(jax.random.fold_in(_gk, 3), (50000,)) ** 2.0).astype(jnp.int32), 99999)
        _o = jnp.argsort(dst, stable=True)
        src = src[_o]
        dst = dst[_o]
        edge_attr_64 = 0.000312547 + 1.00004 * jax.random.normal(jax.random.fold_in(_gk, 11), (50000, 64), jnp.float32)
        edge_type_64 = jax.random.randint(jax.random.fold_in(_gk, 13), (50000,), 0, 64, jnp.int32)
        return (x, src, dst, edge_attr_64, edge_type_64)
    x, src, dst, edge_attr_64, edge_type_64 = _rec_inputs()

    def _L0_gnn_setup():
        import jax, jax.numpy as jnp
        import numpy as np
        N, E, H, DE = (10000, 250000, 256, 64)
        EPS = 1e-05

        def _lin_init(k, fan_in, shape):
            s = 1.0 / np.sqrt(fan_in)
            return jax.random.uniform(k, shape, jnp.float32, -s, s)
        key = jax.random.key(seed)
        ks = jax.random.split(key, 12)
        x = jax.random.normal(ks[0], (N, H), jnp.float32)
        edge_index = jax.random.randint(ks[1], (2, E), 0, N)
        edge_attr = jax.random.normal(ks[2], (E, DE), jnp.float32)
        d_in = H + DE
        W1 = _lin_init(ks[3], d_in, (d_in, H))
        b1 = _lin_init(ks[4], d_in, (H,))
        W2 = _lin_init(ks[5], H, (H, H))
        b2 = _lin_init(ks[6], H, (H,))
        Wg = _lin_init(ks[7], d_in, (d_in, H))
        bg = _lin_init(ks[8], d_in, (H,))
        gamma = jnp.ones((H,), jnp.float32)
        beta = jnp.zeros((H,), jnp.float32)
        return {'x': x, 'edge_index': edge_index, 'edge_attr': edge_attr, 'W1': W1, 'b1': b1, 'W2': W2, 'b2': b2, 'Wg': Wg, 'bg': bg, 'gamma': gamma, 'beta': beta}
    _L0_gnn_all = _L0_gnn_setup()
    _L0_gnn_in = {k: v for k, v in _L0_gnn_all.items() if k in ('W1', 'b1', 'W2', 'b2', 'Wg', 'bg', 'gamma', 'beta')}
    del _L0_gnn_all

    def _L1_gnn_setup():
        import jax, jax.numpy as jnp
        import numpy as np
        N_NODES = 50000
        N_EDGES = 15625
        IN_DIM = 256
        HID = 64
        HEADS = 4
        N_REL = 64
        key = jax.random.key(seed)
        ks = jax.random.split(key, 16)
        s = 0.02
        return {'node_features': jax.random.normal(ks[0], (N_NODES, IN_DIM), jnp.float32), 'edge_index': jax.random.randint(ks[1], (2, N_EDGES), 0, N_NODES, jnp.int32), 'edge_relations': jax.random.randint(ks[2], (N_EDGES,), 0, N_REL, jnp.int32), 'query_emb': jax.random.normal(ks[3], (IN_DIM,), jnp.float32), 'Wq': jax.random.normal(ks[4], (IN_DIM, HID * HEADS), jnp.float32) * s, 'bq': jnp.zeros((HID * HEADS,), jnp.float32), 'Wk': jax.random.normal(ks[5], (IN_DIM, HID * HEADS), jnp.float32) * s, 'bk': jnp.zeros((HID * HEADS,), jnp.float32), 'Wv': jax.random.normal(ks[6], (IN_DIM, HID * HEADS), jnp.float32) * s, 'bv': jnp.zeros((HID * HEADS,), jnp.float32), 'rel_w': jax.random.normal(ks[7], (N_REL, HID), jnp.float32) * s, 'Wo': jax.random.normal(ks[8], (HID * HEADS, IN_DIM), jnp.float32) * s, 'bo': jnp.zeros((IN_DIM,), jnp.float32), 'gamma': jnp.ones((IN_DIM,), jnp.float32), 'beta': jnp.zeros((IN_DIM,), jnp.float32)}
    _L1_gnn_all = _L1_gnn_setup()
    _L1_gnn_in = {k: v for k, v in _L1_gnn_all.items() if k in ('query_emb', 'Wq', 'bq', 'Wk', 'bk', 'Wv', 'bv', 'rel_w', 'Wo', 'bo', 'gamma', 'beta')}
    del _L1_gnn_all
    return {'x': x, 'src': src, 'dst': dst, 'edge_attr_64': edge_attr_64, 'edge_type_64': edge_type_64, 'L0_gnn_W1': _L0_gnn_in['W1'], 'L0_gnn_b1': _L0_gnn_in['b1'], 'L0_gnn_W2': _L0_gnn_in['W2'], 'L0_gnn_b2': _L0_gnn_in['b2'], 'L0_gnn_Wg': _L0_gnn_in['Wg'], 'L0_gnn_bg': _L0_gnn_in['bg'], 'L0_gnn_gamma': _L0_gnn_in['gamma'], 'L0_gnn_beta': _L0_gnn_in['beta'], 'L1_gnn_query_emb': _L1_gnn_in['query_emb'], 'L1_gnn_Wq': _L1_gnn_in['Wq'], 'L1_gnn_bq': _L1_gnn_in['bq'], 'L1_gnn_Wk': _L1_gnn_in['Wk'], 'L1_gnn_bk': _L1_gnn_in['bk'], 'L1_gnn_Wv': _L1_gnn_in['Wv'], 'L1_gnn_bv': _L1_gnn_in['bv'], 'L1_gnn_rel_w': _L1_gnn_in['rel_w'], 'L1_gnn_Wo': _L1_gnn_in['Wo'], 'L1_gnn_bo': _L1_gnn_in['bo'], 'L1_gnn_gamma': _L1_gnn_in['gamma'], 'L1_gnn_beta': _L1_gnn_in['beta']}

def reference(x, src, dst, edge_attr_64, edge_type_64, L0_gnn_W1, L0_gnn_b1, L0_gnn_W2, L0_gnn_b2, L0_gnn_Wg, L0_gnn_bg, L0_gnn_gamma, L0_gnn_beta, L1_gnn_query_emb, L1_gnn_Wq, L1_gnn_bq, L1_gnn_Wk, L1_gnn_bk, L1_gnn_Wv, L1_gnn_bv, L1_gnn_rel_w, L1_gnn_Wo, L1_gnn_bo, L1_gnn_gamma, L1_gnn_beta):
    import jax
    import jax.numpy as jnp

    def _L0_gnn_ref(x, edge_index, edge_attr, W1, b1, W2, b2, Wg, bg, gamma, beta):
        import jax, jax.numpy as jnp
        import numpy as np
        N, E, H, DE = (10000, 250000, 256, 64)
        EPS = 1e-05

        def _lin_init(k, fan_in, shape):
            s = 1.0 / np.sqrt(fan_in)
            return jax.random.uniform(k, shape, jnp.float32, -s, s)
        src, dst = (edge_index[0], edge_index[1])
        ei = jnp.concatenate([x[src], edge_attr], axis=-1)
        core = jnp.maximum(ei @ W1 + b1, 0.0) @ W2 + b2
        gate = jax.nn.sigmoid(ei @ Wg + bg)
        msg = gate * core
        agg = jax.ops.segment_sum(msg, dst, num_segments=x.shape[0])
        out = agg + x
        mu = jnp.mean(out, axis=-1, keepdims=True)
        var = jnp.var(out, axis=-1, keepdims=True)
        out = (out - mu) * jax.lax.rsqrt(var + EPS) * gamma + beta
        return out

    def _L1_gnn_ref(node_features, edge_index, edge_relations, query_emb, Wq, bq, Wk, bk, Wv, bv, rel_w, Wo, bo, gamma, beta):
        import jax, jax.numpy as jnp
        import numpy as np
        N_NODES = 50000
        N_EDGES = 15625
        IN_DIM = 256
        HID = 64
        HEADS = 4
        N_REL = 64
        N = node_features.shape[0]
        D = rel_w.shape[1]
        H = Wq.shape[1] // D
        enh = node_features + 0.1 * query_emb[None, :]
        Q = (enh @ Wq + bq).reshape(N, H, D)
        K = (enh @ Wk + bk).reshape(N, H, D)
        V = (enh @ Wv + bv).reshape(N, H, D)
        src, dst = (edge_index[0], edge_index[1])
        rel = rel_w[edge_relations]
        mod_k = K[src] + 0.2 * rel[:, None, :]
        scores = jnp.einsum('ehd,ehd->eh', Q[dst], mod_k) / D ** 0.5
        seg_max = jax.ops.segment_max(scores, dst, num_segments=N)
        ex = jnp.exp(scores - seg_max[dst])
        denom = jax.ops.segment_sum(ex, dst, num_segments=N)
        w = ex / denom[dst]
        agg = jax.ops.segment_sum(w[:, :, None] * V[src], dst, num_segments=N)
        deg = jax.ops.segment_sum(jnp.ones((src.shape[0],), jnp.float32), dst, num_segments=N)
        msgs = jnp.where(deg[:, None, None] > 0, agg, V)
        out = msgs.reshape(N, H * D) @ Wo + bo
        x = out + node_features
        mu = jnp.mean(x, axis=-1, keepdims=True)
        var = jnp.var(x, axis=-1, keepdims=True)
        return (x - mu) / jnp.sqrt(var + 1e-05) * gamma + beta
    edge_index = jnp.stack([src, dst])
    h = jnp.maximum(_layernorm(x, axis=-1), 0.0)
    x = x + _L0_gnn_ref(h, edge_index, edge_attr_64, L0_gnn_W1, L0_gnn_b1, L0_gnn_W2, L0_gnn_b2, L0_gnn_Wg, L0_gnn_bg, L0_gnn_gamma, L0_gnn_beta)
    h = jnp.maximum(_layernorm(x, axis=-1), 0.0)
    x = x + _L1_gnn_ref(h, edge_index, edge_type_64, L1_gnn_query_emb, L1_gnn_Wq, L1_gnn_bq, L1_gnn_Wk, L1_gnn_bk, L1_gnn_Wv, L1_gnn_bv, L1_gnn_rel_w, L1_gnn_Wo, L1_gnn_bo, L1_gnn_gamma, L1_gnn_beta)
    return x

_drawn_inputs = setup_inputs


def setup_inputs(seed=0):
    import zlib

    import numpy as np

    out = dict(_drawn_inputs(seed))
    spreads = {'L0_gnn_gamma': (1.0, 0.2),
     'L0_gnn_beta': (0.0, 0.1),
     'L1_gnn_bq': (0.0, 0.8),
     'L1_gnn_bk': (0.0, 0.8),
     'L1_gnn_bv': (0.0, 0.429),
     'L1_gnn_bo': (0.0, 0.1),
     'L1_gnn_gamma': (1.0, 0.2),
     'L1_gnn_beta': (0.0, 0.1)}
    factors = {'L0_gnn_bg': 7.728,
     'L1_gnn_query_emb': 8.0,
     'L1_gnn_Wq': 8.0,
     'L1_gnn_Wk': 8.0,
     'L1_gnn_rel_w': 8.0}
    for name, (base, spread) in spreads.items():
        noise = np.random.default_rng([zlib.crc32(name.encode()), seed]).standard_normal(out[name].shape)
        drawn = base * np.exp(spread * noise) if base else spread * noise
        out[name] = jnp.asarray(drawn.astype(out[name].dtype))
    for name, factor in factors.items():
        out[name] = (out[name] * factor).astype(out[name].dtype)
    return out
```

```python
import concourse.bass as bass
from concourse import mybir
from contextlib import ExitStack

NODES, EDGES, HID, EDGE_DIM, RELS, HEADS = 3125, 50000, 256, 64, 64, 4
P = 128
HEAD = HID // HEADS
CHUNK = 256
CHUNKS = -(-EDGES // CHUNK)
WINDOWS = -(-NODES // P)
WPAD = WINDOWS + WINDOWS % 2
BLOCKS = CHUNKS + WINDOWS - 1
HALF_C = CHUNKS // 2
HALF_B = BLOCKS // 2
NO_NODE = 4096
FAR = 8192.0
BIG = 1e30
EPS = 1e-5
SLOTS = 4
AGGW = HID + HEADS
assert CHUNKS % 2 == 0 and BLOCKS % SLOTS == 0


def build(nc, x, src, dst, etype, ea, w1, wg, b_cat, w2, b2_col, ln0, query_col, wqkv, b_qkv, rel, wo, b_o, ln1, out):
    f32, i32, f32r, bf16 = mybir.dt.float32, mybir.dt.int32, mybir.dt.float32r, mybir.dt.bfloat16
    ALU, ACT, AX = mybir.AluOpType, mybir.ActivationFunctionType, mybir.AxisListType
    ds = bass.ds

    edge_in_tab = nc.dram_tensor("edge_in_tab", (WPAD * P, 2 * HID), f32, kind="Internal").ap()
    k_tab = nc.dram_tensor("k_tab", (WPAD * P, 2 * HID), f32, kind="Internal").ap()
    v_tab = nc.dram_tensor("v_tab", (WPAD * P, HID), f32, kind="Internal").ap()
    row_tab = nc.dram_tensor("row_tab", (BLOCKS, 2 * CHUNK), bf16, kind="Internal").ap()

    ctx = ExitStack()
    with ctx:
        def sem(name):
            return ctx.enter_context(nc.semaphore(name))

        def sems(name, n):
            return [sem(f"{name}{i}") for i in range(n)]

        def sb(where, name, shape, dt):
            return where.enter_context(nc.sbuf_tensor(name, shape, dt))

        xs = sb(ctx, "xs", [P, WPAD, HID], f32)
        hs = sb(ctx, "hs", [P, WPAD, HID], f32)
        ident = sb(ctx, "ident", [P, P], f32)
        ident_r = sb(ctx, "ident_r", [P, P], f32r)
        iota_node = sb(ctx, "iota_node", [P, P], f32)
        iota_part = sb(ctx, "iota_part", [P, 1], f32)
        eps_col = sb(ctx, "eps_col", [P, 1], f32)
        stats = sb(ctx, "stats", [P, WPAD, 6], f32)
        mean_var = sb(ctx, "mean_var", [P, WPAD, 2], f32)
        std = sb(ctx, "std", [P, WPAD], f32)
        rstd = sb(ctx, "rstd", [P, WPAD], f32)
        shift = sb(ctx, "shift", [P, WPAD], f32)
        src_col = sb(ctx, "src_col", [P, BLOCKS, 2], i32)
        rel_col = sb(ctx, "rel_col", [P, BLOCKS, 2], f32)
        dst_row = sb(ctx, "dst_row", [HALF_B, 2, CHUNK], f32)
        chunk_i = sb(ctx, "chunk_i", [1, BLOCKS], i32)
        win_i = sb(ctx, "win_i", [1, BLOCKS], i32)
        ends_row = sb(ctx, "ends_row", [HEADS, 2, BLOCKS], f32)
        idx = sb(ctx, "idx", [P, SLOTS, 2], i32)
        h_t = sb(ctx, "h_t", [P, 2, 2, P], f32)
        ln0_sb = sb(ctx, "ln0_sb", [P, 2, HID], f32)
        query_sb = sb(ctx, "query_sb", [P, 2], f32)
        gath = sb(ctx, "gath", [P, SLOTS, 2, 2 * HID], f32)

        l0 = ExitStack()
        with l0:
            w_node = sb(l0, "w_node", [P, 2, 2 * HID], f32)
            w_edge = sb(l0, "w_edge", [P, 2 * HID], f32)
            w_edge_hi = sb(l0, "w_edge_hi", [P, 2 * HID], f32r)
            w_edge_lo = sb(l0, "w_edge_lo", [P, 2 * HID], f32r)
            w2_sb = sb(l0, "w2_sb", [P, 2, HID], f32)
            w2_hi = sb(l0, "w2_hi", [P, 2, HID], f32r)
            w2_lo = sb(l0, "w2_lo", [P, 2, HID], f32r)
            b_cat_sb = sb(l0, "b_cat_sb", [P, 2 * HID], f32)
            b2_sb = sb(l0, "b2_sb", [P, 2], f32)
            node_row = sb(l0, "node_row", [P, 2, 2 * HID], f32)
            ea_in = sb(l0, "ea_in", [P, SLOTS, CHUNK], f32)
            ea_parts = sb(l0, "ea_parts", [P, SLOTS, CHUNK], f32r)
            relu_hi = sb(l0, "relu_hi", [P, 2, 2 * CHUNK], f32r)
            relu_lo = sb(l0, "relu_lo", [P, 2, 2 * CHUNK], f32r)
            gate = sb(l0, "gate", [P, 2, 2, CHUNK], f32)
            msg_t = sb(l0, "msg_t", [P, 2, 2, CHUNK], f32)
            msg_hi = sb(l0, "msg_hi", [P, 2, 2, HID], f32r)
            msg_lo = sb(l0, "msg_lo", [P, 2, 2, HID], f32r)
            hot = sb(l0, "hot", [P, 2, 2, P], f32r)
            nat_i = sb(l0, "nat_i", [HALF_C, 3, 2, CHUNK], i32)
            nat_f = sb(l0, "nat_f", [HALF_C, 3, 2, CHUNK], f32)
            ends_i = sb(l0, "ends_i", [HALF_C, 3, 2], i32)
            ends_w = sb(l0, "ends_w", [HALF_C, 3, 2], f32)
            count = sb(l0, "count", [HALF_C, 2], f32)
            jump = sb(l0, "jump", [HALF_C, 2], f32)
            first_b = sb(l0, "first_b", [HALF_C, 2], f32)
            last_b = sb(l0, "last_b", [HALF_C, 2], f32)
            iota_b = sb(l0, "iota_b", [HALF_C, BLOCKS], f32)
            upto = sb(l0, "upto", [HALF_C, HALF_C], f32)
            ones_c = sb(l0, "ones_c", [HALF_C, CHUNK], f32)
            passed = sb(l0, "passed", [HALF_C, 2, BLOCKS], f32)
            chosen = sb(l0, "chosen", [HALF_C, 2, BLOCKS], f32)
            win_f = sb(l0, "win_f", [1, BLOCKS], f32)
            neg_off = sb(l0, "neg_off", [1, BLOCKS], f32)
            row_b = sb(l0, "row_b", [HALF_B, 2, 2, CHUNK], bf16)

        l1 = ExitStack()
        with l1:
            agg = sb(l1, "agg", [P, WINDOWS, AGGW], f32)
            exp_col = sb(l1, "exp_col", [P, BLOCKS, 2, HEADS], f32)
            rel_parts = sb(l1, "rel_parts", [P, HID], f32r)
            rel_sb = sb(l1, "rel_sb", [P, HEAD], f32)
            wo_sb = sb(l1, "wo_sb", [P, 2, HID], f32)
            qt = ExitStack()
            with qt:
                q_hi = sb(qt, "q_hi", [P, WPAD, HID], f32r)
                q_lo = sb(qt, "q_lo", [P, WPAD, HID], f32r)
                a0 = ExitStack()
                with a0:
                    wqkv_sb = sb(a0, "wqkv_sb", [P, 2, 3 * HID], f32)
                    b_qkv_sb = sb(a0, "b_qkv_sb", [P, 3 * HID], f32)
                    qkv_row = sb(a0, "qkv_row", [P, 2, 3 * HID], f32)
                    k_parts = sb(a0, "k_parts", [P, 2, 2, HID], f32r)
                a1 = ExitStack()
                with a1:
                    spread = sb(a1, "spread", [2, P], bf16)
                    block_row = sb(a1, "block_row", [2, SLOTS, 2, CHUNK], bf16)
                    hot_t = sb(a1, "hot_t", [P, 2, 2, CHUNK], f32r)
                    key_sb = sb(a1, "key_sb", [P, 2, 2, HID], f32)
                    prod = sb(a1, "prod", [P, 2, 2 * HID], f32)
            a2 = ExitStack()
            with a2:
                s_row = sb(a2, "s_row", [HALF_B, 2, HEADS, CHUNK], f32)
                m_row = sb(a2, "m_row", [HALF_B, 2, HEADS, CHUNK], f32)
                reset = sb(a2, "reset", [HALF_B, 2, HEADS * CHUNK + 1], f32)
                same = sb(a2, "same", [HALF_B, 2, 2, CHUNK], f32)
                outside = sb(a2, "outside", [HALF_B, 2, CHUNK], f32)
                tmp_row = sb(a2, "tmp_row", [HALF_B, 2, CHUNK], f32)
                follows = sb(a2, "follows", [HEADS, BLOCKS], f32)
                whole = sb(a2, "whole", [HEADS, BLOCKS], f32)
                into = sb(a2, "into", [HEADS, 2, BLOCKS], f32)
                through = sb(a2, "through", [HEADS, 2, BLOCKS], f32)
                edge_max = sb(a2, "edge_max", [HEADS, 2, BLOCKS], f32)
                run_max = sb(a2, "run_max", [HEADS, 2, BLOCKS], f32)
                carry = sb(a2, "carry", [HEADS, 2, BLOCKS], f32)
                carry_col = sb(a2, "carry_col", [HALF_B, 2, 2, HEADS], f32)
            a3 = ExitStack()
            with a3:
                weighted = sb(a3, "weighted", [P, 2, 2, AGGW], f32)
                hot1 = sb(a3, "hot1", [P, 2, 2, P], f32)
                v_in = sb(a3, "v_in", [P, 2, HID], f32)
                empty = sb(a3, "empty", [P, WINDOWS, HEADS], f32)
                denom = sb(a3, "denom", [P, WINDOWS, HEADS], f32)
                inv = sb(a3, "inv", [P, WINDOWS, HEADS], f32)
                b_o_sb = sb(a3, "b_o_sb", [P, HID], f32)
                ln1_sb = sb(a3, "ln1_sb", [P, 2, HID], f32)
                y_out = sb(a3, "y_out", [P, 2, HID], f32)

        bank = [ctx.enter_context(nc.psum_tensor(f"bank{i}", [P, 512], f32)) for i in range(8)]

        nat_in, x_in, w_in, lw_in, row_out = sem("nat_in"), sem("x_in"), sem("w_in"), sem("lw_in"), sem("row_out")
        pool_step, consts, ident_r_done = sem("pool_step"), sem("consts"), sem("ident_r_done")
        d_step, a_step = sem("d_step"), sem("a_step")
        counted, cumulated, sel_ready, rows_ready, off_ready, cols_ready, meta_ready = (
            sem(n) for n in ("counted", "cumulated", "sel_ready", "rows_ready", "off_ready", "cols_ready", "meta_ready"))
        w_split = sem("w_split")
        var_done, std_done, norm_done = sem("var_done"), sem("std_done"), sem("norm_done")
        h_done, ht_ready, ht_done, proj_ready, row_ready = (
            sem(n) for n in ("h_done", "ht_ready", "ht_done", "proj_ready", "row_ready"))
        row_stored = sems("row_stored", 2)
        gath_in, ea_arrived = sems("gath_in", SLOTS), sems("ea_arrived", SLOTS)
        idx_done, ea_hi_done, ea_lo_done, z_ready, relu_hi_done, relu_lo_done, gate_done, core_ready = (
            sem(n) for n in ("idx_done", "ea_hi_done", "ea_lo_done", "z_ready", "relu_hi_done", "relu_lo_done",
                             "gate_done", "core_ready"))
        msgt_done, msg_ready, msg_hi_done, msg_lo_done, hot_done, sum_ready, sum_added = (
            sem(n) for n in ("msgt_done", "msg_ready", "msg_hi_done", "msg_lo_done", "hot_done", "sum_ready",
                             "sum_added"))
        x1_done = sem("x1_done")
        h2_done, ht2_ready, ht2_done, qkv_ready, qkv_done, k_hi_done, k_lo_done, q_hi_done, q_lo_done = (
            sem(n) for n in ("h2_done", "ht2_ready", "ht2_done", "qkv_ready", "qkv_done", "k_hi_done", "k_lo_done",
                             "q_hi_done", "q_lo_done"))
        kv_stored = sems("kv_stored", 2)
        brow_in, gath1_in = sems("brow_in", SLOTS), sems("gath1_in", SLOTS)
        idx1_done, spread_ready, hot_t_done, key_ready, key_copied, query_ready, prod_done, score_done = (
            sem(n) for n in ("idx1_done", "spread_ready", "hot_t_done", "key_ready", "key_copied", "query_ready",
                             "prod_done", "score_done"))
        srow_ready, local_done, lends_ready, carried, carry_ready, max_done, exp_done, expt_ready, weights_done = (
            sem(n) for n in ("srow_ready", "local_done", "lends_ready", "carried", "carry_ready", "max_done",
                             "exp_done", "expt_ready", "weights_done"))
        gath2_in = sems("gath2_in", SLOTS)
        idx2_done, weighted_done, wsum_done, hot1_done, agg_ready, agg_added = (
            sem(n) for n in ("idx2_done", "weighted_done", "wsum_done", "hot1_done", "agg_ready", "agg_added"))
        v_arrived, y_stored = sems("v_arrived", 2), sems("y_stored", 2)
        ow_in, mix_done, mt_ready, mt_done, o_ready, o_done, y_done = (
            sem(n) for n in ("ow_in", "mix_done", "mt_ready", "mt_done", "o_ready", "o_done", "y_done"))
        idx_seen, rel_in, rel_done, agg_zero = sem("idx_seen"), sem("rel_in"), sem("rel_done"), sem("agg_zero")

        def after(engine, signal, n):
            if not isinstance(n, int) or n > 0:
                engine.wait_ge(signal, n)

        def pipeline(engine, stages, count, body, straight=False):
            rounds = count // body

            def step(k, u):
                for stage, lag in stages:
                    if isinstance(k, int) and not 0 <= body * k + u - lag < count:
                        continue
                    stage(k + (u - lag) // body, (u - lag) % body)

            peeled = -(-(max(lag for _, lag in stages) + 2) // body)
            for k in range(peeled):
                for u in range(body):
                    step(k, u)
            if straight:
                for k in range(peeled, rounds):
                    for u in range(body):
                        step(k, u)
            else:
                with engine.Fori(peeled, rounds) as k:
                    for u in range(body):
                        step(k, u)
            for u in range(max(lag for _, lag in stages)):
                step(rounds, u)

        block = ctx.enter_context(nc.Block())

        @block.sync
        def _(sp):
            for kind, array in enumerate((src, dst, etype)):
                sp.dma_start(nat_i[:, kind, :, :], array[0:CHUNKS, :].rearrange("(g p) e -> p g e", g=2)).then_inc(nat_in, 16)
            with nc.allow_non_contiguous_dma(reason="one number a chunk"):
                sp.dma_start(ends_i[:, 2, :], dst[1:CHUNKS + 1, 0:1].rearrange("(g p) o -> p (g o)", g=2)).then_inc(nat_in, 16)
            sp.dma_start(xs[:], x.rearrange("(w p) f -> p w f", p=P)).then_inc(x_in, 16)
            sp.dma_start(w_node[:, :, 0:HID], w1[0:HID, :].rearrange("(c p) n -> p c n", p=P)).then_inc(w_in, 16)
            sp.dma_start(w_node[:, :, HID:], wg[0:HID, :].rearrange("(c p) n -> p c n", p=P)).then_inc(w_in, 16)
            sp.dma_start(b_cat_sb[:], b_cat.to_broadcast([P, 2 * HID])).then_inc(w_in, 16)
            for half in range(2):
                rows = slice(half * EDGE_DIM, (half + 1) * EDGE_DIM)
                sp.dma_start(w_edge[rows, 0:HID], w1[HID:HID + EDGE_DIM, :]).then_inc(w_in, 16)
                sp.dma_start(w_edge[rows, HID:], wg[HID:HID + EDGE_DIM, :]).then_inc(w_in, 16)
            sp.dma_start(w2_sb[:], w2.rearrange("(c p) n -> p c n", p=P)).then_inc(w_in, 16)
            sp.dma_start(b2_sb[:], b2_col).then_inc(w_in, 16)
            for i in range(2):
                sp.dma_start(ln0_sb[:, i, :], ln0[i:i + 1, :].to_broadcast([P, HID])).then_inc(lw_in, 16)
            sp.dma_start(query_sb[:], query_col).then_inc(lw_in, 16)

            sp.wait_ge(meta_ready, 1)
            for r in range(2):
                sp.dma_start(row_tab[r * HALF_B:(r + 1) * HALF_B, :], row_b[:, r, :, :].rearrange("p k e -> p (k e)")).then_inc(row_out, 16)

            def store_rows(k, q):
                sp.wait_ge(row_ready, 2 * k + q + 1)
                sp.dma_start(edge_in_tab[ds((2 * k + q) * P, P), :], node_row[:, q, :]).then_inc(row_stored[q], 16)

            pipeline(sp, [(store_rows, 0)], WPAD, 2)

            def load_edges(k, q):
                b = SLOTS * k + q
                after(sp, z_ready, b - SLOTS + 1)
                after(sp, ea_lo_done, b - SLOTS + 1)
                c = sp.value_load(chunk_i[0:1, ds(b, 1)], min_val=0, max_val=CHUNKS - 1)
                chunk = ea[ds(c, 1), :, :].rearrange("o d e -> (o d) e")
                for half in range(2):
                    sp.dma_start(ea_in[half * EDGE_DIM:(half + 1) * EDGE_DIM, q, :], chunk).then_inc(ea_arrived[q], 16)

            pipeline(sp, [(load_edges, 0)], BLOCKS, SLOTS)

            sp.wait_ge(sum_added, BLOCKS)
            sp.dma_start(wqkv_sb[:], wqkv.rearrange("(c p) n -> p c n", p=P)).then_inc(rel_in, 16)
            sp.dma_start(b_qkv_sb[:], b_qkv.to_broadcast([P, 3 * HID])).then_inc(rel_in, 16)
            for half in range(2):
                sp.dma_start(rel_sb[half * RELS:(half + 1) * RELS, :], rel).then_inc(rel_in, 16)
            sp.dma_start(wo_sb[:], wo.rearrange("(c p) n -> p c n", p=P)).then_inc(rel_in, 16)

            def store_kv(k, q):
                w = 2 * k + q
                sp.wait_ge(k_lo_done, w + 1)
                sp.wait_ge(k_hi_done, w + 1)
                sp.dma_start(k_tab[ds(w * P, P), :], k_parts[:, q, :, :].bitcast(f32).rearrange("p a f -> p (a f)")).then_inc(kv_stored[q], 16)
                sp.dma_start(v_tab[ds(w * P, P), :], qkv_row[:, q, HID:2 * HID]).then_inc(kv_stored[q], 16)

            pipeline(sp, [(store_kv, 0)], WPAD, 2)

            for q in range(2):
                sp.wait_ge(kv_stored[q], 32 * (WPAD // 2))
            sp.wait_ge(q_lo_done, WPAD)
            sp.wait_ge(row_out, 32)
            sp.wait_ge(consts, 2)

            def load_block_row(k, q):
                b = SLOTS * k + q
                after(sp, spread_ready, b - SLOTS + 1)
                sp.dma_start(block_row[0:1, q, :, :].rearrange("p k e -> p (k e)"), row_tab[ds(b, 1), :]).then_inc(brow_in[q], 16)

            pipeline(sp, [(load_block_row, 0)], BLOCKS, SLOTS)

            sp.wait_ge(weights_done, 4)
            sp.dma_start(b_o_sb[:], b_o.to_broadcast([P, HID])).then_inc(ow_in, 16)
            for i in range(2):
                sp.dma_start(ln1_sb[:, i, :], ln1[i:i + 1, :].to_broadcast([P, HID])).then_inc(ow_in, 16)
            for w in range(WINDOWS):
                q = w % 2
                after(sp, mix_done, w - 1)
                sp.dma_start(v_in[:, q, :], v_tab[w * P:(w + 1) * P, :]).then_inc(v_arrived[q], 16)
            for w in range(WINDOWS):
                rows = min(P, NODES - w * P)
                sp.wait_ge(y_done, w + 1)
                sp.dma_start(out[w * P:w * P + rows, :], y_out[0:rows, w % 2, :]).then_inc(y_stored[w % 2], 16)
            sp.wait_ge(y_stored[0], 16 * ((WINDOWS + 1) // 2))
            sp.wait_ge(y_stored[1], 16 * (WINDOWS // 2))

        @block.gpsimd
        def _(pool):
            steps = [0]

            def step(ins):
                steps[0] += 1
                ins.then_inc(pool_step, 1)
                pool.wait_ge(pool_step, steps[0])

            g = nc.gpsimd
            g.iota(iota_b[:], pattern=[[1, BLOCKS]], base=0, channel_multiplier=0, allow_small_or_imprecise_dtypes=True)
            g.iota(iota_node[:], pattern=[[1, P]], base=0, channel_multiplier=0, allow_small_or_imprecise_dtypes=True)
            g.iota(iota_part[:], pattern=[[0, 1]], base=0, channel_multiplier=1, allow_small_or_imprecise_dtypes=True)
            g.memset(eps_col[:], EPS)
            g.memset(ones_c[:], 1.0)
            step(g.memset(ident[:], 0.0))
            step(g.affine_select(out=ident[:], in_=ident[:], compare_op=ALU.not_equal, fill=1.0, base=0,
                                 pattern=[[-1, P]], channel_multiplier=1))
            step(g.memset(upto[:], 1.0))
            g.affine_select(out=upto[:], in_=upto[:], compare_op=ALU.is_ge, fill=0.0, base=0,
                            pattern=[[1, HALF_C]], channel_multiplier=-1).then_inc(consts, 1)

            def gather(table, width, arrived, idx_signal, freed):
                def stage(k, q):
                    b = SLOTS * k + q
                    after(pool, freed, b - SLOTS + 1)
                    g.tensor_copy(idx[:, q, :], src_col[:, ds(b, 1), :].rearrange("p o i -> p (o i)")).then_inc(idx_signal, 1)
                    pool.wait_ge(idx_signal, b + 1)
                    pool.sem_inc(idx_seen, 1)
                    for i in range(2):
                        g.indirect_dma_start(gath[:, q, i, 0:width], None, table,
                                             bass.IndirectOffsetOnAxis(ap=idx[:, q, i:i + 1], axis=0)).then_inc(arrived[q], 16)
                return stage

            pool.wait_ge(meta_ready, 1)
            for q in range(2):
                pool.wait_ge(row_stored[q], 16 * (WPAD // 2))
            pipeline(pool, [(gather(edge_in_tab, 2 * HID, gath_in, idx_done, z_ready), 0)], BLOCKS, SLOTS)

            for q in range(2):
                pool.wait_ge(kv_stored[q], 32 * (WPAD // 2))
            step(g.memset(spread[:], 1.0))
            step(g.affine_select(out=spread[:], in_=spread[:], compare_op=ALU.is_equal, fill=float(RELS), base=0,
                                 pattern=[[0, P]], channel_multiplier=1))
            step(g.affine_select(out=spread[:], in_=spread[:], compare_op=ALU.is_ge, fill=0.0, base=0,
                                 pattern=[[1, P]], channel_multiplier=-RELS))
            step(g.memset(block_row[:], 0.0))
            g.affine_select(out=block_row[:], in_=block_row[:], compare_op=ALU.is_ge, fill=1.0, base=1,
                            pattern=[[0, SLOTS], [-1, 2], [0, CHUNK]], channel_multiplier=-1).then_inc(consts, 1)
            pipeline(pool, [(gather(k_tab, 2 * HID, gath1_in, idx1_done, key_ready), 0)], BLOCKS, SLOTS)
            pool.wait_ge(key_ready, BLOCKS)
            g.memset(agg[:], 0.0).then_inc(agg_zero, 1)
            pipeline(pool, [(gather(v_tab, HID, gath2_in, idx2_done, weighted_done), 0)], BLOCKS, SLOTS)

        @block.scalar
        def _(act):
            s = nc.scalar
            act.wait_ge(consts, 1)
            s.copy(ident_r[:], ident[:]).then_inc(ident_r_done, 1)
            act.wait_ge(w_in, 9 * 16)
            s.copy(w_edge_hi[:], w_edge[:]).then_inc(w_split, 1)
            s.copy(w2_hi[:], w2_sb[:]).then_inc(w_split, 1)

            def norm_relu(w):
                s.activation(hs[:, ds(w, 1), :].rearrange("p o f -> p (o f)"), xs[:, ds(w, 1), :].rearrange("p o f -> p (o f)"),
                             ACT.Relu, bias=shift[:, ds(w, 1)], scale=rstd[:, ds(w, 1)])

            def normed(done):
                def stage(k, q):
                    w = 2 * k + q
                    s.activation(hs[:, ds(w, 1), :].rearrange("p o f -> p (o f)"),
                                 xs[:, ds(w, 1), :].rearrange("p o f -> p (o f)"), ACT.Relu,
                                 bias=shift[:, ds(w, 1)], scale=rstd[:, ds(w, 1)]).then_inc(done, 1)
                return stage

            def copy_ht(k, q):
                w = 2 * k + q
                act.wait_ge(ht_ready, w + 1)
                after(act, proj_ready, w - 1)
                s.copy(h_t[:, q, :, :], bank[q][:, 0:HID].rearrange("p (c n) -> p c n", c=2)).then_inc(ht_done, 1)

            act.wait_ge(var_done, 1)
            s.activation(std[:], mean_var[:, :, 1], ACT.Sqrt, bias=eps_col[:]).then_inc(std_done, 1)
            act.wait_ge(norm_done, 1)
            pipeline(act, [(normed(h_done), 0), (copy_ht, 1)], WPAD, 2)

            def split_edges(k, q):
                b = SLOTS * k + q
                act.wait_ge(ea_arrived[q], 32 * (k + 1))
                after(act, z_ready, b - SLOTS + 1)
                s.copy(ea_parts[:, q, :], ea_in[:, q, :]).then_inc(ea_hi_done, 1)

            def relu_and_gate(k, q):
                b = SLOTS * k + q
                act.wait_ge(z_ready, b + 1)
                after(act, core_ready, b - 1)
                s.activation(relu_hi[:, q % 2, :], bank[q % 2][:], ACT.Relu).then_inc(relu_hi_done, 1)
                after(act, msgt_done, b - 1)
                s.activation(gate[:, q % 2, :, :].rearrange("p c e -> p (c e)"), bank[2 + q % 2][:], ACT.Sigmoid).then_inc(gate_done, 1)

            def split_message(k, q):
                b = SLOTS * k + q
                act.wait_ge(msg_ready, b + 1)
                after(act, sum_ready, b - 1)
                s.copy(msg_hi[:, q % 2, :, :].rearrange("p i f -> p (i f)"), bank[6][:]).then_inc(msg_hi_done, 1)

            pipeline(act, [(relu_and_gate, 1), (split_edges, 0), (split_message, 3)], BLOCKS, SLOTS)

            act.wait_ge(var_done, 2)
            s.activation(std[:], mean_var[:, :, 1], ACT.Sqrt, bias=eps_col[:]).then_inc(std_done, 1)
            act.wait_ge(norm_done, 2)
            act.wait_ge(var_done, 3)
            s.activation(std[:], mean_var[:, :, 1], ACT.Sqrt, bias=eps_col[:]).then_inc(std_done, 1)
            act.wait_ge(norm_done, 3)
            act.wait_ge(lw_in, 3 * 16)
            act.wait_ge(rel_in, 5 * 16)
            for h in range(HEADS):
                last = s.mul(rel_parts[:, h * HEAD:(h + 1) * HEAD], rel_sb[:], 0.2)
            last.then_inc(rel_done, 1)
            s.mul(query_sb[:], query_sb[:], 0.1).then_inc(a_step, 1)
            act.wait_ge(a_step, 1)

            def enhance(k, q):
                w = 2 * k + q
                act.wait_ge(ht2_ready, w + 1)
                after(act, qkv_ready, w - 1)
                for c in range(2):
                    last = s.activation(h_t[:, q, c, :], bank[q][:, c * P:(c + 1) * P], ACT.Identity, bias=query_sb[:, c:c + 1])
                last.then_inc(ht2_done, 1)

            def high_parts(k, q):
                w = 2 * k + q
                act.wait_ge(qkv_done, w + 1)
                if not isinstance(w, int) or w >= 2:
                    act.wait_ge(kv_stored[q], 32 * k)
                s.copy(k_parts[:, q, 0, :], qkv_row[:, q, 0:HID]).then_inc(k_hi_done, 1)
                s.mul(q_hi[:, ds(w, 1), :].rearrange("p o f -> p (o f)"), qkv_row[:, q, 2 * HID:], 1 / HEAD ** 0.5).then_inc(q_hi_done, 1)

            pipeline(act, [(high_parts, 2), (normed(h2_done), 0), (enhance, 1)], WPAD, 2)

            def copy_keys(k, q):
                b = SLOTS * k + q
                act.wait_ge(key_ready, b + 1)
                after(act, prod_done, b - 1)
                s.copy(key_sb[:, q % 2, :, :].rearrange("p i f -> p (i f)"), bank[2 + q % 2][:]).then_inc(key_copied, 1)

            for q in range(2):
                act.wait_ge(kv_stored[q], 32 * (WPAD // 2))
            pipeline(act, [(copy_keys, 0)], BLOCKS, SLOTS)

            act.wait_ge(max_done, 1)
            flat = m_row[:].rearrange("p r h e -> p (r h e)")
            s.activation(flat, flat, ACT.Exp).then_inc(exp_done, 1)

            def weight_sums(k, q):
                b = SLOTS * k + q
                after(act, agg_ready, b - 1)
                s.copy(weighted[:, q % 2, :, HID:], exp_col[:, ds(b, 1), :, :].rearrange("p o i h -> p (o i) h")).then_inc(wsum_done, 1)

            act.wait_ge(weights_done, 4)
            pipeline(act, [(weight_sums, 0)], BLOCKS, SLOTS)

            for w in range(WINDOWS):
                act.wait_ge(mt_ready, w + 1)
                if w >= 2:
                    act.wait_ge(o_ready, w - 1)
                s.copy(h_t[:, w % 2, :, :], bank[w % 2][:, 0:HID].rearrange("p (c n) -> p c n", c=2)).then_inc(mt_done, 1)
            act.wait_ge(var_done, 4)
            s.activation(std[:, 0:WINDOWS], mean_var[:, 0:WINDOWS, 1], ACT.Sqrt, bias=eps_col[:]).then_inc(std_done, 1)

        @block.vector
        def _(dve):
            v = nc.vector
            steps = [0]

            def step(ins):
                steps[0] += 1
                ins.then_inc(d_step, 1)
                dve.wait_ge(d_step, steps[0])

            dve.wait_ge(nat_in, 4 * 16)
            dve.wait_ge(consts, 1)
            v.tensor_copy(ends_i[:, 0, :], nat_i[:, 1, :, 0])
            step(v.tensor_copy(ends_i[:, 1, :], nat_i[:, 1, :, CHUNK - 1]))
            step(v.tensor_scalar(ends_i[:], ends_i[:], P.bit_length() - 1, None, ALU.arith_shift_right))
            step(v.tensor_copy(nat_f[:], nat_i[:]))
            step(v.tensor_scalar(ends_w[:], ends_i[:], float(WINDOWS - 1), None, ALU.min))
            v.scalar_tensor_tensor(count[:], in0=ends_w[:, 1, :], scalar=1.0, in1=ends_w[:, 0, :], op0=ALU.add, op1=ALU.subtract).then_inc(counted, 1)
            v.scalar_tensor_tensor(jump[:], in0=ends_w[:, 2, :], scalar=-1.0, in1=ends_w[:, 1, :], op0=ALU.add, op1=ALU.subtract).then_inc(counted, 1)
            dve.wait_ge(cumulated, 1)
            step(v.tensor_copy(last_b[:], bank[0][0:HALF_C, 0:2]))
            step(v.tensor_tensor(first_b[:], last_b[:], count[:], ALU.subtract))
            for c in range(2):
                v.tensor_scalar(passed[:, c, :], iota_b[:], last_b[:, c:c + 1], None, ALU.is_ge)
                step(v.tensor_scalar(chosen[:, c, :], iota_b[:], first_b[:, c:c + 1], None, ALU.is_ge))
            v.tensor_tensor(chosen[:], chosen[:], passed[:], ALU.subtract).then_inc(sel_ready, 1)
            dve.wait_ge(rows_ready, 1)
            v.tensor_scalar(chunk_i[:], bank[0][0:1, 0:BLOCKS], float(CHUNKS - 1), None, ALU.min)
            step(v.tensor_tensor(win_f[:], bank[1][0:1, 0:BLOCKS], iota_b[0:1, :], ALU.add))
            step(v.tensor_scalar(win_f[:], win_f[:], ends_w[0:1, 0, 0:1], None, ALU.add))
            step(v.tensor_tensor(win_f[:], win_f[:], bank[2][0:1, 0:BLOCKS], ALU.mult))
            v.tensor_copy(win_i[:], win_f[:])
            step(v.tensor_scalar(neg_off[:], bank[2][0:1, 0:BLOCKS], -FAR, FAR, ALU.mult, ALU.add))
            v.scalar_tensor_tensor(neg_off[:], in0=win_f[:], scalar=-float(P), in1=neg_off[:], op0=ALU.mult, op1=ALU.add).then_inc(off_ready, 1)
            dve.wait_ge(cols_ready, 1)
            v.tensor_copy(src_col[:].rearrange("p b i -> p i b"), bank[0][:, 0:2 * BLOCKS].rearrange("p (i b) -> p i b", i=2))
            v.tensor_copy(rel_col[:].rearrange("p b i -> p i b"), bank[1][:, 0:2 * BLOCKS].rearrange("p (i b) -> p i b", i=2))
            v.tensor_copy(ends_row[:], bank[4][0:HEADS, 0:2 * BLOCKS].rearrange("p (i b) -> p i b", i=2))
            step(v.tensor_scalar(dst_row[:], bank[2][0:HALF_B, :].rearrange("p (r e) -> p r e", r=2), 255.0, -1.0, ALU.min, ALU.max))
            v.tensor_copy(row_b[:, :, 1, :], bank[3][0:HALF_B, :].rearrange("p (r e) -> p r e", r=2))
            v.tensor_copy(row_b[:, :, 0, :], dst_row[:]).then_inc(meta_ready, 1)

            dve.wait_ge(w_split, 2)
            v.tensor_tensor(w_edge_lo[:], w_edge[:], w_edge_hi[:], ALU.subtract)
            v.tensor_tensor(w2_lo[:], w2_sb[:], w2_hi[:], ALU.subtract).then_inc(w_split, 1)

            def statistics(rows):
                def one(k, q):
                    w = 2 * k + q
                    v.bn_stats(stats[:, ds(w, 1), :].rearrange("p o s -> p (o s)"), rows[:, ds(w, 1), :].rearrange("p o f -> p (o f)"))

                pipeline(dve, [(one, 0)], WPAD, 2)
                step(v.engine_nop())
                for w in range(WPAD):
                    last = v.bn_aggr(mean_var[:, w, :], stats[:, w, :])
                last.then_inc(var_done, 1)

            def scale_and_shift(n):
                dve.wait_ge(std_done, n)
                step(v.reciprocal(rstd[:], std[:]))
                v.scalar_tensor_tensor(shift[:], in0=mean_var[:, :, 0], scalar=-1.0, in1=rstd[:], op0=ALU.mult, op1=ALU.mult).then_inc(norm_done, 1)

            dve.wait_ge(x_in, 16)
            statistics(xs)
            scale_and_shift(1)

            def add_bias(k, q):
                w = 2 * k + q
                dve.wait_ge(proj_ready, w + 1)
                if not isinstance(w, int) or w >= 2:
                    dve.wait_ge(row_stored[q], 16 * k)
                v.tensor_tensor(node_row[:, q, :], bank[2 + q][:], b_cat_sb[:], ALU.add).then_inc(row_ready, 1)

            pipeline(dve, [(add_bias, 0)], WPAD, 2)

            def low_edges(k, q):
                b = SLOTS * k + q
                dve.wait_ge(ea_hi_done, b + 1)
                rows = slice(EDGE_DIM, 2 * EDGE_DIM)
                v.tensor_tensor(ea_parts[rows, q, :], ea_in[rows, q, :], ea_parts[rows, q, :], ALU.subtract).then_inc(ea_lo_done, 1)

            def low_relu(k, q):
                b = SLOTS * k + q
                dve.wait_ge(relu_hi_done, b + 1)
                v.scalar_tensor_tensor(relu_lo[:, q % 2, :], in0=bank[q % 2][:], scalar=0.0, in1=relu_hi[:, q % 2, :],
                                       op0=ALU.max, op1=ALU.subtract).then_inc(relu_lo_done, 1)

            def message(k, q):
                b = SLOTS * k + q
                dve.wait_ge(core_ready, b + 1)
                dve.wait_ge(gate_done, b + 1)
                after(dve, msg_ready, b - 1)
                for c in range(2):
                    last = v.scalar_tensor_tensor(msg_t[:, q % 2, c, :], in0=bank[4 + q % 2][:, c * CHUNK:(c + 1) * CHUNK],
                                                  scalar=b2_sb[:, c:c + 1], in1=gate[:, q % 2, c, :], op0=ALU.add, op1=ALU.mult)
                last.then_inc(msgt_done, 1)

            def one_hot(k, q):
                b = SLOTS * k + q
                after(dve, sum_ready, b - 1)
                for i in range(2):
                    last = v.tensor_scalar(hot[:, q % 2, i, :], iota_node[:], rel_col[:, ds(b, 1), i], None, ALU.is_equal)
                last.then_inc(hot_done, 1)

            def low_message(k, q):
                b = SLOTS * k + q
                dve.wait_ge(msg_hi_done, b + 1)
                v.tensor_tensor(msg_lo[:, q % 2, :, :].rearrange("p i f -> p (i f)"), bank[6][:],
                                msg_hi[:, q % 2, :, :].rearrange("p i f -> p (i f)"), ALU.subtract).then_inc(msg_lo_done, 1)

            def add_sums(k, q):
                b = SLOTS * k + q
                dve.wait_ge(sum_ready, b + 1)
                after(dve, sum_added, b)
                w = dve.value_load(win_i[0:1, ds(b, 1)], min_val=0, max_val=WINDOWS - 1)
                rows = hs[:, ds(w, 1), :].rearrange("p o f -> p (o f)")
                v.tensor_tensor(rows, rows, bank[7][:, 0:HID], ALU.add).then_inc(sum_added, 1)

            pipeline(dve, [(add_sums, 4), (low_relu, 1), (low_edges, 0), (message, 2), (one_hot, 3), (low_message, 3)],
                     BLOCKS, SLOTS)
            dve.wait_ge(sum_added, BLOCKS)

            statistics(hs)
            scale_and_shift(2)
            dve.wait_ge(norm_done, 2)
            dve.wait_ge(lw_in, 3 * 16)
            base = steps[0]

            def residual(k, q):
                w = 2 * k + q
                hrow, xrow = (t[:, ds(w, 1), :].rearrange("p o f -> p (o f)") for t in (hs, xs))
                v.tensor_scalar(hrow, hrow, mean_var[:, ds(w, 1), 0], rstd[:, ds(w, 1)], ALU.subtract, ALU.mult).then_inc(d_step, 1)
                dve.wait_ge(d_step, base + 3 * w + 1)
                v.tensor_tensor(hrow, hrow, ln0_sb[:, 0, :], ALU.mult).then_inc(d_step, 1)
                dve.wait_ge(d_step, base + 3 * w + 2)
                v.tensor_tensor(hrow, hrow, ln0_sb[:, 1, :], ALU.add).then_inc(d_step, 1)
                dve.wait_ge(d_step, base + 3 * w + 3)
                v.tensor_tensor(xrow, xrow, hrow, ALU.add).then_inc(x1_done, 1)

            pipeline(dve, [(residual, 0)], WPAD, 2)
            steps[0] += 3 * WPAD
            dve.wait_ge(x1_done, WPAD)
            statistics(xs)
            scale_and_shift(3)

            dve.wait_ge(rel_done, 1)
            for h in range(HEADS):
                last = v.scalar_tensor_tensor(rel_parts[RELS:, h * HEAD:(h + 1) * HEAD], in0=rel_sb[RELS:, :], scalar=0.2,
                                              in1=rel_parts[RELS:, h * HEAD:(h + 1) * HEAD], op0=ALU.mult, op1=ALU.subtract)
            last.then_inc(rel_done, 1)

            def qkv_bias(k, q):
                w = 2 * k + q
                dve.wait_ge(qkv_ready, w + 1)
                if not isinstance(w, int) or w >= 2:
                    dve.wait_ge(kv_stored[q], 32 * k)
                after(dve, q_hi_done, w - 1)
                after(dve, q_lo_done, w - 1)
                v.tensor_tensor(qkv_row[:, q, 0:2 * HID], bank[2 + q][:], b_qkv_sb[:, 0:2 * HID], ALU.add)
                v.tensor_tensor(qkv_row[:, q, 2 * HID:], bank[4 + q][:, 0:HID], b_qkv_sb[:, 2 * HID:], ALU.add).then_inc(qkv_done, 1)

            def low_parts(k, q):
                w = 2 * k + q
                dve.wait_ge(k_hi_done, w + 1)
                v.tensor_tensor(k_parts[:, q, 1, :], qkv_row[:, q, 0:HID], k_parts[:, q, 0, :], ALU.subtract).then_inc(k_lo_done, 1)
                dve.wait_ge(q_hi_done, w + 1)
                hi, lo = (t[:, ds(w, 1), :].rearrange("p o f -> p (o f)") for t in (q_hi, q_lo))
                v.scalar_tensor_tensor(lo, in0=qkv_row[:, q, 2 * HID:], scalar=1 / HEAD ** 0.5, in1=hi,
                                       op0=ALU.mult, op1=ALU.subtract).then_inc(q_lo_done, 1)

            pipeline(dve, [(low_parts, 1), (qkv_bias, 0)], WPAD, 2)

            def one_hot_t(k, q):
                b = SLOTS * k + q
                dve.wait_ge(spread_ready, b + 1)
                after(dve, query_ready, b - 1)
                v.tensor_scalar(hot_t[:, q % 2, :, :].rearrange("p k e -> p (k e)"), bank[q % 2][:], iota_part[:], None,
                                ALU.is_equal).then_inc(hot_t_done, 1)

            def products(k, q):
                b = SLOTS * k + q
                dve.wait_ge(key_copied, b + 1)
                dve.wait_ge(query_ready, b + 1)
                after(dve, score_done, b - 1)
                v.tensor_tensor(prod[:, q % 2, :], bank[4 + q % 2][:], key_sb[:, q % 2, :, :].rearrange("p i f -> p (i f)"),
                                ALU.mult).then_inc(prod_done, 1)

            def scores(k, q):
                b = SLOTS * k + q
                dve.wait_ge(prod_done, b + 1)
                v.tensor_reduce(out=exp_col[:, ds(b, 1), :, :].rearrange("p o i h -> p (o i h)"),
                                in_=prod[:, q % 2, :].rearrange("p (j d) -> p j d", d=HEAD), axis=AX.X, op=ALU.add).then_inc(score_done, 1)

            for q in range(2):
                dve.wait_ge(kv_stored[q], 32 * (WPAD // 2))
            dve.wait_ge(consts, 2)
            pipeline(dve, [(scores, 2), (one_hot_t, 0), (products, 1)], BLOCKS, SLOTS)
            dve.wait_ge(score_done, BLOCKS)
            dve.wait_ge(key_ready, BLOCKS)

            step(v.tensor_scalar(outside[:], dst_row[:], 0.0, BIG, ALU.is_ge, ALU.mult))
            step(v.tensor_scalar(tmp_row[:], dst_row[:], float(P - 1), BIG, ALU.is_le, ALU.mult))
            step(v.tensor_tensor(outside[:], outside[:], tmp_row[:], ALU.add))
            step(v.tensor_scalar(outside[:], outside[:], 2 * BIG, None, ALU.subtract))
            step(v.memset(reset[:], -BIG))
            step(v.tensor_tensor(tmp_row[:, :, 1:], dst_row[:, :, 1:], dst_row[:, :, 0:CHUNK - 1], ALU.is_equal))
            for r in range(2):
                for h in range(HEADS):
                    last = v.tensor_scalar(reset[:, r, h * CHUNK + 1:(h + 1) * CHUNK], tmp_row[:, r, 1:], BIG, BIG, ALU.mult, ALU.subtract)
            step(last)
            for r in range(2):
                for i, e in enumerate((0, CHUNK - 1)):
                    step(v.tensor_scalar(same[:, r, i, :], dst_row[:, r, :], dst_row[:, r, e:e + 1], BIG, ALU.is_equal, ALU.mult))
            step(v.tensor_scalar(same[:], same[:], BIG, None, ALU.subtract))
            step(v.memset(follows[:], 0.0))
            v.tensor_tensor(follows[:, 1:], ends_row[:, 0, 1:], ends_row[:, 1, 0:BLOCKS - 1], ALU.is_equal)
            step(v.tensor_tensor(whole[:], ends_row[:, 0, :], ends_row[:, 1, :], ALU.is_equal))
            step(v.memset(into[:], 0.0))
            step(v.tensor_copy(into[:, 0, :], follows[:]))
            step(v.tensor_copy(into[:, 1, 0:BLOCKS - 1], follows[:, 1:]))
            for i in range(2):
                step(v.tensor_tensor(through[:, i, :], into[:, i, :], whole[:], ALU.mult))
            step(v.tensor_scalar(into[:], into[:], BIG, BIG, ALU.mult, ALU.subtract))
            step(v.tensor_scalar(through[:], through[:], BIG, BIG, ALU.mult, ALU.subtract))
            dve.wait_ge(srow_ready, 1)
            for r in range(2):
                for hp in range(2):
                    for j in range(2):
                        last = v.tensor_tensor(s_row[:, r, 2 * hp + j, :], bank[2 * r + hp][0:HALF_B, j * CHUNK:(j + 1) * CHUNK],
                                               outside[:, r, :], ALU.add)
            step(last)
            for r in range(2):
                rows = m_row[:, r, :, :].rearrange("p h e -> p (h e)")
                step(v.tensor_tensor_scan(rows, reset[:, r, 0:HEADS * CHUNK], s_row[:, r, :, :].rearrange("p h e -> p (h e)"), -BIG, ALU.add, ALU.max))
            for r in range(2):
                rows = m_row[:, r, :, :].rearrange("p h e -> p (h e)")
                last = v.tensor_tensor_scan(rows[:, ::-1], reset[:, r, HEADS * CHUNK:0:-1], rows[:, ::-1], -BIG, ALU.add, ALU.max)
            last.then_inc(local_done, 1)
            dve.wait_ge(lends_ready, 1)
            for i in range(2):
                last = v.tensor_copy(edge_max[:, i, :], bank[4 + i][0:HEADS, 0:BLOCKS])
            step(last)
            v.tensor_tensor_scan(run_max[:, 0, :], through[:, 0, :], edge_max[:, 1, :], -BIG, ALU.add, ALU.max)
            step(v.tensor_tensor_scan(run_max[:, 1, ::-1], through[:, 1, ::-1], edge_max[:, 0, ::-1], -BIG, ALU.add, ALU.max))
            step(v.memset(carry[:], -BIG))
            v.tensor_tensor(carry[:, 0, 1:], run_max[:, 0, 0:BLOCKS - 1], into[:, 0, 1:], ALU.add)
            v.tensor_tensor(carry[:, 1, 0:BLOCKS - 1], run_max[:, 1, 1:], into[:, 1, 0:BLOCKS - 1], ALU.add).then_inc(carried, 1)
            dve.wait_ge(carry_ready, 1)
            step(v.tensor_copy(carry_col[:], bank[6][0:HALF_B, 0:4 * HEADS].rearrange("p (r i h) -> p r i h", r=2, i=2)))
            for i in range(2):
                for r in range(2):
                    for h in range(HEADS):
                        last = v.scalar_tensor_tensor(m_row[:, r, h, :], in0=same[:, r, i, :], scalar=carry_col[:, r, i, h:h + 1],
                                                      in1=m_row[:, r, h, :], op0=ALU.add, op1=ALU.max)
                step(last)
            v.tensor_tensor(m_row[:], s_row[:], m_row[:], ALU.subtract).then_inc(max_done, 1)
            for r in range(2):
                for i in range(2):
                    dve.wait_ge(expt_ready, 2 * r + i + 1)
                    v.tensor_copy(exp_col[:, r * HALF_B:(r + 1) * HALF_B, i, :].rearrange("p b h -> p h b"),
                                  bank[2 * r + i][:, 0:HEADS * HALF_B].rearrange("p (h b) -> p h b", h=HEADS)).then_inc(weights_done, 1)
            dve.wait_ge(weights_done, 4)

            def weight_values(k, q):
                b = SLOTS * k + q
                dve.wait_ge(gath2_in[q], 32 * (k + 1))
                after(dve, agg_ready, b - 1)
                for i in range(2):
                    last = v.tensor_tensor(
                        weighted[:, q % 2, i, 0:HID].rearrange("p (h d) -> p h d", h=HEADS),
                        gath[:, q, i, 0:HID].rearrange("p (h d) -> p h d", h=HEADS),
                        exp_col[:, ds(b, 1), i, :].rearrange("p o h -> p h o").to_broadcast([P, HEADS, HEAD]), ALU.mult)
                last.then_inc(weighted_done, 1)
                for i in range(2):
                    last = v.tensor_scalar(hot1[:, q % 2, i, :], iota_node[:], rel_col[:, ds(b, 1), i], None, ALU.is_equal)
                last.then_inc(hot1_done, 1)

            def add_agg(k, q):
                b = SLOTS * k + q
                dve.wait_ge(agg_ready, b + 1)
                after(dve, agg_added, b)
                w = dve.value_load(win_i[0:1, ds(b, 1)], min_val=0, max_val=WINDOWS - 1)
                rows = agg[:, ds(w, 1), :].rearrange("p o f -> p (o f)")
                v.tensor_tensor(rows, rows, bank[q % 2][:, 0:AGGW], ALU.add).then_inc(agg_added, 1)

            dve.wait_ge(agg_zero, 1)
            pipeline(dve, [(weight_values, 0), (add_agg, 2)], BLOCKS, SLOTS)
            dve.wait_ge(agg_added, BLOCKS)

            step(v.tensor_scalar(empty[:], agg[:, :, HID:], 0.0, None, ALU.is_equal))
            step(v.tensor_tensor(denom[:], agg[:, :, HID:], empty[:], ALU.add))
            step(v.reciprocal(inv[:], denom[:]))
            dve.wait_ge(ow_in, 3 * 16)

            def mix(w):
                q = w % 2
                dve.wait_ge(v_arrived[q], 16 * (w // 2 + 1))
                heads = agg[:, w, 0:HID].rearrange("p (h d) -> p h d", h=HEADS)
                own = v_in[:, q, :].rearrange("p (h d) -> p h d", h=HEADS)
                v.tensor_tensor(heads, heads, inv[:, w, :].unsqueeze(2).to_broadcast([P, HEADS, HEAD]), ALU.mult)
                step(v.tensor_tensor(own, own, empty[:, w, :].unsqueeze(2).to_broadcast([P, HEADS, HEAD]), ALU.mult))
                v.tensor_tensor(heads, heads, own, ALU.add).then_inc(mix_done, 1)

            def project_out(w):
                dve.wait_ge(o_ready, w + 1)
                step(v.tensor_tensor(hs[:, w, :], hs[:, w, :], bank[2 + w % 2][:, 0:HID], ALU.add))
                step(v.tensor_tensor(hs[:, w, :], hs[:, w, :], b_o_sb[:], ALU.add))
                v.engine_nop().then_inc(o_done, 1)
                step(v.bn_stats(stats[:, w, :], hs[:, w, :]))
                step(v.bn_aggr(mean_var[:, w, :], stats[:, w, :]))

            for w in range(WINDOWS + 2):
                if w < WINDOWS:
                    mix(w)
                if w >= 2:
                    project_out(w - 2)
            v.engine_nop().then_inc(var_done, 1)
            dve.wait_ge(std_done, 4)
            step(v.reciprocal(rstd[:, 0:WINDOWS], std[:, 0:WINDOWS]))
            for w in range(WINDOWS):
                step(v.tensor_scalar(hs[:, w, :], hs[:, w, :], mean_var[:, w, 0:1], rstd[:, w:w + 1], ALU.subtract, ALU.mult))
                step(v.tensor_tensor(hs[:, w, :], hs[:, w, :], ln1_sb[:, 0, :], ALU.mult))
                step(v.tensor_tensor(hs[:, w, :], hs[:, w, :], ln1_sb[:, 1, :], ALU.add))
                if w >= 2:
                    dve.wait_ge(y_stored[w % 2], 16 * (w // 2))
                v.tensor_tensor(y_out[:, w % 2, :], hs[:, w, :], xs[:, w, :], ALU.add).then_inc(y_done, 1)

        @block.tensor
        def _(pe):
            def mm(out_, lhs, rhs, start, stop):
                return nc.tensor.matmul(out_, lhsT=lhs, rhs=rhs, start=start, stop=stop)

            def tr(out_, in_, start=True, stop=True):
                return nc.tensor.matmul(out_, lhsT=in_, rhs=ident[:], is_transpose=True, start=start, stop=stop)

            pe.wait_ge(consts, 1)
            pe.wait_ge(counted, 2)
            mm(bank[0][0:HALF_C, 0:2], upto[:], count[:], True, False)
            mm(bank[0][0:HALF_C, 1:2], ones_c[:, 0:HALF_C], count[:, 0:1], False, True).then_inc(cumulated, 1)
            pe.wait_ge(sel_ready, 1)
            for c in range(2):
                mm(bank[0][0:1, 0:BLOCKS], ones_c[:, 0:1], passed[:, c, :], c == 0, c == 1)
            for c in range(2):
                mm(bank[1][0:1, 0:BLOCKS], jump[:, c:c + 1], passed[:, c, :], c == 0, c == 1)
            for c in range(2):
                last = mm(bank[2][0:1, 0:BLOCKS], ones_c[:, 0:1], chosen[:, c, :], c == 0, c == 1)
            last.then_inc(rows_ready, 1)
            pe.wait_ge(off_ready, 1)
            for i in range(2):
                cols = slice(i * BLOCKS, (i + 1) * BLOCKS)
                for c in range(2):
                    mm(bank[0][:, cols], nat_f[:, 0, c, i * P:(i + 1) * P], chosen[:, c, :], c == 0, c == 1)
                for c in range(2):
                    mm(bank[1][:, cols], nat_f[:, 1, c, i * P:(i + 1) * P], chosen[:, c, :], c == 0, False)
                mm(bank[1][:, cols], ones_c[0:1, 0:P], neg_off[:], False, True)
                e = i * (CHUNK - 1)
                for c in range(2):
                    mm(bank[4][0:HEADS, cols], nat_f[:, 1, c, e:e + 1].to_broadcast([HALF_C, HEADS]), chosen[:, c, :], c == 0, c == 1)
            for r in range(2):
                some = slice(r * HALF_B, (r + 1) * HALF_B)
                cols = slice(r * CHUNK, (r + 1) * CHUNK)
                for c in range(2):
                    mm(bank[2][0:HALF_B, cols], chosen[:, c, some], nat_f[:, 1, c, :], c == 0, False)
                mm(bank[2][0:HALF_B, cols], neg_off[0:1, some], ones_c[0:1, :], False, True)
                for c in range(2):
                    last = mm(bank[3][0:HALF_B, cols], chosen[:, c, some], nat_f[:, 2, c, :], c == 0, c == 1)
            last.then_inc(cols_ready, 1)
            pe.wait_ge(meta_ready, 1)
            pe.wait_ge(w_in, 9 * 16)

            def transpose_rows(rows, source_done, freed, ready):
                def stage(k, q):
                    w = 2 * k + q
                    pe.wait_ge(source_done, w + 1)
                    after(pe, freed, w - 1)
                    for c in range(2):
                        last = tr(bank[q][:, c * P:(c + 1) * P], rows[:, w, c * P:(c + 1) * P], c == 0, c == 1)
                    last.then_inc(ready, 1)
                return stage

            def project_nodes(k, q):
                w = 2 * k + q
                pe.wait_ge(ht_done, w + 1)
                after(pe, row_ready, w - 1)
                for c in range(2):
                    last = mm(bank[2 + q][:], h_t[:, q, c, :], w_node[:, c, :], c == 0, c == 1)
                last.then_inc(proj_ready, 1)

            pipeline(pe, [(transpose_rows(hs, h_done, ht_done, ht_ready), 0), (project_nodes, 1)], WPAD, 2, straight=True)
            pe.wait_ge(row_ready, WPAD)
            pe.wait_ge(w_split, 3)
            pe.wait_ge(ident_r_done, 1)

            def edge_inputs(k, q):
                b = SLOTS * k + q
                pe.wait_ge(gath_in[q], 32 * (k + 1))
                pe.wait_ge(ea_lo_done, b + 1)
                after(pe, relu_lo_done, b - 1)
                after(pe, gate_done, b - 1)
                for m in range(4):
                    to = bank[2 * (m // 2) + q % 2][:, (m % 2) * CHUNK:(m % 2 + 1) * CHUNK]
                    for i in range(2):
                        tr(to[:, i * P:(i + 1) * P], gath[:, q, i, m * P:(m + 1) * P], i == 0, False)
                    mm(to, w_edge_hi[:, m * P:(m + 1) * P], ea_parts[:, q, :], False, False)
                    last = mm(to, w_edge_lo[:, m * P:(m + 1) * P], ea_parts[:, q, :], False, True)
                last.then_inc(z_ready, 1)

            def core(k, q):
                b = SLOTS * k + q
                pe.wait_ge(relu_hi_done, b + 1)
                after(pe, msgt_done, b - 1)
                for m in range(2):
                    to = bank[4 + q % 2][:, m * CHUNK:(m + 1) * CHUNK]
                    for c in range(2):
                        mm(to, w2_hi[:, c, m * P:(m + 1) * P], relu_hi[:, q % 2, c * CHUNK:(c + 1) * CHUNK], c == 0, False)
                        mm(to, w2_lo[:, c, m * P:(m + 1) * P], relu_hi[:, q % 2, c * CHUNK:(c + 1) * CHUNK], False, False)
                    if m == 0:
                        pe.wait_ge(relu_lo_done, b + 1)
                    for c in range(2):
                        last = mm(to, w2_hi[:, c, m * P:(m + 1) * P], relu_lo[:, q % 2, c * CHUNK:(c + 1) * CHUNK], False, c == 1)
                last.then_inc(core_ready, 1)

            def message_rows(k, q):
                b = SLOTS * k + q
                pe.wait_ge(msgt_done, b + 1)
                after(pe, msg_lo_done, b)
                for i in range(2):
                    for c in range(2):
                        last = tr(bank[6][:, i * HID + c * P:i * HID + (c + 1) * P], msg_t[:, q % 2, c, i * P:(i + 1) * P])
                last.then_inc(msg_ready, 1)

            def sum_messages(k, q):
                b = SLOTS * k + q
                pe.wait_ge(msg_lo_done, b + 1)
                pe.wait_ge(hot_done, b + 1)
                after(pe, sum_added, b)
                to = bank[7][:, 0:HID]
                for i in range(2):
                    mm(to, hot[:, q % 2, i, :], msg_hi[:, q % 2, i, :], i == 0, False)
                    last = mm(to, hot[:, q % 2, i, :], msg_lo[:, q % 2, i, :], False, i == 1)
                last.then_inc(sum_ready, 1)

            pipeline(pe, [(edge_inputs, 0), (sum_messages, 3), (message_rows, 2), (core, 1)], BLOCKS, SLOTS)
            pe.wait_ge(sum_added, BLOCKS)
            pe.wait_ge(rel_in, 5 * 16)

            def project_qkv(k, q):
                w = 2 * k + q
                pe.wait_ge(ht2_done, w + 1)
                after(pe, qkv_done, w - 1)
                for c in range(2):
                    mm(bank[2 + q][:], h_t[:, q, c, :], wqkv_sb[:, c, 0:2 * HID], c == 0, c == 1)
                for c in range(2):
                    last = mm(bank[4 + q][:, 0:HID], h_t[:, q, c, :], wqkv_sb[:, c, 2 * HID:], c == 0, c == 1)
                last.then_inc(qkv_ready, 1)

            pipeline(pe, [(transpose_rows(hs, h2_done, ht2_done, ht2_ready), 0), (project_qkv, 1)], WPAD, 2, straight=True)
            pe.wait_ge(qkv_done, WPAD)
            pe.wait_ge(q_lo_done, WPAD)
            pe.wait_ge(rel_done, 2)
            pe.wait_ge(consts, 2)

            def spread_row(k, q):
                b = SLOTS * k + q
                pe.wait_ge(brow_in[q], 16 * (k + 1))
                after(pe, hot_t_done, b - 1)
                mm(bank[q % 2][:], spread[:], block_row[:, q, :, :].rearrange("p k e -> p (k e)"), True, True).then_inc(spread_ready, 1)

            def keys_and_queries(k, q):
                b = SLOTS * k + q
                pe.wait_ge(gath1_in[q], 32 * (k + 1))
                pe.wait_ge(hot_t_done, b + 1)
                after(pe, key_copied, b - 1)
                for i in range(2):
                    to = bank[2 + q % 2][:, i * HID:(i + 1) * HID]
                    for part in range(2):
                        mm(to, ident_r[:], gath[:, q, i, part * HID:(part + 1) * HID].bitcast(f32r), part == 0, False)
                    last = mm(to, hot_t[:, q % 2, 1, i * P:(i + 1) * P], rel_parts[:], False, True)
                last.then_inc(key_ready, 1)
                after(pe, prod_done, b - 1)
                w = pe.value_load(win_i[0:1, ds(b, 1)], min_val=0, max_val=WINDOWS - 1)
                for i in range(2):
                    to = bank[4 + q % 2][:, i * HID:(i + 1) * HID]
                    for table in (q_hi, q_lo):
                        last = mm(to, hot_t[:, q % 2, 0, i * P:(i + 1) * P], table[:, ds(w, 1), :].rearrange("p o f -> p (o f)"),
                                  table is q_hi, table is q_lo)
                last.then_inc(query_ready, 1)

            pipeline(pe, [(spread_row, 0), (keys_and_queries, 1)], BLOCKS, SLOTS)

            pe.wait_ge(score_done, BLOCKS)
            for r in range(2):
                for h in range(HEADS):
                    for i in range(2):
                        at = (h % 2) * CHUNK + i * P
                        last = tr(bank[2 * r + h // 2][0:HALF_B, at:at + P], exp_col[:, r * HALF_B:(r + 1) * HALF_B, i, h])
            last.then_inc(srow_ready, 1)
            pe.wait_ge(local_done, 1)
            for i, e in enumerate((0, CHUNK - 1)):
                for r in range(2):
                    last = mm(bank[4 + i][0:HEADS, r * HALF_B:(r + 1) * HALF_B], m_row[:, r, :, e], ident[0:HALF_B, 0:HALF_B], True, True)
            last.then_inc(lends_ready, 1)
            pe.wait_ge(carried, 1)
            for r in range(2):
                for i in range(2):
                    at = (2 * r + i) * HEADS
                    last = mm(bank[6][0:HALF_B, at:at + HEADS], carry[:, i, r * HALF_B:(r + 1) * HALF_B], ident[0:HEADS, 0:HEADS], True, True)
            last.then_inc(carry_ready, 1)
            pe.wait_ge(exp_done, 1)
            for r in range(2):
                for i in range(2):
                    for h in range(HEADS):
                        last = nc.tensor.matmul(bank[2 * r + i][:, h * HALF_B:(h + 1) * HALF_B], lhsT=m_row[:, r, h, i * P:(i + 1) * P],
                                                rhs=ident[0:HALF_B, 0:HALF_B], is_transpose=True, start=True, stop=True)
                    last.then_inc(expt_ready, 1)
            pe.wait_ge(weights_done, 4)

            def aggregate(k, q):
                b = SLOTS * k + q
                pe.wait_ge(hot1_done, b + 1)
                pe.wait_ge(wsum_done, b + 1)
                after(pe, agg_added, b - 1)
                for i in range(2):
                    last = mm(bank[q % 2][:, 0:AGGW], hot1[:, q % 2, i, :], weighted[:, q % 2, i, :], i == 0, i == 1)
                last.then_inc(agg_ready, 1)

            pipeline(pe, [(aggregate, 0)], BLOCKS, SLOTS)
            pe.wait_ge(agg_added, BLOCKS)

            for w in range(WINDOWS + 1):
                q = w % 2
                if w < WINDOWS:
                    pe.wait_ge(mix_done, w + 1)
                    if w >= 2:
                        pe.wait_ge(mt_done, w - 1)
                    for c in range(2):
                        last = tr(bank[q][:, c * P:(c + 1) * P], agg[:, w, c * P:(c + 1) * P], c == 0, c == 1)
                    last.then_inc(mt_ready, 1)
                if w >= 1:
                    q = (w - 1) % 2
                    pe.wait_ge(mt_done, w)
                    if w >= 3:
                        pe.wait_ge(o_done, w - 2)
                    for c in range(2):
                        last = mm(bank[2 + q][:, 0:HID], h_t[:, q, c, :], wo_sb[:, c, :], c == 0, c == 1)
                    last.then_inc(o_ready, 1)


def kernel(x, src, dst, edge_attr_64, edge_type_64, L0_gnn_W1, L0_gnn_b1, L0_gnn_W2, L0_gnn_b2, L0_gnn_Wg, L0_gnn_bg,
           L0_gnn_gamma, L0_gnn_beta, L1_gnn_query_emb, L1_gnn_Wq, L1_gnn_bq, L1_gnn_Wk, L1_gnn_bk, L1_gnn_Wv,
           L1_gnn_bv, L1_gnn_rel_w, L1_gnn_Wo, L1_gnn_bo, L1_gnn_gamma, L1_gnn_beta):
    import numpy as np
    import concourse.bacc as bacc
    from concourse import mybir as mb
    from concourse.bass_utils import run_bass_kernel_spmd

    def rows(a, n, fill):
        a = np.asarray(a)
        full = np.full((n * CHUNK,) + a.shape[1:], fill, a.dtype)
        full[:a.shape[0]] = a
        return full.reshape((n, CHUNK) + a.shape[1:])

    def col(a):
        return np.ascontiguousarray(np.asarray(a).reshape(2, P).T)

    x = np.asarray(x)
    x_pad = np.zeros((WPAD * P, HID), x.dtype)
    x_pad[:NODES] = x
    arrays = {
        "x": x_pad,
        "src": rows(src, CHUNKS + 1, 0),
        "dst": rows(dst, CHUNKS + 1, NO_NODE),
        "etype": rows(edge_type_64, CHUNKS + 1, 0),
        "ea": np.ascontiguousarray(rows(edge_attr_64, CHUNKS, 0).transpose(0, 2, 1)),
        "w1": np.asarray(L0_gnn_W1),
        "wg": np.asarray(L0_gnn_Wg),
        "b_cat": np.concatenate([np.asarray(L0_gnn_b1), np.asarray(L0_gnn_bg)])[None, :],
        "w2": np.asarray(L0_gnn_W2),
        "b2_col": col(L0_gnn_b2),
        "ln0": np.stack([np.asarray(L0_gnn_gamma), np.asarray(L0_gnn_beta)]),
        "query_col": col(L1_gnn_query_emb),
        "wqkv": np.concatenate([np.asarray(a) for a in (L1_gnn_Wk, L1_gnn_Wv, L1_gnn_Wq)], axis=1),
        "b_qkv": np.concatenate([np.asarray(a) for a in (L1_gnn_bk, L1_gnn_bv, L1_gnn_bq)])[None, :],
        "rel": np.asarray(L1_gnn_rel_w),
        "wo": np.asarray(L1_gnn_Wo),
        "b_o": np.asarray(L1_gnn_bo)[None, :],
        "ln1": np.stack([np.asarray(L1_gnn_gamma), np.asarray(L1_gnn_beta)]),
    }
    nc = bacc.Bacc("TRN2", target_bir_lowering=False, num_devices=1)
    args = [nc.dram_tensor(f"in_{name}", a.shape, mb.dt.from_np(a.dtype), kind="ExternalInput").ap() for name, a in arrays.items()]
    result = nc.dram_tensor("out_x", (NODES, HID), mb.dt.float32, kind="ExternalOutput").ap()
    build(nc, *args, result)
    got = run_bass_kernel_spmd(nc, [{f"in_{name}": a for name, a in arrays.items()}], core_ids=[0])
    return got.results[0]["out_x"]
```

```python
import concourse.bass as bass
from concourse import mybir
from contextlib import ExitStack

NODES, EDGES, HID, EDGE_DIM, RELS, HEADS = 3125, 50000, 256, 64, 64, 4
P = 128
HEAD = HID // HEADS
CHUNK = 256
CHUNKS = -(-EDGES // CHUNK)
WINDOWS = -(-NODES // P)
WPAD = WINDOWS + WINDOWS % 2
BLOCKS = CHUNKS + WINDOWS - 1
HALF_C = CHUNKS // 2
HALF_B = BLOCKS // 2
NO_NODE = 4096
FAR = 8192.0
BIG = 1e30
EPS = 1e-5
SLOTS = 4
SHARES = 32
AGGW = HID + HEADS
assert CHUNKS % 2 == 0 and BLOCKS % SLOTS == 0


def build(nc, x, src, dst, etype, ea, w1, wg, b_cat, w2, b2, ln0, query_col, wqkv, b_qkv, rel, wo, b_o, ln1, out):
    f32, i32, f32r, bf16 = mybir.dt.float32, mybir.dt.int32, mybir.dt.float32r, mybir.dt.bfloat16
    ALU, ACT, AX = mybir.AluOpType, mybir.ActivationFunctionType, mybir.AxisListType
    ds = bass.ds

    edge_in_tab = nc.dram_tensor("edge_in_tab", (WPAD * P, 2 * HID), f32, kind="Internal").ap()
    k_tab = nc.dram_tensor("k_tab", (WPAD * P, 2 * HID), f32, kind="Internal").ap()
    v_tab = nc.dram_tensor("v_tab", (WPAD * P, HID), f32, kind="Internal").ap()
    row_tab = nc.dram_tensor("row_tab", (BLOCKS, 2 * CHUNK), bf16, kind="Internal").ap()

    ctx = ExitStack()
    with ctx:
        def sem(name):
            return ctx.enter_context(nc.semaphore(name))

        def sems(name, n):
            return [sem(f"{name}{i}") for i in range(n)]

        def sb(where, name, shape, dt):
            return where.enter_context(nc.sbuf_tensor(name, shape, dt))

        xs = sb(ctx, "xs", [P, WPAD, HID], f32)
        hs = sb(ctx, "hs", [P, WPAD, HID], f32)
        ident = sb(ctx, "ident", [P, P], f32)
        ident_r = sb(ctx, "ident_r", [P, P], f32r)
        iota_node = sb(ctx, "iota_node", [P, P], f32)
        iota_part = sb(ctx, "iota_part", [P, 1], f32)
        eps_col = sb(ctx, "eps_col", [P, 1], f32)
        one_col = sb(ctx, "one_col", [P, 1], f32)
        stats = sb(ctx, "stats", [P, WPAD, 6], f32)
        mean_var = sb(ctx, "mean_var", [P, WPAD, 2], f32)
        std = sb(ctx, "std", [P, WPAD], f32)
        rstd = sb(ctx, "rstd", [P, WPAD], f32)
        shift = sb(ctx, "shift", [P, WPAD], f32)
        src_col = sb(ctx, "src_col", [P, BLOCKS, 2], i32)
        rel_col = sb(ctx, "rel_col", [P, BLOCKS, 2], f32)
        dst_row = sb(ctx, "dst_row", [HALF_B, 2, CHUNK], f32)
        chunk_i = sb(ctx, "chunk_i", [1, BLOCKS], i32)
        win_i = sb(ctx, "win_i", [1, BLOCKS], i32)
        ends_row = sb(ctx, "ends_row", [HEADS, 2, BLOCKS], f32)
        idx = sb(ctx, "idx", [P, 2, SLOTS, 2], i32)
        ht_hi = sb(ctx, "ht_hi", [P, 2, 2, P], f32r)
        ht_lo = sb(ctx, "ht_lo", [P, 2, 2, P], f32r)
        share = sb(ctx, "share", [2 * SHARES, P], f32r)
        ln0_sb = sb(ctx, "ln0_sb", [P, 2, HID], f32)
        query_sb = sb(ctx, "query_sb", [P, 2], f32)
        gath = sb(ctx, "gath", [P, SLOTS, 2, 2 * HID], f32)

        l0 = ExitStack()
        with l0:
            w_node = sb(l0, "w_node", [P, 2, 2 * HID], f32)
            w_node_hi = sb(l0, "w_node_hi", [P, 2, 2 * HID], f32r)
            w_node_lo = sb(l0, "w_node_lo", [P, 2, 2 * HID], f32r)
            w_edge = sb(l0, "w_edge", [P, 2 * HID], f32)
            w_edge_hi = sb(l0, "w_edge_hi", [P, 2 * HID], f32r)
            w_edge_lo = sb(l0, "w_edge_lo", [P, 2 * HID], f32r)
            w2_sb = sb(l0, "w2_sb", [P, 2, HID], f32)
            w2_hi = sb(l0, "w2_hi", [P, 2, HID], f32r)
            w2_lo = sb(l0, "w2_lo", [P, 2, HID], f32r)
            b_cat_sb = sb(l0, "b_cat_sb", [P, 2 * HID], f32)
            b2_sb = sb(l0, "b2_sb", [2 * SHARES, HID], f32)
            b2_parts = sb(l0, "b2_parts", [2 * SHARES, HID], f32r)
            node_row = sb(l0, "node_row", [P, 2, 2 * HID], f32)
            ea_in = sb(l0, "ea_in", [P, SLOTS, CHUNK], f32)
            ea_parts = sb(l0, "ea_parts", [P, SLOTS, CHUNK], f32r)
            relu_hi = sb(l0, "relu_hi", [P, 2, 2 * CHUNK], f32r)
            relu_lo = sb(l0, "relu_lo", [P, 2, 2 * CHUNK], f32r)
            gate = sb(l0, "gate", [P, 2, 2 * HID], f32)
            gate_in = sb(l0, "gate_in", [P, 2, 2 * HID], f32)
            msg = sb(l0, "msg", [P, 2, 2 * HID], f32)
            msg_hi = sb(l0, "msg_hi", [P, 2, 2, HID], f32r)
            msg_lo = sb(l0, "msg_lo", [P, 2, 2, HID], f32r)
            dist = sb(l0, "dist", [P, 2, 2, P], f32)
            hot = sb(l0, "hot", [P, 2, 2, P], f32r)
            nat_i = sb(l0, "nat_i", [HALF_C, 3, 2, CHUNK], i32)
            nat_f = sb(l0, "nat_f", [HALF_C, 3, 2, CHUNK], f32)
            ends_i = sb(l0, "ends_i", [HALF_C, 3, 2], i32)
            ends_w = sb(l0, "ends_w", [HALF_C, 3, 2], f32)
            count = sb(l0, "count", [HALF_C, 2], f32)
            jump = sb(l0, "jump", [HALF_C, 2], f32)
            first_b = sb(l0, "first_b", [HALF_C, 2], f32)
            last_b = sb(l0, "last_b", [HALF_C, 2], f32)
            iota_b = sb(l0, "iota_b", [HALF_C, BLOCKS], f32)
            upto = sb(l0, "upto", [HALF_C, HALF_C], f32)
            ones_c = sb(l0, "ones_c", [HALF_C, CHUNK], f32)
            passed = sb(l0, "passed", [HALF_C, 2, BLOCKS], f32)
            chosen = sb(l0, "chosen", [HALF_C, 2, BLOCKS], f32)
            win_f = sb(l0, "win_f", [1, BLOCKS], f32)
            neg_off = sb(l0, "neg_off", [1, BLOCKS], f32)
            row_b = sb(l0, "row_b", [HALF_B, 2, 2, CHUNK], bf16)

        l1 = ExitStack()
        with l1:
            agg = sb(l1, "agg", [P, WINDOWS, AGGW], f32)
            exp_col = sb(l1, "exp_col", [P, BLOCKS, 2, HEADS], f32)
            rel_parts = sb(l1, "rel_parts", [P, HID], f32r)
            rel_sb = sb(l1, "rel_sb", [P, HEAD], f32)
            wo_hi = sb(l1, "wo_hi", [P, 2, HID], f32r)
            wo_lo = sb(l1, "wo_lo", [P, 2, HID], f32r)
            qt = ExitStack()
            with qt:
                q_hi = sb(qt, "q_hi", [P, WPAD, HID], f32r)
                q_lo = sb(qt, "q_lo", [P, WPAD, HID], f32r)
                a0 = ExitStack()
                with a0:
                    wqkv_hi = sb(a0, "wqkv_hi", [P, 2, 3 * HID], f32r)
                    wqkv_lo = sb(a0, "wqkv_lo", [P, 2, 3 * HID], f32r)
                    b_qkv_sb = sb(a0, "b_qkv_sb", [P, 3 * HID], f32)
                    qkv_row = sb(a0, "qkv_row", [P, 2, 3 * HID], f32)
                    k_parts = sb(a0, "k_parts", [P, 2, 2, HID], f32r)
                a1 = ExitStack()
                with a1:
                    spread = sb(a1, "spread", [2, P], bf16)
                    block_row = sb(a1, "block_row", [2, SLOTS, 2, CHUNK], bf16)
                    hot_t = sb(a1, "hot_t", [P, 2, 2, CHUNK], f32r)
                    key_sb = sb(a1, "key_sb", [P, 2, 2, HID], f32)
                    prod = sb(a1, "prod", [P, 2, 2 * HID], f32)
            a2 = ExitStack()
            with a2:
                s_row = sb(a2, "s_row", [HALF_B, 2, HEADS, CHUNK], f32)
                m_row = sb(a2, "m_row", [HALF_B, 2, HEADS, CHUNK], f32)
                reset = sb(a2, "reset", [HALF_B, 2, HEADS * CHUNK + 1], f32)
                same = sb(a2, "same", [HALF_B, 2, 2, CHUNK], f32)
                outside = sb(a2, "outside", [HALF_B, 2, CHUNK], f32)
                tmp_row = sb(a2, "tmp_row", [HALF_B, 2, CHUNK], f32)
                follows = sb(a2, "follows", [HEADS, BLOCKS], f32)
                whole = sb(a2, "whole", [HEADS, BLOCKS], f32)
                into = sb(a2, "into", [HEADS, 2, BLOCKS], f32)
                through = sb(a2, "through", [HEADS, 2, BLOCKS], f32)
                edge_max = sb(a2, "edge_max", [HEADS, 2, BLOCKS], f32)
                run_max = sb(a2, "run_max", [HEADS, 2, BLOCKS], f32)
                carry = sb(a2, "carry", [HEADS, 2, BLOCKS], f32)
                carry_col = sb(a2, "carry_col", [HALF_B, 2, 2, HEADS], f32)
            a3 = ExitStack()
            with a3:
                weighted = sb(a3, "weighted", [P, 2, 2, AGGW], f32)
                hot1 = sb(a3, "hot1", [P, 2, 2, P], f32)
                v_in = sb(a3, "v_in", [P, 2, HID], f32)
                empty = sb(a3, "empty", [P, WINDOWS, HEADS], f32)
                denom = sb(a3, "denom", [P, WINDOWS, HEADS], f32)
                inv = sb(a3, "inv", [P, WINDOWS, HEADS], f32)
                b_o_sb = sb(a3, "b_o_sb", [2 * SHARES, HID], f32)
                b_o_parts = sb(a3, "b_o_parts", [2 * SHARES, HID], f32r)
                ln1_sb = sb(a3, "ln1_sb", [P, 2, HID], f32)
                y_out = sb(a3, "y_out", [P, 2, HID], f32)

        arriving = agg[:].rearrange("p w f -> p (w f)")
        wqkv_sb = arriving[:, 0:6 * HID].rearrange("p (c n) -> p c n", c=2)
        wo_sb = arriving[:, 6 * HID:8 * HID].rearrange("p (c n) -> p c n", c=2)

        bank = [ctx.enter_context(nc.psum_tensor(f"bank{i}", [P, 512], f32)) for i in range(8)]

        nat_in, x_in, w_in, lw_in, row_out = sem("nat_in"), sem("x_in"), sem("w_in"), sem("lw_in"), sem("row_out")
        pool_step, consts, act_consts = sem("pool_step"), sem("consts"), sem("act_consts")
        d_step, a_step = sem("d_step"), sem("a_step")
        counted, cumulated, sel_ready, rows_ready, off_ready, cols_ready, meta_ready = (
            sem(n) for n in ("counted", "cumulated", "sel_ready", "rows_ready", "off_ready", "cols_ready", "meta_ready"))
        w_hi_done, w_lo_done, wqkv_hi_done, wqkv_lo_done, bo_hi_done, bo_lo_done = (
            sem(n) for n in ("w_hi_done", "w_lo_done", "wqkv_hi_done", "wqkv_lo_done", "bo_hi_done", "bo_lo_done"))
        var_done, std_done, norm_done = sem("var_done"), sem("std_done"), sem("norm_done")
        h_done, ht_ready, ht_hi_done, ht_lo_done, proj_ready, row_ready = (
            sem(n) for n in ("h_done", "ht_ready", "ht_hi_done", "ht_lo_done", "proj_ready", "row_ready"))
        row_stored = sems("row_stored", 2)
        gath_in, ea_arrived = sems("gath_in", SLOTS), sems("ea_arrived", SLOTS)
        idx_done, ea_hi_done, ea_lo_done, z_ready, relu_hi_done, relu_lo_done, gate_done, core_ready = (
            sem(n) for n in ("idx_done", "ea_hi_done", "ea_lo_done", "z_ready", "relu_hi_done", "relu_lo_done",
                             "gate_done", "core_ready"))
        gate_ready, gate_added, msg_done, msg_hi_done, msg_lo_done, dist_done, hot_done, sum_ready, sum_added = (
            sem(n) for n in ("gate_ready", "gate_added", "msg_done", "msg_hi_done", "msg_lo_done", "dist_done", "hot_done",
                             "sum_ready", "sum_added"))
        beta_added, beta1_added, n1_done, scaled_done, x1_done = (
            sem(n) for n in ("beta_added", "beta1_added", "n1_done", "scaled_done", "x1_done"))
        h2_done, ht2_ready, ht2_hi_done, ht2_lo_done, qkv_ready, qkv_done, k_hi_done, k_lo_done, q_hi_done, q_lo_done = (
            sem(n) for n in ("h2_done", "ht2_ready", "ht2_hi_done", "ht2_lo_done", "qkv_ready", "qkv_done", "k_hi_done", "k_lo_done",
                             "q_hi_done", "q_lo_done"))
        k_stored, v_stored = sems("k_stored", 2), sems("v_stored", 2)
        brow_in, gath1_in = sems("brow_in", SLOTS), sems("gath1_in", SLOTS)
        idx1_done, spread_ready, hot_t_done, key_ready, key_copied, query_ready, prod_done, score_done = (
            sem(n) for n in ("idx1_done", "spread_ready", "hot_t_done", "key_ready", "key_copied", "query_ready",
                             "prod_done", "score_done"))
        srow_ready, local_done, lends_ready, carried, carry_ready, max_done, exp_done, expt_ready, weights_done = (
            sem(n) for n in ("srow_ready", "local_done", "lends_ready", "carried", "carry_ready", "max_done",
                             "exp_done", "expt_ready", "weights_done"))
        gath2_in = sems("gath2_in", SLOTS)
        idx2_done, weighted_done, wsum_done, hot1_done, agg_ready, agg_added = (
            sem(n) for n in ("idx2_done", "weighted_done", "wsum_done", "hot1_done", "agg_ready", "agg_added"))
        v_arrived, y_stored = sems("v_arrived", 2), sems("y_stored", 2)
        ow_in, inv_done, mean_done, mix_done, mt_ready, mt_hi_done, mt_lo_done, o_ready, o_done = (
            sem(n) for n in ("ow_in", "inv_done", "mean_done", "mix_done", "mt_ready", "mt_hi_done", "mt_lo_done",
                             "o_ready", "o_done"))
        x2_normed, x2_scaled, y_done = sem("x2_normed"), sem("x2_scaled"), sem("y_done")
        idx_seen, rel_in, rel_done, agg_zero = sem("idx_seen"), sem("rel_in"), sem("rel_done"), sem("agg_zero")

        def after(engine, signal, n):
            if not isinstance(n, int) or n > 0:
                engine.wait_ge(signal, n)

        def pipeline(engine, stages, count, body, straight=False):
            rounds = count // body

            def step(k, u):
                for stage, lag in stages:
                    if isinstance(k, int) and not 0 <= body * k + u - lag < count:
                        continue
                    stage(k + (u - lag) // body, (u - lag) % body)

            peeled = -(-(max(lag for _, lag in stages) + 2) // body)
            for k in range(peeled):
                for u in range(body):
                    step(k, u)
            if straight:
                for k in range(peeled, rounds):
                    for u in range(body):
                        step(k, u)
            else:
                with engine.Fori(peeled, rounds) as k:
                    for u in range(body):
                        step(k, u)
            for u in range(max(lag for _, lag in stages)):
                step(rounds, u)

        def node_phase_over(engine):
            for q in range(2):
                engine.wait_ge(k_stored[q], 16 * (WPAD // 2))
                engine.wait_ge(v_stored[q], 16 * (WPAD // 2))

        block = ctx.enter_context(nc.Block())

        @block.sync
        def _(sp):
            for kind, array in enumerate((src, dst, etype)):
                sp.dma_start(nat_i[:, kind, :, :], array[0:CHUNKS, :].rearrange("(g p) e -> p g e", g=2)).then_inc(nat_in, 16)
            with nc.allow_non_contiguous_dma(reason="one number a chunk"):
                sp.dma_start(ends_i[:, 2, :], dst[1:CHUNKS + 1, 0:1].rearrange("(g p) o -> p (g o)", g=2)).then_inc(nat_in, 16)
            sp.dma_start(xs[:], x.rearrange("(w p) f -> p w f", p=P)).then_inc(x_in, 16)
            sp.dma_start(w_node[:, :, 0:HID], w1[0:HID, :].rearrange("(c p) n -> p c n", p=P)).then_inc(w_in, 16)
            sp.dma_start(w_node[:, :, HID:], wg[0:HID, :].rearrange("(c p) n -> p c n", p=P)).then_inc(w_in, 16)
            sp.dma_start(b_cat_sb[:], b_cat.to_broadcast([P, 2 * HID])).then_inc(w_in, 16)
            for half in range(2):
                rows = slice(half * EDGE_DIM, (half + 1) * EDGE_DIM)
                sp.dma_start(w_edge[rows, 0:HID], w1[HID:HID + EDGE_DIM, :]).then_inc(w_in, 16)
                sp.dma_start(w_edge[rows, HID:], wg[HID:HID + EDGE_DIM, :]).then_inc(w_in, 16)
            sp.dma_start(w2_sb[:], w2.rearrange("(c p) n -> p c n", p=P)).then_inc(w_in, 16)
            sp.dma_start(b2_sb[:], b2.to_broadcast([2 * SHARES, HID])).then_inc(w_in, 16)
            for i in range(2):
                sp.dma_start(ln0_sb[:, i, :], ln0[i:i + 1, :].to_broadcast([P, HID])).then_inc(lw_in, 16)
            sp.dma_start(query_sb[:], query_col).then_inc(lw_in, 16)

            sp.wait_ge(meta_ready, 1)
            for r in range(2):
                sp.dma_start(row_tab[r * HALF_B:(r + 1) * HALF_B, :], row_b[:, r, :, :].rearrange("p k e -> p (k e)")).then_inc(row_out, 16)

            def store_rows(k, q):
                sp.wait_ge(row_ready, 2 * k + q + 1)
                sp.dma_start(edge_in_tab[ds((2 * k + q) * P, P), :], node_row[:, q, :]).then_inc(row_stored[q], 16)

            pipeline(sp, [(store_rows, 0)], WPAD, 2)

            def load_edges(k, q):
                b = SLOTS * k + q
                after(sp, ea_lo_done, b - SLOTS + 1)
                c = sp.value_load(chunk_i[0:1, ds(b, 1)], min_val=0, max_val=CHUNKS - 1)
                chunk = ea[ds(c, 1), :, :].rearrange("o d e -> (o d) e")
                for half in range(2):
                    sp.dma_start(ea_in[half * EDGE_DIM:(half + 1) * EDGE_DIM, q, :], chunk).then_inc(ea_arrived[q], 16)

            pipeline(sp, [(load_edges, 0)], BLOCKS, SLOTS)

            sp.wait_ge(sum_added, BLOCKS)
            sp.dma_start(wqkv_sb, wqkv.rearrange("(c p) n -> p c n", p=P)).then_inc(rel_in, 16)
            sp.dma_start(b_qkv_sb[:], b_qkv.to_broadcast([P, 3 * HID])).then_inc(rel_in, 16)
            for half in range(2):
                sp.dma_start(rel_sb[half * RELS:(half + 1) * RELS, :], rel).then_inc(rel_in, 16)
            sp.dma_start(wo_sb, wo.rearrange("(c p) n -> p c n", p=P)).then_inc(rel_in, 16)

            def store_values(k, q):
                w = 2 * k + q
                sp.wait_ge(qkv_done, w + 1)
                sp.dma_start(v_tab[ds(w * P, P), :], qkv_row[:, q, HID:2 * HID]).then_inc(v_stored[q], 16)

            def store_keys(k, q):
                w = 2 * k + q
                sp.wait_ge(k_lo_done, w + 1)
                sp.wait_ge(k_hi_done, w + 1)
                sp.dma_start(k_tab[ds(w * P, P), :], k_parts[:, q, :, :].bitcast(f32).rearrange("p a f -> p (a f)")).then_inc(k_stored[q], 16)

            pipeline(sp, [(store_values, 0), (store_keys, 2)], WPAD, 2)

            node_phase_over(sp)
            sp.wait_ge(q_lo_done, WPAD)
            sp.wait_ge(row_out, 32)
            sp.wait_ge(consts, 2)

            def load_block_row(k, q):
                b = SLOTS * k + q
                after(sp, spread_ready, b - SLOTS + 1)
                sp.dma_start(block_row[0:1, q, :, :].rearrange("p k e -> p (k e)"), row_tab[ds(b, 1), :]).then_inc(brow_in[q], 16)

            pipeline(sp, [(load_block_row, 0)], BLOCKS, SLOTS)

            sp.wait_ge(weights_done, 4)
            sp.dma_start(b_o_sb[:], b_o.to_broadcast([2 * SHARES, HID])).then_inc(ow_in, 16)
            for i in range(2):
                sp.dma_start(ln1_sb[:, i, :], ln1[i:i + 1, :].to_broadcast([P, HID])).then_inc(ow_in, 16)
            for w in range(WINDOWS):
                q = w % 2
                after(sp, mix_done, w - 1)
                sp.dma_start(v_in[:, q, :], v_tab[w * P:(w + 1) * P, :]).then_inc(v_arrived[q], 16)
            for w in range(WINDOWS):
                rows = min(P, NODES - w * P)
                sp.wait_ge(y_done, w + 1)
                sp.dma_start(out[w * P:w * P + rows, :], y_out[0:rows, w % 2, :]).then_inc(y_stored[w % 2], 16)
            sp.wait_ge(y_stored[0], 16 * ((WINDOWS + 1) // 2))
            sp.wait_ge(y_stored[1], 16 * (WINDOWS // 2))

        @block.gpsimd
        def _(pool):
            steps = [0]

            def step(ins):
                steps[0] += 1
                ins.then_inc(pool_step, 1)
                pool.wait_ge(pool_step, steps[0])

            g = nc.gpsimd
            g.iota(iota_b[:], pattern=[[1, BLOCKS]], base=0, channel_multiplier=0, allow_small_or_imprecise_dtypes=True)
            g.iota(iota_node[:], pattern=[[1, P]], base=0, channel_multiplier=0, allow_small_or_imprecise_dtypes=True)
            g.iota(iota_part[:], pattern=[[0, 1]], base=0, channel_multiplier=1, allow_small_or_imprecise_dtypes=True)
            g.memset(eps_col[:], EPS)
            g.memset(one_col[:], 1.0)
            g.memset(ones_c[:], 1.0)
            step(g.memset(ident[:], 0.0))
            step(g.affine_select(out=ident[:], in_=ident[:], compare_op=ALU.not_equal, fill=1.0, base=0,
                                 pattern=[[-1, P]], channel_multiplier=1))
            step(g.memset(upto[:], 1.0))
            g.affine_select(out=upto[:], in_=upto[:], compare_op=ALU.is_ge, fill=0.0, base=0,
                            pattern=[[1, HALF_C]], channel_multiplier=-1).then_inc(consts, 1)

            def gather_blocks(table, width, arrived, idx_signal, freed):
                def one(first, u, half):
                    b, q = first + u, u % SLOTS
                    if q == 0:
                        g.tensor_copy(idx[:, half, :, :], src_col[:, ds(b, SLOTS), :]).then_inc(idx_signal, 1)
                    after(pool, freed, b - SLOTS + 1)
                    if q == 0:
                        pool.wait_ge(idx_signal, b // SLOTS + 1)
                    pool.sem_inc(idx_seen, 1)
                    for i in range(2):
                        g.indirect_dma_start(gath[:, q, i, 0:width], None, table,
                                             bass.IndirectOffsetOnAxis(ap=idx[:, half, q, i:i + 1], axis=0)).then_inc(arrived[q], 16)

                for u in range(SLOTS):
                    one(0, u, 0)
                with pool.Fori(0, (BLOCKS - SLOTS) // (2 * SLOTS)) as k:
                    for u in range(2 * SLOTS):
                        one(2 * SLOTS * k + SLOTS, u, 1 - u // SLOTS)

            pool.wait_ge(meta_ready, 1)
            for q in range(2):
                pool.wait_ge(row_stored[q], 16 * (WPAD // 2))
            gather_blocks(edge_in_tab, 2 * HID, gath_in, idx_done, gate_added)
            pool.wait_ge(lw_in, 3 * 16)
            g.tensor_tensor(xs[:], xs[:], ln0_sb[:, 1:2, :].to_broadcast([P, WPAD, HID]), ALU.add).then_inc(beta_added, 1)

            node_phase_over(pool)
            step(g.memset(spread[:], 1.0))
            step(g.affine_select(out=spread[:], in_=spread[:], compare_op=ALU.is_equal, fill=float(RELS), base=0,
                                 pattern=[[0, P]], channel_multiplier=1))
            step(g.affine_select(out=spread[:], in_=spread[:], compare_op=ALU.is_ge, fill=0.0, base=0,
                                 pattern=[[1, P]], channel_multiplier=-RELS))
            step(g.memset(block_row[:], 0.0))
            g.affine_select(out=block_row[:], in_=block_row[:], compare_op=ALU.is_ge, fill=1.0, base=1,
                            pattern=[[0, SLOTS], [-1, 2], [0, CHUNK]], channel_multiplier=-1).then_inc(consts, 1)
            gather_blocks(k_tab, 2 * HID, gath1_in, idx1_done, key_ready)
            pool.wait_ge(key_ready, BLOCKS)
            g.memset(agg[:], 0.0).then_inc(agg_zero, 1)
            gather_blocks(v_tab, HID, gath2_in, idx2_done, weighted_done)

            pool.wait_ge(ow_in, 3 * 16)
            g.tensor_tensor(xs[:], xs[:], ln1_sb[:, 1:2, :].to_broadcast([P, WPAD, HID]), ALU.add).then_inc(beta1_added, 1)
            pool.wait_ge(inv_done, 1)
            for w in range(WINDOWS):
                heads = agg[:, w, 0:HID].rearrange("p (h d) -> p h d", h=HEADS)
                g.tensor_tensor(heads, heads, inv[:, w, :].unsqueeze(2).to_broadcast([P, HEADS, HEAD]), ALU.mult).then_inc(mean_done, 1)

        @block.scalar
        def _(act):
            s = nc.scalar
            act.wait_ge(consts, 1)
            s.copy(ident_r[:], ident[:]).then_inc(act_consts, 1)
            s.mul(share[:], ones_c[0:2 * SHARES, 0:P], 1 / SHARES).then_inc(act_consts, 1)
            act.wait_ge(w_in, 9 * 16)
            s.copy(w_node_hi[:], w_node[:]).then_inc(w_hi_done, 1)
            s.copy(w_edge_hi[:], w_edge[:]).then_inc(w_hi_done, 1)
            s.copy(w2_hi[:], w2_sb[:]).then_inc(w_hi_done, 1)
            s.copy(b2_parts[:], b2_sb[:]).then_inc(w_hi_done, 1)

            def normed(done):
                def stage(k, q):
                    w = 2 * k + q
                    s.activation(hs[:, ds(w, 1), :].rearrange("p o f -> p (o f)"),
                                 xs[:, ds(w, 1), :].rearrange("p o f -> p (o f)"), ACT.Relu,
                                 bias=shift[:, ds(w, 1)], scale=rstd[:, ds(w, 1)]).then_inc(done, 1)
                return stage

            def high_rows(k, q):
                w = 2 * k + q
                act.wait_ge(ht_ready, w + 1)
                after(act, proj_ready, w - 1)
                s.copy(ht_hi[:, q, :, :], bank[q][:, 0:HID].rearrange("p (c n) -> p c n", c=2)).then_inc(ht_hi_done, 1)

            act.wait_ge(var_done, 1)
            s.activation(std[:], mean_var[:, :, 1], ACT.Sqrt, bias=eps_col[:]).then_inc(std_done, 1)
            act.wait_ge(norm_done, 1)
            pipeline(act, [(normed(h_done), 0), (high_rows, 1)], WPAD, 2)

            def split_edges(k, q):
                b = SLOTS * k + q
                act.wait_ge(ea_arrived[q], 32 * (k + 1))
                after(act, z_ready, b - SLOTS + 1)
                s.copy(ea_parts[:, q, :], ea_in[:, q, :]).then_inc(ea_hi_done, 1)

            def relu_inner(k, q):
                b = SLOTS * k + q
                act.wait_ge(z_ready, b + 1)
                after(act, core_ready, b - 1)
                s.activation(relu_hi[:, q % 2, :], bank[q % 2][:], ACT.Relu).then_inc(relu_hi_done, 1)

            def gates(k, q):
                b = SLOTS * k + q
                act.wait_ge(gate_added, b + 1)
                after(act, msg_done, b - 1)
                s.activation(gate[:, q % 2, :], gate_in[:, q % 2, :], ACT.Sigmoid).then_inc(gate_done, 1)

            def high_message(k, q):
                b = SLOTS * k + q
                act.wait_ge(msg_done, b + 1)
                after(act, sum_ready, b - 1)
                s.copy(msg_hi[:, q % 2, :, :].rearrange("p i f -> p (i f)"), msg[:, q % 2, :]).then_inc(msg_hi_done, 1)

            def distances(k, q):
                b = SLOTS * k + q
                after(act, hot_done, b - 1)
                for i in range(2):
                    last = s.activation(dist[:, q % 2, i, :], iota_node[:], ACT.Square, bias=rel_col[:, ds(b, 1), i], scale=-1.0)
                last.then_inc(dist_done, 1)

            def one_hot(k, q):
                b = SLOTS * k + q
                act.wait_ge(dist_done, b + 1)
                after(act, sum_ready, b - 1)
                s.activation(hot[:, q % 2, :, :], dist[:, q % 2, :, :], ACT.Relu, bias=one_col[:], scale=-1.0).then_inc(hot_done, 1)

            pipeline(act, [(split_edges, 0), (distances, 3), (relu_inner, 2), (one_hot, 4), (high_message, 4), (gates, 3)], BLOCKS, SLOTS)

            act.wait_ge(var_done, 2)
            s.activation(std[:], mean_var[:, :, 1], ACT.Sqrt, bias=eps_col[:]).then_inc(std_done, 1)
            act.wait_ge(norm_done, 2)

            def norm_messages(k, q):
                w = 2 * k + q
                rows = hs[:, ds(w, 1), :].rearrange("p o f -> p (o f)")
                s.activation(rows, rows, ACT.Identity, bias=shift[:, ds(w, 1)], scale=rstd[:, ds(w, 1)]).then_inc(n1_done, 1)

            pipeline(act, [(norm_messages, 0)], WPAD, 2)
            act.wait_ge(rel_in, 5 * 16)
            s.copy(wqkv_hi[:], wqkv_sb).then_inc(wqkv_hi_done, 1)
            s.copy(wo_hi[:], wo_sb).then_inc(wqkv_hi_done, 1)
            act.wait_ge(var_done, 3)
            s.activation(std[:], mean_var[:, :, 1], ACT.Sqrt, bias=eps_col[:]).then_inc(std_done, 1)
            act.wait_ge(norm_done, 3)
            act.wait_ge(lw_in, 3 * 16)
            for h in range(HEADS):
                last = s.mul(rel_parts[:, h * HEAD:(h + 1) * HEAD], rel_sb[:], 0.2)
            last.then_inc(rel_done, 1)
            s.mul(query_sb[:], query_sb[:], 0.1).then_inc(a_step, 1)
            act.wait_ge(a_step, 1)

            def enhance(k, q):
                w = 2 * k + q
                act.wait_ge(ht2_ready, w + 1)
                after(act, qkv_ready, w - 1)
                for c in range(2):
                    last = s.activation(ht_hi[:, q, c, :], bank[q][:, c * P:(c + 1) * P], ACT.Identity, bias=query_sb[:, c:c + 1])
                last.then_inc(ht2_hi_done, 1)

            def high_parts(k, q):
                w = 2 * k + q
                act.wait_ge(qkv_done, w + 1)
                if not isinstance(w, int) or w >= 2:
                    act.wait_ge(k_stored[q], 16 * k)
                s.copy(k_parts[:, q, 0, :], qkv_row[:, q, 0:HID]).then_inc(k_hi_done, 1)
                s.mul(q_hi[:, ds(w, 1), :].rearrange("p o f -> p (o f)"), qkv_row[:, q, 2 * HID:], 1 / HEAD ** 0.5).then_inc(q_hi_done, 1)

            pipeline(act, [(enhance, 1), (normed(h2_done), 0), (high_parts, 3)], WPAD, 2)

            def copy_keys(k, q):
                b = SLOTS * k + q
                act.wait_ge(key_ready, b + 1)
                after(act, prod_done, b - 1)
                s.copy(key_sb[:, q % 2, :, :].rearrange("p i f -> p (i f)"), bank[2 + q % 2][:]).then_inc(key_copied, 1)

            node_phase_over(act)
            pipeline(act, [(copy_keys, 0)], BLOCKS, SLOTS)

            act.wait_ge(max_done, 1)
            flat = m_row[:].rearrange("p r h e -> p (r h e)")
            s.activation(flat, flat, ACT.Exp).then_inc(exp_done, 1)

            def weight_sums(k, q):
                b = SLOTS * k + q
                after(act, agg_ready, b - 1)
                s.copy(weighted[:, q % 2, :, HID:], exp_col[:, ds(b, 1), :, :].rearrange("p o i h -> p (o i) h")).then_inc(wsum_done, 1)

            act.wait_ge(weights_done, 4)
            pipeline(act, [(weight_sums, 0)], BLOCKS, SLOTS)

            act.wait_ge(ow_in, 3 * 16)
            s.copy(b_o_parts[:], b_o_sb[:]).then_inc(bo_hi_done, 1)
            for w in range(WINDOWS):
                act.wait_ge(mt_ready, w + 1)
                after(act, o_ready, w - 1)
                s.copy(ht_hi[:, w % 2, :, :], bank[w % 2][:, 0:HID].rearrange("p (c n) -> p c n", c=2)).then_inc(mt_hi_done, 1)
            act.wait_ge(var_done, 4)
            s.activation(std[:, 0:WINDOWS], mean_var[:, 0:WINDOWS, 1], ACT.Sqrt, bias=eps_col[:]).then_inc(std_done, 1)
            act.wait_ge(norm_done, 4)
            for w in range(WINDOWS):
                s.activation(hs[:, w, :], hs[:, w, :], ACT.Identity, bias=shift[:, w:w + 1], scale=rstd[:, w:w + 1]).then_inc(x2_normed, 1)

        @block.vector
        def _(dve):
            v = nc.vector
            steps = [0]

            def step(ins):
                steps[0] += 1
                ins.then_inc(d_step, 1)
                dve.wait_ge(d_step, steps[0])

            dve.wait_ge(nat_in, 4 * 16)
            dve.wait_ge(consts, 1)
            v.tensor_copy(ends_i[:, 0, :], nat_i[:, 1, :, 0])
            step(v.tensor_copy(ends_i[:, 1, :], nat_i[:, 1, :, CHUNK - 1]))
            step(v.tensor_scalar(ends_i[:], ends_i[:], P.bit_length() - 1, None, ALU.arith_shift_right))
            step(v.tensor_copy(nat_f[:], nat_i[:]))
            step(v.tensor_scalar(ends_w[:], ends_i[:], float(WINDOWS - 1), None, ALU.min))
            v.scalar_tensor_tensor(count[:], in0=ends_w[:, 1, :], scalar=1.0, in1=ends_w[:, 0, :], op0=ALU.add, op1=ALU.subtract).then_inc(counted, 1)
            v.scalar_tensor_tensor(jump[:], in0=ends_w[:, 2, :], scalar=-1.0, in1=ends_w[:, 1, :], op0=ALU.add, op1=ALU.subtract).then_inc(counted, 1)
            dve.wait_ge(cumulated, 1)
            step(v.tensor_copy(last_b[:], bank[0][0:HALF_C, 0:2]))
            step(v.tensor_tensor(first_b[:], last_b[:], count[:], ALU.subtract))
            for c in range(2):
                v.tensor_scalar(passed[:, c, :], iota_b[:], last_b[:, c:c + 1], None, ALU.is_ge)
                step(v.tensor_scalar(chosen[:, c, :], iota_b[:], first_b[:, c:c + 1], None, ALU.is_ge))
            v.tensor_tensor(chosen[:], chosen[:], passed[:], ALU.subtract).then_inc(sel_ready, 1)
            dve.wait_ge(rows_ready, 1)
            v.tensor_scalar(chunk_i[:], bank[0][0:1, 0:BLOCKS], float(CHUNKS - 1), None, ALU.min)
            step(v.tensor_tensor(win_f[:], bank[1][0:1, 0:BLOCKS], iota_b[0:1, :], ALU.add))
            step(v.tensor_scalar(win_f[:], win_f[:], ends_w[0:1, 0, 0:1], None, ALU.add))
            step(v.tensor_tensor(win_f[:], win_f[:], bank[2][0:1, 0:BLOCKS], ALU.mult))
            v.tensor_copy(win_i[:], win_f[:])
            step(v.tensor_scalar(neg_off[:], bank[2][0:1, 0:BLOCKS], -FAR, FAR, ALU.mult, ALU.add))
            v.scalar_tensor_tensor(neg_off[:], in0=win_f[:], scalar=-float(P), in1=neg_off[:], op0=ALU.mult, op1=ALU.add).then_inc(off_ready, 1)
            dve.wait_ge(cols_ready, 1)
            v.tensor_copy(src_col[:].rearrange("p b i -> p i b"), bank[0][:, 0:2 * BLOCKS].rearrange("p (i b) -> p i b", i=2))
            v.tensor_copy(rel_col[:].rearrange("p b i -> p i b"), bank[1][:, 0:2 * BLOCKS].rearrange("p (i b) -> p i b", i=2))
            v.tensor_copy(ends_row[:], bank[4][0:HEADS, 0:2 * BLOCKS].rearrange("p (i b) -> p i b", i=2))
            step(v.tensor_scalar(dst_row[:], bank[2][0:HALF_B, :].rearrange("p (r e) -> p r e", r=2), 255.0, -1.0, ALU.min, ALU.max))
            v.tensor_copy(row_b[:, :, 1, :], bank[3][0:HALF_B, :].rearrange("p (r e) -> p r e", r=2))
            v.tensor_copy(row_b[:, :, 0, :], dst_row[:]).then_inc(meta_ready, 1)

            dve.wait_ge(w_hi_done, 4)
            v.tensor_tensor(w_node_lo[:], w_node[:], w_node_hi[:], ALU.subtract).then_inc(w_lo_done, 1)
            v.tensor_tensor(w_edge_lo[:], w_edge[:], w_edge_hi[:], ALU.subtract)
            v.tensor_tensor(b2_parts[SHARES:, :], b2_sb[SHARES:, :], b2_parts[SHARES:, :], ALU.subtract)
            v.tensor_tensor(w2_lo[:], w2_sb[:], w2_hi[:], ALU.subtract).then_inc(w_lo_done, 1)

            def row_statistics(rows, w):
                v.bn_stats(stats[:, ds(w, 1), :].rearrange("p o s -> p (o s)"), rows[:, ds(w, 1), :].rearrange("p o f -> p (o f)"))

            def aggregate_statistics(n):
                step(v.engine_nop())
                for w in range(n):
                    last = v.bn_aggr(mean_var[:, w, :], stats[:, w, :])
                last.then_inc(var_done, 1)

            def statistics(rows):
                pipeline(dve, [(lambda k, q: row_statistics(rows, 2 * k + q), 0)], WPAD, 2)
                aggregate_statistics(WPAD)

            def scale_and_shift(n):
                dve.wait_ge(std_done, n)
                step(v.reciprocal(rstd[:], std[:]))
                v.scalar_tensor_tensor(shift[:], in0=mean_var[:, :, 0], scalar=-1.0, in1=rstd[:], op0=ALU.mult, op1=ALU.mult).then_inc(norm_done, 1)

            dve.wait_ge(x_in, 16)
            statistics(xs)
            scale_and_shift(1)

            def low_rows(k, q):
                w = 2 * k + q
                dve.wait_ge(ht_hi_done, w + 1)
                v.tensor_tensor(ht_lo[:, q, :, :], bank[q][:, 0:HID].rearrange("p (c n) -> p c n", c=2), ht_hi[:, q, :, :],
                                ALU.subtract).then_inc(ht_lo_done, 1)

            def add_bias(k, q):
                w = 2 * k + q
                dve.wait_ge(proj_ready, w + 1)
                if not isinstance(w, int) or w >= 2:
                    dve.wait_ge(row_stored[q], 16 * k)
                v.tensor_tensor(node_row[:, q, :], bank[2 + q][:], b_cat_sb[:], ALU.add).then_inc(row_ready, 1)

            pipeline(dve, [(low_rows, 0), (add_bias, 1)], WPAD, 2)

            def low_edges(k, q):
                b = SLOTS * k + q
                dve.wait_ge(ea_hi_done, b + 1)
                rows = slice(EDGE_DIM, 2 * EDGE_DIM)
                v.tensor_tensor(ea_parts[rows, q, :], ea_in[rows, q, :], ea_parts[rows, q, :], ALU.subtract).then_inc(ea_lo_done, 1)

            def low_relu(k, q):
                b = SLOTS * k + q
                dve.wait_ge(relu_hi_done, b + 1)
                v.scalar_tensor_tensor(relu_lo[:, q % 2, :], in0=bank[q % 2][:], scalar=0.0, in1=relu_hi[:, q % 2, :],
                                       op0=ALU.max, op1=ALU.subtract).then_inc(relu_lo_done, 1)

            def add_gate(k, q):
                b = SLOTS * k + q
                dve.wait_ge(gath_in[q], 32 * (k + 1))
                dve.wait_ge(gate_ready, b + 1)
                after(dve, gate_done, b - 1)
                v.tensor_tensor(gate_in[:, q % 2, :].rearrange("p (i f) -> p i f", i=2),
                                bank[2 + q % 2][:].rearrange("p (i f) -> p i f", i=2), gath[:, q, :, HID:],
                                ALU.add).then_inc(gate_added, 1)

            def message(k, q):
                b = SLOTS * k + q
                dve.wait_ge(core_ready, b + 1)
                dve.wait_ge(gate_done, b + 1)
                after(dve, msg_lo_done, b - 1)
                v.tensor_tensor(msg[:, q % 2, :], bank[4 + q % 2][:], gate[:, q % 2, :], ALU.mult).then_inc(msg_done, 1)

            def low_message(k, q):
                b = SLOTS * k + q
                dve.wait_ge(msg_hi_done, b + 1)
                v.tensor_tensor(msg_lo[:, q % 2, :, :].rearrange("p i f -> p (i f)"), msg[:, q % 2, :],
                                msg_hi[:, q % 2, :, :].rearrange("p i f -> p (i f)"), ALU.subtract).then_inc(msg_lo_done, 1)

            def add_sums(k, q):
                b = SLOTS * k + q
                dve.wait_ge(sum_ready, b + 1)
                after(dve, sum_added, b)
                w = dve.value_load(win_i[0:1, ds(b, 1)], min_val=0, max_val=WINDOWS - 1)
                rows = hs[:, ds(w, 1), :].rearrange("p o f -> p (o f)")
                v.tensor_tensor(rows, rows, bank[6 + q % 2][:, 0:HID], ALU.add).then_inc(sum_added, 1)

            pipeline(dve, [(message, 3), (low_relu, 2), (add_gate, 2), (low_edges, 0), (low_message, 3), (add_sums, 4)],
                     BLOCKS, SLOTS)
            dve.wait_ge(sum_added, BLOCKS)

            statistics(hs)
            scale_and_shift(2)
            dve.wait_ge(beta_added, 1)

            def scale(k, q):
                w = 2 * k + q
                dve.wait_ge(n1_done, w + 1)
                rows = hs[:, ds(w, 1), :].rearrange("p o f -> p (o f)")
                v.tensor_tensor(rows, rows, ln0_sb[:, 0, :], ALU.mult).then_inc(scaled_done, 1)

            def residual(k, q):
                w = 2 * k + q
                dve.wait_ge(scaled_done, w + 1)
                hrow, xrow = (t[:, ds(w, 1), :].rearrange("p o f -> p (o f)") for t in (hs, xs))
                v.tensor_tensor(xrow, xrow, hrow, ALU.add).then_inc(x1_done, 1)

            def x1_stats(k, q):
                w = 2 * k + q
                dve.wait_ge(x1_done, w + 1)
                row_statistics(xs, w)

            pipeline(dve, [(scale, 0), (residual, 1), (x1_stats, 2)], WPAD, 2)
            aggregate_statistics(WPAD)
            scale_and_shift(3)

            dve.wait_ge(wqkv_hi_done, 2)
            v.tensor_tensor(wqkv_lo[:], wqkv_sb, wqkv_hi[:], ALU.subtract)
            v.tensor_tensor(wo_lo[:], wo_sb, wo_hi[:], ALU.subtract).then_inc(wqkv_lo_done, 1)
            dve.wait_ge(rel_done, 1)
            for h in range(HEADS):
                last = v.scalar_tensor_tensor(rel_parts[RELS:, h * HEAD:(h + 1) * HEAD], in0=rel_sb[RELS:, :], scalar=0.2,
                                              in1=rel_parts[RELS:, h * HEAD:(h + 1) * HEAD], op0=ALU.mult, op1=ALU.subtract)
            last.then_inc(rel_done, 1)

            def low_enhanced(k, q):
                w = 2 * k + q
                dve.wait_ge(ht2_hi_done, w + 1)
                for c in range(2):
                    last = v.scalar_tensor_tensor(ht_lo[:, q, c, :], in0=bank[q][:, c * P:(c + 1) * P], scalar=query_sb[:, c:c + 1],
                                                  in1=ht_hi[:, q, c, :], op0=ALU.add, op1=ALU.subtract)
                last.then_inc(ht2_lo_done, 1)

            def qkv_bias(k, q):
                w = 2 * k + q
                dve.wait_ge(qkv_ready, w + 1)
                if not isinstance(w, int) or w >= 2:
                    dve.wait_ge(v_stored[q], 16 * k)
                after(dve, q_hi_done, w - 1)
                after(dve, q_lo_done, w - 1)
                v.tensor_tensor(qkv_row[:, q, 0:2 * HID], bank[2 + q][:], b_qkv_sb[:, 0:2 * HID], ALU.add)
                v.tensor_tensor(qkv_row[:, q, 2 * HID:], bank[4 + q][:, 0:HID], b_qkv_sb[:, 2 * HID:], ALU.add).then_inc(qkv_done, 1)

            def low_parts(k, q):
                w = 2 * k + q
                dve.wait_ge(k_hi_done, w + 1)
                v.tensor_tensor(k_parts[:, q, 1, :], qkv_row[:, q, 0:HID], k_parts[:, q, 0, :], ALU.subtract).then_inc(k_lo_done, 1)
                dve.wait_ge(q_hi_done, w + 1)
                hi, lo = (t[:, ds(w, 1), :].rearrange("p o f -> p (o f)") for t in (q_hi, q_lo))
                v.scalar_tensor_tensor(lo, in0=qkv_row[:, q, 2 * HID:], scalar=1 / HEAD ** 0.5, in1=hi,
                                       op0=ALU.mult, op1=ALU.subtract).then_inc(q_lo_done, 1)

            pipeline(dve, [(low_enhanced, 0), (qkv_bias, 1), (low_parts, 2)], WPAD, 2)

            def one_hot_t(k, q):
                b = SLOTS * k + q
                dve.wait_ge(spread_ready, b + 1)
                after(dve, query_ready, b - 1)
                v.tensor_scalar(hot_t[:, q % 2, :, :].rearrange("p k e -> p (k e)"), bank[q % 2][:], iota_part[:], None,
                                ALU.is_equal).then_inc(hot_t_done, 1)

            def products(k, q):
                b = SLOTS * k + q
                dve.wait_ge(key_copied, b + 1)
                dve.wait_ge(query_ready, b + 1)
                after(dve, score_done, b - 1)
                v.tensor_tensor(prod[:, q % 2, :], bank[4 + q % 2][:], key_sb[:, q % 2, :, :].rearrange("p i f -> p (i f)"),
                                ALU.mult).then_inc(prod_done, 1)

            def scores(k, q):
                b = SLOTS * k + q
                dve.wait_ge(prod_done, b + 1)
                v.tensor_reduce(out=exp_col[:, ds(b, 1), :, :].rearrange("p o i h -> p (o i h)"),
                                in_=prod[:, q % 2, :].rearrange("p (j d) -> p j d", d=HEAD), axis=AX.X, op=ALU.add).then_inc(score_done, 1)

            node_phase_over(dve)
            dve.wait_ge(consts, 2)
            pipeline(dve, [(scores, 2), (one_hot_t, 0), (products, 1)], BLOCKS, SLOTS)
            dve.wait_ge(score_done, BLOCKS)
            dve.wait_ge(key_ready, BLOCKS)

            step(v.tensor_scalar(outside[:], dst_row[:], 0.0, BIG, ALU.is_ge, ALU.mult))
            step(v.tensor_scalar(tmp_row[:], dst_row[:], float(P - 1), BIG, ALU.is_le, ALU.mult))
            step(v.tensor_tensor(outside[:], outside[:], tmp_row[:], ALU.add))
            step(v.tensor_scalar(outside[:], outside[:], 2 * BIG, None, ALU.subtract))
            step(v.memset(reset[:], -BIG))
            step(v.tensor_tensor(tmp_row[:, :, 1:], dst_row[:, :, 1:], dst_row[:, :, 0:CHUNK - 1], ALU.is_equal))
            for r in range(2):
                for h in range(HEADS):
                    last = v.tensor_scalar(reset[:, r, h * CHUNK + 1:(h + 1) * CHUNK], tmp_row[:, r, 1:], BIG, BIG, ALU.mult, ALU.subtract)
            step(last)
            for r in range(2):
                for i, e in enumerate((0, CHUNK - 1)):
                    step(v.tensor_scalar(same[:, r, i, :], dst_row[:, r, :], dst_row[:, r, e:e + 1], BIG, ALU.is_equal, ALU.mult))
            step(v.tensor_scalar(same[:], same[:], BIG, None, ALU.subtract))
            step(v.memset(follows[:], 0.0))
            v.tensor_tensor(follows[:, 1:], ends_row[:, 0, 1:], ends_row[:, 1, 0:BLOCKS - 1], ALU.is_equal)
            step(v.tensor_tensor(whole[:], ends_row[:, 0, :], ends_row[:, 1, :], ALU.is_equal))
            step(v.memset(into[:], 0.0))
            step(v.tensor_copy(into[:, 0, :], follows[:]))
            step(v.tensor_copy(into[:, 1, 0:BLOCKS - 1], follows[:, 1:]))
            for i in range(2):
                step(v.tensor_tensor(through[:, i, :], into[:, i, :], whole[:], ALU.mult))
            step(v.tensor_scalar(into[:], into[:], BIG, BIG, ALU.mult, ALU.subtract))
            step(v.tensor_scalar(through[:], through[:], BIG, BIG, ALU.mult, ALU.subtract))
            dve.wait_ge(srow_ready, 1)
            for r in range(2):
                for hp in range(2):
                    for j in range(2):
                        last = v.tensor_tensor(s_row[:, r, 2 * hp + j, :], bank[2 * r + hp][0:HALF_B, j * CHUNK:(j + 1) * CHUNK],
                                               outside[:, r, :], ALU.add)
            step(last)
            for r in range(2):
                rows = m_row[:, r, :, :].rearrange("p h e -> p (h e)")
                step(v.tensor_tensor_scan(rows, reset[:, r, 0:HEADS * CHUNK], s_row[:, r, :, :].rearrange("p h e -> p (h e)"), -BIG, ALU.add, ALU.max))
            for r in range(2):
                rows = m_row[:, r, :, :].rearrange("p h e -> p (h e)")
                last = v.tensor_tensor_scan(rows[:, ::-1], reset[:, r, HEADS * CHUNK:0:-1], rows[:, ::-1], -BIG, ALU.add, ALU.max)
            last.then_inc(local_done, 1)
            dve.wait_ge(lends_ready, 1)
            for i in range(2):
                last = v.tensor_copy(edge_max[:, i, :], bank[4 + i][0:HEADS, 0:BLOCKS])
            step(last)
            v.tensor_tensor_scan(run_max[:, 0, :], through[:, 0, :], edge_max[:, 1, :], -BIG, ALU.add, ALU.max)
            step(v.tensor_tensor_scan(run_max[:, 1, ::-1], through[:, 1, ::-1], edge_max[:, 0, ::-1], -BIG, ALU.add, ALU.max))
            step(v.memset(carry[:], -BIG))
            v.tensor_tensor(carry[:, 0, 1:], run_max[:, 0, 0:BLOCKS - 1], into[:, 0, 1:], ALU.add)
            v.tensor_tensor(carry[:, 1, 0:BLOCKS - 1], run_max[:, 1, 1:], into[:, 1, 0:BLOCKS - 1], ALU.add).then_inc(carried, 1)
            dve.wait_ge(carry_ready, 1)
            step(v.tensor_copy(carry_col[:], bank[6][0:HALF_B, 0:4 * HEADS].rearrange("p (r i h) -> p r i h", r=2, i=2)))
            for i in range(2):
                for r in range(2):
                    for h in range(HEADS):
                        last = v.scalar_tensor_tensor(m_row[:, r, h, :], in0=same[:, r, i, :], scalar=carry_col[:, r, i, h:h + 1],
                                                      in1=m_row[:, r, h, :], op0=ALU.add, op1=ALU.max)
                step(last)
            v.tensor_tensor(m_row[:], s_row[:], m_row[:], ALU.subtract).then_inc(max_done, 1)
            for r in range(2):
                for i in range(2):
                    dve.wait_ge(expt_ready, 2 * r + i + 1)
                    v.tensor_copy(exp_col[:, r * HALF_B:(r + 1) * HALF_B, i, :].rearrange("p b h -> p h b"),
                                  bank[2 * r + i][:, 0:HEADS * HALF_B].rearrange("p (h b) -> p h b", h=HEADS)).then_inc(weights_done, 1)
            dve.wait_ge(weights_done, 4)

            def weight_values(k, q):
                b = SLOTS * k + q
                dve.wait_ge(gath2_in[q], 32 * (k + 1))
                after(dve, agg_ready, b - 1)
                for i in range(2):
                    last = v.tensor_tensor(
                        weighted[:, q % 2, i, 0:HID].rearrange("p (h d) -> p h d", h=HEADS),
                        gath[:, q, i, 0:HID].rearrange("p (h d) -> p h d", h=HEADS),
                        exp_col[:, ds(b, 1), i, :].rearrange("p o h -> p h o").to_broadcast([P, HEADS, HEAD]), ALU.mult)
                last.then_inc(weighted_done, 1)
                for i in range(2):
                    last = v.tensor_scalar(hot1[:, q % 2, i, :], iota_node[:], rel_col[:, ds(b, 1), i], None, ALU.is_equal)
                last.then_inc(hot1_done, 1)

            def add_agg(k, q):
                b = SLOTS * k + q
                dve.wait_ge(agg_ready, b + 1)
                after(dve, agg_added, b)
                w = dve.value_load(win_i[0:1, ds(b, 1)], min_val=0, max_val=WINDOWS - 1)
                rows = agg[:, ds(w, 1), :].rearrange("p o f -> p (o f)")
                v.tensor_tensor(rows, rows, bank[q % 2][:, 0:AGGW], ALU.add).then_inc(agg_added, 1)

            dve.wait_ge(agg_zero, 1)
            pipeline(dve, [(weight_values, 0), (add_agg, 2)], BLOCKS, SLOTS)
            dve.wait_ge(agg_added, BLOCKS)

            step(v.tensor_scalar(empty[:], agg[:, :, HID:], 0.0, None, ALU.is_equal))
            step(v.tensor_tensor(denom[:], agg[:, :, HID:], empty[:], ALU.add))
            v.reciprocal(inv[:], denom[:]).then_inc(inv_done, 1)
            dve.wait_ge(bo_hi_done, 1)
            v.tensor_tensor(b_o_parts[SHARES:, :], b_o_sb[SHARES:, :], b_o_parts[SHARES:, :], ALU.subtract).then_inc(bo_lo_done, 1)

            def mix(w):
                dve.wait_ge(v_arrived[w % 2], 16 * (w // 2 + 1))
                dve.wait_ge(mean_done, w + 1)
                v.scalar_tensor_tensor(agg[:, w, 0:HID], in0=v_in[:, w % 2, :], scalar=empty[:, w, 0:1], in1=agg[:, w, 0:HID],
                                       op0=ALU.mult, op1=ALU.add).then_inc(mix_done, 1)

            def low_mixed(w):
                dve.wait_ge(mt_hi_done, w + 1)
                v.tensor_tensor(ht_lo[:, w % 2, :, :], bank[w % 2][:, 0:HID].rearrange("p (c n) -> p c n", c=2),
                                ht_hi[:, w % 2, :, :], ALU.subtract).then_inc(mt_lo_done, 1)

            def add_h(w):
                dve.wait_ge(o_ready, w + 1)
                v.tensor_tensor(hs[:, w, :], hs[:, w, :], bank[2 + w % 2][:, 0:HID], ALU.add).then_inc(o_done, 1)

            def out_stats(w):
                dve.wait_ge(o_done, w + 1)
                row_statistics(hs, w)

            for w in range(WINDOWS + 4):
                for stage, lag in ((mix, 0), (low_mixed, 1), (add_h, 3), (out_stats, 4)):
                    if 0 <= w - lag < WINDOWS:
                        stage(w - lag)
            aggregate_statistics(WINDOWS)
            scale_and_shift(4)
            dve.wait_ge(beta1_added, 1)
            for w in range(WINDOWS + 1):
                if w < WINDOWS:
                    dve.wait_ge(x2_normed, w + 1)
                    v.tensor_tensor(hs[:, w, :], hs[:, w, :], ln1_sb[:, 0, :], ALU.mult).then_inc(x2_scaled, 1)
                if w >= 1:
                    q = (w - 1) % 2
                    dve.wait_ge(x2_scaled, w)
                    if w >= 3:
                        dve.wait_ge(y_stored[q], 16 * ((w - 1) // 2))
                    v.tensor_tensor(y_out[:, q, :], hs[:, w - 1, :], xs[:, w - 1, :], ALU.add).then_inc(y_done, 1)

        @block.tensor
        def _(pe):
            def mm(out_, lhs, rhs, start, stop):
                return nc.tensor.matmul(out_, lhsT=lhs, rhs=rhs, start=start, stop=stop)

            def tr(out_, in_, start=True, stop=True):
                return nc.tensor.matmul(out_, lhsT=in_, rhs=ident[:], is_transpose=True, start=start, stop=stop)

            pe.wait_ge(consts, 1)
            pe.wait_ge(counted, 2)
            mm(bank[0][0:HALF_C, 0:2], upto[:], count[:], True, False)
            mm(bank[0][0:HALF_C, 1:2], ones_c[:, 0:HALF_C], count[:, 0:1], False, True).then_inc(cumulated, 1)
            pe.wait_ge(sel_ready, 1)
            for c in range(2):
                mm(bank[0][0:1, 0:BLOCKS], ones_c[:, 0:1], passed[:, c, :], c == 0, c == 1)
            for c in range(2):
                mm(bank[1][0:1, 0:BLOCKS], jump[:, c:c + 1], passed[:, c, :], c == 0, c == 1)
            for c in range(2):
                last = mm(bank[2][0:1, 0:BLOCKS], ones_c[:, 0:1], chosen[:, c, :], c == 0, c == 1)
            last.then_inc(rows_ready, 1)
            pe.wait_ge(off_ready, 1)
            for i in range(2):
                cols = slice(i * BLOCKS, (i + 1) * BLOCKS)
                for c in range(2):
                    mm(bank[0][:, cols], nat_f[:, 0, c, i * P:(i + 1) * P], chosen[:, c, :], c == 0, c == 1)
                for c in range(2):
                    mm(bank[1][:, cols], nat_f[:, 1, c, i * P:(i + 1) * P], chosen[:, c, :], c == 0, False)
                mm(bank[1][:, cols], ones_c[0:1, 0:P], neg_off[:], False, True)
                e = i * (CHUNK - 1)
                for c in range(2):
                    mm(bank[4][0:HEADS, cols], nat_f[:, 1, c, e:e + 1].to_broadcast([HALF_C, HEADS]), chosen[:, c, :], c == 0, c == 1)
            for r in range(2):
                some = slice(r * HALF_B, (r + 1) * HALF_B)
                cols = slice(r * CHUNK, (r + 1) * CHUNK)
                for c in range(2):
                    mm(bank[2][0:HALF_B, cols], chosen[:, c, some], nat_f[:, 1, c, :], c == 0, False)
                mm(bank[2][0:HALF_B, cols], neg_off[0:1, some], ones_c[0:1, :], False, True)
                for c in range(2):
                    last = mm(bank[3][0:HALF_B, cols], chosen[:, c, some], nat_f[:, 2, c, :], c == 0, c == 1)
            last.then_inc(cols_ready, 1)
            pe.wait_ge(meta_ready, 1)
            pe.wait_ge(w_in, 9 * 16)

            def transpose_rows(rows, source_done, freed, ready):
                def stage(k, q):
                    w = 2 * k + q
                    pe.wait_ge(source_done, w + 1)
                    after(pe, freed, w - 1)
                    for c in range(2):
                        last = tr(bank[q][:, c * P:(c + 1) * P], rows[:, w, c * P:(c + 1) * P], c == 0, c == 1)
                    last.then_inc(ready, 1)
                return stage

            def three_products(to, q, hi, lo, cols, stop=True):
                for c in range(2):
                    mm(to, ht_hi[:, q, c, :], hi[:, c, cols], c == 0, False)
                    mm(to, ht_hi[:, q, c, :], lo[:, c, cols], False, False)
                    last = mm(to, ht_lo[:, q, c, :], hi[:, c, cols], False, stop and c == 1)
                return last

            def project_nodes(k, q):
                w = 2 * k + q
                pe.wait_ge(ht_lo_done, w + 1)
                after(pe, row_ready, w - 1)
                three_products(bank[2 + q][:], q, w_node_hi, w_node_lo, slice(0, 2 * HID)).then_inc(proj_ready, 1)

            pe.wait_ge(w_lo_done, 2)
            pipeline(pe, [(transpose_rows(hs, h_done, ht_lo_done, ht_ready), 0), (project_nodes, 1)], WPAD, 2, straight=True)
            pe.wait_ge(row_ready, WPAD)
            pe.wait_ge(act_consts, 2)

            def edge_inputs(k, q):
                b = SLOTS * k + q
                pe.wait_ge(gath_in[q], 32 * (k + 1))
                pe.wait_ge(ea_lo_done, b + 1)
                after(pe, relu_lo_done, b - 1)
                for m in range(2):
                    to = bank[q % 2][:, m * CHUNK:(m + 1) * CHUNK]
                    for i in range(2):
                        tr(to[:, i * P:(i + 1) * P], gath[:, q, i, m * P:(m + 1) * P], i == 0, False)
                    mm(to, w_edge_hi[:, m * P:(m + 1) * P], ea_parts[:, q, :], False, False)
                    last = mm(to, w_edge_lo[:, m * P:(m + 1) * P], ea_parts[:, q, :], False, True)
                last.then_inc(z_ready, 1)
                after(pe, gate_added, b - 1)
                for i in range(2):
                    to = bank[2 + q % 2][:, i * HID:(i + 1) * HID]
                    mm(to, ea_parts[:, q, i * P:(i + 1) * P], w_edge_hi[:, HID:], True, False)
                    last = mm(to, ea_parts[:, q, i * P:(i + 1) * P], w_edge_lo[:, HID:], False, True)
                last.then_inc(gate_ready, 1)

            def core(k, q):
                b = SLOTS * k + q
                pe.wait_ge(relu_lo_done, b + 1)
                after(pe, msg_done, b - 1)
                for i in range(2):
                    to = bank[4 + q % 2][:, i * HID:(i + 1) * HID]
                    mm(to, share[:], b2_parts[:], True, False)
                    for c in range(2):
                        tile = slice(c * CHUNK + i * P, c * CHUNK + (i + 1) * P)
                        mm(to, relu_hi[:, q % 2, tile], w2_hi[:, c, :], False, False)
                        mm(to, relu_hi[:, q % 2, tile], w2_lo[:, c, :], False, False)
                        last = mm(to, relu_lo[:, q % 2, tile], w2_hi[:, c, :], False, c == 1)
                last.then_inc(core_ready, 1)

            def sum_messages(k, q):
                b = SLOTS * k + q
                pe.wait_ge(msg_lo_done, b + 1)
                pe.wait_ge(hot_done, b + 1)
                after(pe, sum_added, b - 1)
                to = bank[6 + q % 2][:, 0:HID]
                for i in range(2):
                    mm(to, hot[:, q % 2, i, :], msg_hi[:, q % 2, i, :], i == 0, False)
                    last = mm(to, hot[:, q % 2, i, :], msg_lo[:, q % 2, i, :], False, i == 1)
                last.then_inc(sum_ready, 1)

            pipeline(pe, [(edge_inputs, 0), (sum_messages, 3), (core, 1)], BLOCKS, SLOTS)
            pe.wait_ge(sum_added, BLOCKS)
            pe.wait_ge(rel_in, 5 * 16)

            def project_qkv(k, q):
                w = 2 * k + q
                pe.wait_ge(ht2_lo_done, w + 1)
                after(pe, qkv_done, w - 1)
                three_products(bank[2 + q][:], q, wqkv_hi, wqkv_lo, slice(0, 2 * HID))
                three_products(bank[4 + q][:, 0:HID], q, wqkv_hi, wqkv_lo, slice(2 * HID, 3 * HID)).then_inc(qkv_ready, 1)

            pe.wait_ge(wqkv_lo_done, 1)
            pipeline(pe, [(transpose_rows(hs, h2_done, ht2_lo_done, ht2_ready), 0), (project_qkv, 1)], WPAD, 2, straight=True)
            pe.wait_ge(qkv_done, WPAD)
            pe.wait_ge(q_lo_done, WPAD)
            pe.wait_ge(rel_done, 2)
            pe.wait_ge(consts, 2)

            def spread_row(k, q):
                b = SLOTS * k + q
                pe.wait_ge(brow_in[q], 16 * (k + 1))
                after(pe, hot_t_done, b - 1)
                mm(bank[q % 2][:], spread[:], block_row[:, q, :, :].rearrange("p k e -> p (k e)"), True, True).then_inc(spread_ready, 1)

            def keys_and_queries(k, q):
                b = SLOTS * k + q
                pe.wait_ge(gath1_in[q], 32 * (k + 1))
                pe.wait_ge(hot_t_done, b + 1)
                after(pe, key_copied, b - 1)
                for i in range(2):
                    to = bank[2 + q % 2][:, i * HID:(i + 1) * HID]
                    for part in range(2):
                        mm(to, ident_r[:], gath[:, q, i, part * HID:(part + 1) * HID].bitcast(f32r), part == 0, False)
                    last = mm(to, hot_t[:, q % 2, 1, i * P:(i + 1) * P], rel_parts[:], False, True)
                last.then_inc(key_ready, 1)
                after(pe, prod_done, b - 1)
                w = pe.value_load(win_i[0:1, ds(b, 1)], min_val=0, max_val=WINDOWS - 1)
                for i in range(2):
                    to = bank[4 + q % 2][:, i * HID:(i + 1) * HID]
                    for table in (q_hi, q_lo):
                        last = mm(to, hot_t[:, q % 2, 0, i * P:(i + 1) * P], table[:, ds(w, 1), :].rearrange("p o f -> p (o f)"),
                                  table is q_hi, table is q_lo)
                last.then_inc(query_ready, 1)

            pipeline(pe, [(spread_row, 0), (keys_and_queries, 1)], BLOCKS, SLOTS)

            pe.wait_ge(score_done, BLOCKS)
            for r in range(2):
                for h in range(HEADS):
                    for i in range(2):
                        at = (h % 2) * CHUNK + i * P
                        last = tr(bank[2 * r + h // 2][0:HALF_B, at:at + P], exp_col[:, r * HALF_B:(r + 1) * HALF_B, i, h])
            last.then_inc(srow_ready, 1)
            pe.wait_ge(local_done, 1)
            for i, e in enumerate((0, CHUNK - 1)):
                for r in range(2):
                    last = mm(bank[4 + i][0:HEADS, r * HALF_B:(r + 1) * HALF_B], m_row[:, r, :, e], ident[0:HALF_B, 0:HALF_B], True, True)
            last.then_inc(lends_ready, 1)
            pe.wait_ge(carried, 1)
            for r in range(2):
                for i in range(2):
                    at = (2 * r + i) * HEADS
                    last = mm(bank[6][0:HALF_B, at:at + HEADS], carry[:, i, r * HALF_B:(r + 1) * HALF_B], ident[0:HEADS, 0:HEADS], True, True)
            last.then_inc(carry_ready, 1)
            pe.wait_ge(exp_done, 1)
            for r in range(2):
                for i in range(2):
                    for h in range(HEADS):
                        last = nc.tensor.matmul(bank[2 * r + i][:, h * HALF_B:(h + 1) * HALF_B], lhsT=m_row[:, r, h, i * P:(i + 1) * P],
                                                rhs=ident[0:HALF_B, 0:HALF_B], is_transpose=True, start=True, stop=True)
                    last.then_inc(expt_ready, 1)
            pe.wait_ge(weights_done, 4)

            def aggregate(k, q):
                b = SLOTS * k + q
                pe.wait_ge(hot1_done, b + 1)
                pe.wait_ge(wsum_done, b + 1)
                after(pe, agg_added, b - 1)
                for i in range(2):
                    last = mm(bank[q % 2][:, 0:AGGW], hot1[:, q % 2, i, :], weighted[:, q % 2, i, :], i == 0, i == 1)
                last.then_inc(agg_ready, 1)

            pipeline(pe, [(aggregate, 0)], BLOCKS, SLOTS)
            pe.wait_ge(agg_added, BLOCKS)

            pe.wait_ge(bo_lo_done, 1)
            for w in range(WINDOWS + 2):
                if w < WINDOWS:
                    q = w % 2
                    pe.wait_ge(mix_done, w + 1)
                    after(pe, mt_lo_done, w - 1)
                    for c in range(2):
                        last = tr(bank[q][:, c * P:(c + 1) * P], agg[:, w, c * P:(c + 1) * P], c == 0, c == 1)
                    last.then_inc(mt_ready, 1)
                if w >= 2:
                    q = w % 2
                    pe.wait_ge(mt_lo_done, w - 1)
                    after(pe, o_done, w - 3)
                    to = bank[2 + q][:, 0:HID]
                    three_products(to, q, wo_hi, wo_lo, slice(0, HID), stop=False)
                    mm(to, share[:], b_o_parts[:], False, True).then_inc(o_ready, 1)


def kernel(x, src, dst, edge_attr_64, edge_type_64, L0_gnn_W1, L0_gnn_b1, L0_gnn_W2, L0_gnn_b2, L0_gnn_Wg, L0_gnn_bg,
           L0_gnn_gamma, L0_gnn_beta, L1_gnn_query_emb, L1_gnn_Wq, L1_gnn_bq, L1_gnn_Wk, L1_gnn_bk, L1_gnn_Wv,
           L1_gnn_bv, L1_gnn_rel_w, L1_gnn_Wo, L1_gnn_bo, L1_gnn_gamma, L1_gnn_beta):
    import numpy as np
    import concourse.bacc as bacc
    from concourse import mybir as mb
    from concourse.bass_utils import run_bass_kernel_spmd

    def rows(a, n, fill):
        a = np.asarray(a)
        full = np.full((n * CHUNK,) + a.shape[1:], fill, a.dtype)
        full[:a.shape[0]] = a
        return full.reshape((n, CHUNK) + a.shape[1:])

    def col(a):
        return np.ascontiguousarray(np.asarray(a).reshape(2, P).T)

    x = np.asarray(x)
    x_pad = np.zeros((WPAD * P, HID), x.dtype)
    x_pad[:NODES] = x
    arrays = {
        "x": x_pad,
        "src": rows(src, CHUNKS + 1, 0),
        "dst": rows(dst, CHUNKS + 1, NO_NODE),
        "etype": rows(edge_type_64, CHUNKS + 1, 0),
        "ea": np.ascontiguousarray(rows(edge_attr_64, CHUNKS, 0).transpose(0, 2, 1)),
        "w1": np.asarray(L0_gnn_W1),
        "wg": np.asarray(L0_gnn_Wg),
        "b_cat": np.concatenate([np.asarray(L0_gnn_b1), np.asarray(L0_gnn_bg)])[None, :],
        "w2": np.asarray(L0_gnn_W2),
        "b2": np.asarray(L0_gnn_b2)[None, :],
        "ln0": np.stack([np.asarray(L0_gnn_gamma), np.asarray(L0_gnn_beta)]),
        "query_col": col(L1_gnn_query_emb),
        "wqkv": np.concatenate([np.asarray(a) for a in (L1_gnn_Wk, L1_gnn_Wv, L1_gnn_Wq)], axis=1),
        "b_qkv": np.concatenate([np.asarray(a) for a in (L1_gnn_bk, L1_gnn_bv, L1_gnn_bq)])[None, :],
        "rel": np.asarray(L1_gnn_rel_w),
        "wo": np.asarray(L1_gnn_Wo),
        "b_o": np.asarray(L1_gnn_bo)[None, :],
        "ln1": np.stack([np.asarray(L1_gnn_gamma), np.asarray(L1_gnn_beta)]),
    }
    nc = bacc.Bacc("TRN2", target_bir_lowering=False, num_devices=1)
    args = [nc.dram_tensor(f"in_{name}", a.shape, mb.dt.from_np(a.dtype), kind="ExternalInput").ap() for name, a in arrays.items()]
    result = nc.dram_tensor("out_x", (NODES, HID), mb.dt.float32, kind="ExternalOutput").ap()
    build(nc, *args, result)
    got = run_bass_kernel_spmd(nc, [{f"in_{name}": a for name, a in arrays.items()}], core_ids=[0])
    return got.results[0]["out_x"]
```

```python
import concourse.bass as bass
from concourse import mybir
from contextlib import ExitStack

NODES, EDGES, HID, EDGE_DIM, RELS, HEADS = 3125, 50000, 256, 64, 64, 4
P = 128
HEAD = HID // HEADS
CHUNK = 256
CHUNKS = -(-EDGES // CHUNK)
WINDOWS = -(-NODES // P)
WPAD = WINDOWS + WINDOWS % 2
BLOCKS = CHUNKS + WINDOWS - 1
HALF_C = CHUNKS // 2
HALF_B = BLOCKS // 2
NO_NODE = 4096
FAR = 8192.0
BIG = 1e30
EPS = 1e-5
SLOTS = 4
EARLY = 13
RING = 5
SHARES = 32
AGGW = HID + HEADS
assert CHUNKS % 2 == 0 and BLOCKS % SLOTS == 0 and BLOCKS % (2 * RING) == 0


def build(nc, x, src, dst, etype, ea, w1, wg, b_cat, w2, b2, ln0, query_col, wqkv, b_qkv, rel, wo, b_o, ln1, out):
    f32, i32, f32r, bf16 = mybir.dt.float32, mybir.dt.int32, mybir.dt.float32r, mybir.dt.bfloat16
    ALU, ACT, AX = mybir.AluOpType, mybir.ActivationFunctionType, mybir.AxisListType
    ds = bass.ds

    edge_in_tab = nc.dram_tensor("edge_in_tab", (WPAD * P, 2 * HID), f32, kind="Internal").ap()
    kv_tab = nc.dram_tensor("kv_tab", (WPAD * P, 2 * HID), f32, kind="Internal").ap()
    block_values = nc.dram_tensor("block_values", (BLOCKS // 2, P, 2, 2 * HID), f32, kind="Internal").ap()
    row_tab = nc.dram_tensor("row_tab", (BLOCKS, 2 * CHUNK), bf16, kind="Internal").ap()

    ctx = ExitStack()
    with ctx:
        def sem(name):
            return ctx.enter_context(nc.semaphore(name))

        def sems(name, n):
            return [sem(f"{name}{i}") for i in range(n)]

        def sb(where, name, shape, dt):
            return where.enter_context(nc.sbuf_tensor(name, shape, dt))

        xs = sb(ctx, "xs", [P, WPAD, HID], f32)
        hs = sb(ctx, "hs", [P, WPAD, HID], f32)
        ident = sb(ctx, "ident", [P, P], f32)
        iota_node = sb(ctx, "iota_node", [P, P], f32)
        iota_part = sb(ctx, "iota_part", [P, 1], f32)
        eps_col = sb(ctx, "eps_col", [P, 1], f32)
        one_col = sb(ctx, "one_col", [P, 1], f32)
        stats = sb(ctx, "stats", [P, WPAD, 6], f32)
        mean_var = sb(ctx, "mean_var", [P, WPAD, 2], f32)
        std = sb(ctx, "std", [P, WPAD], f32)
        rstd = sb(ctx, "rstd", [P, WPAD], f32)
        shift = sb(ctx, "shift", [P, WPAD], f32)
        src_col = sb(ctx, "src_col", [P, BLOCKS, 2], i32)
        rel_col = sb(ctx, "rel_col", [P, BLOCKS, 2], f32)
        dst_row = sb(ctx, "dst_row", [HALF_B, 2, CHUNK], f32)
        chunk_i = sb(ctx, "chunk_i", [1, BLOCKS], i32)
        win_i = sb(ctx, "win_i", [1, BLOCKS], i32)
        ends_row = sb(ctx, "ends_row", [HEADS, 2, BLOCKS], f32)
        idx = sb(ctx, "idx", [P, 2, SLOTS, 2], i32)
        ht_hi = sb(ctx, "ht_hi", [P, 2, 2, P], f32r)
        ht_lo = sb(ctx, "ht_lo", [P, 2, 2, P], f32r)
        share = sb(ctx, "share", [2 * SHARES, P], f32r)
        ln0_sb = sb(ctx, "ln0_sb", [P, 2, HID], f32)
        query_sb = sb(ctx, "query_sb", [P, 2], f32)
        gath = sb(ctx, "gath", [P, SLOTS, 2, 2 * HID], f32)

        l0 = ExitStack()
        with l0:
            w_node = sb(l0, "w_node", [P, 2, 2 * HID], f32)
            w_node_hi = sb(l0, "w_node_hi", [P, 2, 2 * HID], f32r)
            w_node_lo = sb(l0, "w_node_lo", [P, 2, 2 * HID], f32r)
            w_edge = sb(l0, "w_edge", [P, 2 * HID], f32)
            w_edge_hi = sb(l0, "w_edge_hi", [P, 2 * HID], f32r)
            w_edge_lo = sb(l0, "w_edge_lo", [P, 2 * HID], f32r)
            w2_sb = sb(l0, "w2_sb", [P, 2, HID], f32)
            w2_hi = sb(l0, "w2_hi", [P, 2, HID], f32r)
            w2_lo = sb(l0, "w2_lo", [P, 2, HID], f32r)
            b_cat_sb = sb(l0, "b_cat_sb", [P, 2 * HID], f32)
            b2_sb = sb(l0, "b2_sb", [2 * SHARES, HID], f32)
            b2_parts = sb(l0, "b2_parts", [2 * SHARES, HID], f32r)
            node_row = sb(l0, "node_row", [P, 2, 2 * HID], f32)
            ea_in = sb(l0, "ea_in", [P, SLOTS, CHUNK], f32)
            ea_parts = sb(l0, "ea_parts", [P, SLOTS, CHUNK], f32r)
            relu_hi = sb(l0, "relu_hi", [P, 2, 2 * CHUNK], f32r)
            relu_lo = sb(l0, "relu_lo", [P, 2, 2 * CHUNK], f32r)
            gate = sb(l0, "gate", [P, 2, 2 * HID], f32)
            gate_in = sb(l0, "gate_in", [P, 2, 2 * HID], f32)
            msg = sb(l0, "msg", [P, 2, 2 * HID], f32)
            msg_hi = sb(l0, "msg_hi", [P, 2, 2, HID], f32r)
            msg_lo = sb(l0, "msg_lo", [P, 2, 2, HID], f32r)
            dist = sb(l0, "dist", [P, 2, 2, P], f32)
            hot = sb(l0, "hot", [P, 2, 2, P], f32r)
            nat_i = sb(l0, "nat_i", [HALF_C, 3, 2, CHUNK], i32)
            nat_f = sb(l0, "nat_f", [HALF_C, 3, 2, CHUNK], f32)
            ends_i = sb(l0, "ends_i", [HALF_C, 3, 2], i32)
            ends_w = sb(l0, "ends_w", [HALF_C, 3, 2], f32)
            count = sb(l0, "count", [HALF_C, 2], f32)
            jump = sb(l0, "jump", [HALF_C, 2], f32)
            first_b = sb(l0, "first_b", [HALF_C, 2], f32)
            last_b = sb(l0, "last_b", [HALF_C, 2], f32)
            iota_b = sb(l0, "iota_b", [HALF_C, BLOCKS], f32)
            upto = sb(l0, "upto", [HALF_C, HALF_C], f32)
            ones_c = sb(l0, "ones_c", [HALF_C, CHUNK], f32)
            passed = sb(l0, "passed", [HALF_C, 2, BLOCKS], f32)
            chosen = sb(l0, "chosen", [HALF_C, 2, BLOCKS], f32)
            win_f = sb(l0, "win_f", [1, BLOCKS], f32)
            neg_off = sb(l0, "neg_off", [1, BLOCKS], f32)
            row_b = sb(l0, "row_b", [HALF_B, 2, 2, CHUNK], bf16)

        l1 = ExitStack()
        with l1:
            agg = sb(l1, "agg", [P, WINDOWS, AGGW], f32)
            exp_col = sb(l1, "exp_col", [P, BLOCKS, 2, HEADS], f32)
            rel_parts = sb(l1, "rel_parts", [P, HID], f32r)
            spread = sb(l1, "spread", [2, P], bf16)
            block_row = sb(l1, "block_row", [2, SLOTS, 2, CHUNK], bf16)
            rel_sb = sb(l1, "rel_sb", [P, HEAD], f32)
            wo_hi = sb(l1, "wo_hi", [P, 2, HID], f32r)
            wo_lo = sb(l1, "wo_lo", [P, 2, HID], f32r)
            qt = ExitStack()
            with qt:
                q_hi = sb(qt, "q_hi", [P, WPAD, HID], f32r)
                q_lo = sb(qt, "q_lo", [P, WPAD, HID], f32r)
                a0 = ExitStack()
                with a0:
                    wqkv_hi = sb(a0, "wqkv_hi", [P, 2, 3 * HID], f32r)
                    wqkv_lo = sb(a0, "wqkv_lo", [P, 2, 3 * HID], f32r)
                    b_qkv_sb = sb(a0, "b_qkv_sb", [P, 3 * HID], f32)
                    qkv_row = sb(a0, "qkv_row", [P, 2, 3 * HID], f32)
                a1 = ExitStack()
                with a1:
                    hot_t = sb(a1, "hot_t", [P, 2, 2, CHUNK], f32r)
                    key_sb = sb(a1, "key_sb", [P, 2, 2, HID], f32)
                    prod = sb(a1, "prod", [P, 2, 2 * HID], f32)
            a2 = ExitStack()
            with a2:
                s_row = sb(a2, "s_row", [HALF_B, 2, HEADS, CHUNK], f32)
                m_row = sb(a2, "m_row", [HALF_B, 2, HEADS, CHUNK], f32)
                edge_max = sb(a2, "edge_max", [HEADS, 2, BLOCKS], f32)
                run_max = sb(a2, "run_max", [HEADS, 2, BLOCKS], f32)
                carry = sb(a2, "carry", [HEADS, 2, BLOCKS], f32)
                carry_col = sb(a2, "carry_col", [HALF_B, 2, 2, HEADS], f32)
            a3 = ExitStack()
            with a3:
                values = sb(a3, "values", [P, RING, 2, 2 * HID], f32)
                weighted = sb(a3, "weighted", [P, RING, 2, AGGW], f32)
                dist1 = sb(a3, "dist1", [P, RING, 2, P], f32)
                hot1 = sb(a3, "hot1", [P, RING, 2, P], f32)
                v_in = sb(a3, "v_in", [P, 2, HID], f32)
                empty = sb(a3, "empty", [P, WINDOWS, HEADS], f32)
                denom = sb(a3, "denom", [P, WINDOWS, HEADS], f32)
                inv = sb(a3, "inv", [P, WINDOWS, HEADS], f32)
                b_o_sb = sb(a3, "b_o_sb", [2 * SHARES, HID], f32)
                b_o_parts = sb(a3, "b_o_parts", [2 * SHARES, HID], f32r)
                ln1_sb = sb(a3, "ln1_sb", [P, 2, HID], f32)

        arriving = agg[:].rearrange("p w f -> p (w f)")
        wqkv_sb = arriving[:, 0:6 * HID].rearrange("p (c n) -> p c n", c=2)
        wo_sb = arriving[:, 6 * HID:8 * HID].rearrange("p (c n) -> p c n", c=2)

        used = [0]

        def in_agg(rows, *dims):
            size = 1
            for d in dims:
                size *= d
            flat = arriving[0:rows, used[0]:used[0] + size]
            used[0] += size
            if len(dims) == 1:
                return flat
            letters = "abc"[:len(dims)]
            return flat.rearrange(f"p ({' '.join(letters)}) -> p {' '.join(letters)}", **dict(zip(letters[1:], dims[1:])))

        reset = in_agg(HALF_B, 2, HEADS * CHUNK + 1)
        same = in_agg(HALF_B, 2, 2, CHUNK)
        outside = in_agg(HALF_B, 2, CHUNK)
        tmp_row = in_agg(HALF_B, 2, CHUNK)
        follows, whole = in_agg(HEADS, BLOCKS), in_agg(HEADS, BLOCKS)
        into, through = in_agg(HEADS, 2, BLOCKS), in_agg(HEADS, 2, BLOCKS)

        bank = [ctx.enter_context(nc.psum_tensor(f"bank{i}", [P, 512], f32)) for i in range(8)]

        nat_in, x_in, w_in, lw_in, row_out = sem("nat_in"), sem("x_in"), sem("w_in"), sem("lw_in"), sem("row_out")
        pool_step, consts, share_done = sem("pool_step"), sem("consts"), sem("share_done")
        d_step, a_step = sem("d_step"), sem("a_step")
        counted, cumulated, sel_ready, rows_ready, off_ready, cols_ready, meta_ready = (
            sem(n) for n in ("counted", "cumulated", "sel_ready", "rows_ready", "off_ready", "cols_ready", "meta_ready"))
        w_hi_done, w_lo_done, wqkv_hi_done, wqkv_lo_done, bo_hi_done, bo_lo_done = (
            sem(n) for n in ("w_hi_done", "w_lo_done", "wqkv_hi_done", "wqkv_lo_done", "bo_hi_done", "bo_lo_done"))
        var_done, std_done, norm_done = sem("var_done"), sem("std_done"), sem("norm_done")
        h_done, ht_ready, ht_hi_done, ht_lo_done, proj_ready, row_ready = (
            sem(n) for n in ("h_done", "ht_ready", "ht_hi_done", "ht_lo_done", "proj_ready", "row_ready"))
        row_stored = sems("row_stored", 2)
        gath_in, ea_arrived = sems("gath_in", SLOTS), sems("ea_arrived", SLOTS)
        idx_done, ea_hi_done, ea_lo_done, z_ready, relu_hi_done, relu_lo_done, gate_done, core_ready = (
            sem(n) for n in ("idx_done", "ea_hi_done", "ea_lo_done", "z_ready", "relu_hi_done", "relu_lo_done",
                             "gate_done", "core_ready"))
        gate_ready, gate_added, msg_done, msg_hi_done, msg_lo_done, dist_done, hot_done, sum_ready, sum_added = (
            sem(n) for n in ("gate_ready", "gate_added", "msg_done", "msg_hi_done", "msg_lo_done", "dist_done", "hot_done",
                             "sum_ready", "sum_added"))
        beta_added, beta1_added, n1_done, scaled_done, x1_done = (
            sem(n) for n in ("beta_added", "beta1_added", "n1_done", "scaled_done", "x1_done"))
        h2_done, ht2_ready, ht2_hi_done, ht2_lo_done, qkv_ready, qkv_done, q_hi_done, q_lo_done = (
            sem(n) for n in ("h2_done", "ht2_ready", "ht2_hi_done", "ht2_lo_done", "qkv_ready", "qkv_done",
                             "q_hi_done", "q_lo_done"))
        kv_stored = sems("kv_stored", 2)
        brow_in, gath1_in = sems("brow_in", SLOTS), sems("gath1_in", SLOTS)
        idx1_done, spread_ready, hot_t_done, key_ready, key_copied, query_ready, prod_done, score_done = (
            sem(n) for n in ("idx1_done", "spread_ready", "hot_t_done", "key_ready", "key_copied", "query_ready",
                             "prod_done", "score_done"))
        srow_ready, local_done, lends_ready, carried, carry_ready, max_done, exp_done, expt_ready, weights_done = (
            sem(n) for n in ("srow_ready", "local_done", "lends_ready", "carried", "carry_ready", "max_done",
                             "exp_done", "expt_ready", "weights_done"))
        values_saved, values_in = sems("values_saved", SLOTS), sems("values_in", RING)
        weighted_done, dist1_done, hot1_done, agg_ready, agg_added = (
            sem(n) for n in ("weighted_done", "dist1_done", "hot1_done", "agg_ready", "agg_added"))
        v_arrived, y_stored = sems("v_arrived", 2), sem("y_stored")
        ow_in, inv_done, mean_done, mix_done, mt_ready, mt_hi_done, mt_lo_done, o_ready, o_done = (
            sem(n) for n in ("ow_in", "inv_done", "mean_done", "mix_done", "mt_ready", "mt_hi_done", "mt_lo_done",
                             "o_ready", "o_done"))
        x2_normed, x2_scaled, x2_scaled_early, y_early_done, y_late_done = (
            sem(n) for n in ("x2_normed", "x2_scaled", "x2_scaled_early", "y_early_done", "y_late_done"))
        idx_seen, rel_in, rel_done, agg_zero = sem("idx_seen"), sem("rel_in"), sem("rel_done"), sem("agg_zero")
        segments_known = sem("segments_known")

        def after(engine, signal, n):
            if not isinstance(n, int) or n > 0:
                engine.wait_ge(signal, n)

        def pipeline(engine, stages, count, body, straight=False):
            rounds = count // body

            def step(k, u):
                for stage, lag in stages:
                    if isinstance(k, int) and not 0 <= body * k + u - lag < count:
                        continue
                    stage(k + (u - lag) // body, (u - lag) % body)

            peeled = -(-max(lag for _, lag in stages) // body) + 1
            for k in range(peeled):
                for u in range(body):
                    step(k, u)
            if straight:
                for k in range(peeled, rounds):
                    for u in range(body):
                        step(k, u)
            else:
                with engine.Fori(peeled, rounds) as k:
                    for u in range(body):
                        step(k, u)
            for u in range(max(lag for _, lag in stages)):
                step(rounds, u)

        def node_phase_over(engine):
            for q in range(2):
                engine.wait_ge(kv_stored[q], 16 * (WPAD // 2))

        block = ctx.enter_context(nc.Block())

        @block.sync
        def _(sp):
            for kind, array in enumerate((src, dst, etype)):
                sp.dma_start(nat_i[:, kind, :, :], array[0:CHUNKS, :].rearrange("(g p) e -> p g e", g=2)).then_inc(nat_in, 16)
            with nc.allow_non_contiguous_dma(reason="one number a chunk"):
                sp.dma_start(ends_i[:, 2, :], dst[1:CHUNKS + 1, 0:1].rearrange("(g p) o -> p (g o)", g=2)).then_inc(nat_in, 16)
            sp.dma_start(xs[:], x.rearrange("(w p) f -> p w f", p=P)).then_inc(x_in, 16)
            sp.dma_start(w_node[:, :, 0:HID], w1[0:HID, :].rearrange("(c p) n -> p c n", p=P)).then_inc(w_in, 16)
            sp.dma_start(w_node[:, :, HID:], wg[0:HID, :].rearrange("(c p) n -> p c n", p=P)).then_inc(w_in, 16)
            sp.dma_start(b_cat_sb[:], b_cat.to_broadcast([P, 2 * HID])).then_inc(w_in, 16)
            for half in range(2):
                rows = slice(half * EDGE_DIM, (half + 1) * EDGE_DIM)
                sp.dma_start(w_edge[rows, 0:HID], w1[HID:HID + EDGE_DIM, :]).then_inc(w_in, 16)
                sp.dma_start(w_edge[rows, HID:], wg[HID:HID + EDGE_DIM, :]).then_inc(w_in, 16)
            sp.dma_start(w2_sb[:], w2.rearrange("(c p) n -> p c n", p=P)).then_inc(w_in, 16)
            sp.dma_start(b2_sb[:], b2.to_broadcast([2 * SHARES, HID])).then_inc(w_in, 16)
            for i in range(2):
                sp.dma_start(ln0_sb[:, i, :], ln0[i:i + 1, :].to_broadcast([P, HID])).then_inc(lw_in, 16)
            sp.dma_start(query_sb[:], query_col).then_inc(lw_in, 16)

            sp.wait_ge(meta_ready, 1)
            for r in range(2):
                sp.dma_start(row_tab[r * HALF_B:(r + 1) * HALF_B, :], row_b[:, r, :, :].rearrange("p k e -> p (k e)")).then_inc(row_out, 16)

            def store_rows(k, q):
                sp.wait_ge(row_ready, 2 * k + q + 1)
                sp.dma_start(edge_in_tab[ds((2 * k + q) * P, P), :], node_row[:, q, :]).then_inc(row_stored[q], 16)

            pipeline(sp, [(store_rows, 0)], WPAD, 2)

            def load_edges(k, q):
                b = SLOTS * k + q
                after(sp, ea_lo_done, b - SLOTS + 1)
                c = sp.value_load(chunk_i[0:1, ds(b, 1)], min_val=0, max_val=CHUNKS - 1)
                chunk = ea[ds(c, 1), :, :].rearrange("o d e -> (o d) e")
                for half in range(2):
                    sp.dma_start(ea_in[half * EDGE_DIM:(half + 1) * EDGE_DIM, q, :], chunk).then_inc(ea_arrived[q], 16)

            pipeline(sp, [(load_edges, 0)], BLOCKS, SLOTS)

            sp.wait_ge(sum_added, BLOCKS)
            sp.dma_start(wqkv_sb, wqkv.rearrange("(c p) n -> p c n", p=P)).then_inc(rel_in, 16)
            sp.dma_start(b_qkv_sb[:], b_qkv.to_broadcast([P, 3 * HID])).then_inc(rel_in, 16)
            for half in range(2):
                sp.dma_start(rel_sb[half * RELS:(half + 1) * RELS, :], rel).then_inc(rel_in, 16)
            sp.dma_start(wo_sb, wo.rearrange("(c p) n -> p c n", p=P)).then_inc(rel_in, 16)

            def store_keys_values(k, q):
                w = 2 * k + q
                sp.wait_ge(qkv_done, w + 1)
                sp.dma_start(kv_tab[ds(w * P, P), :], qkv_row[:, q, 0:2 * HID]).then_inc(kv_stored[q], 16)

            pipeline(sp, [(store_keys_values, 0)], WPAD, 2)

            sp.wait_ge(row_out, 32)
            sp.wait_ge(consts, 2)

            def load_block_row(k, q):
                b = SLOTS * k + q
                after(sp, spread_ready, b - SLOTS + 1)
                sp.dma_start(block_row[0:1, q, :, :].rearrange("p k e -> p (k e)"), row_tab[ds(b, 1), :]).then_inc(brow_in[q], 16)

            def save_values(k, q):
                b = SLOTS * k + q
                sp.wait_ge(gath1_in[q], 32 * (k + 1))
                sp.dma_start(block_values[ds(2 * k + q // 2, 1), :, q % 2, :].rearrange("o p (i f) -> (o p) i f", i=2), gath[:, q, :, HID:]).then_inc(values_saved[q], 16)

            pipeline(sp, [(load_block_row, 0), (save_values, 3)], BLOCKS, SLOTS)

            for q in range(SLOTS):
                sp.wait_ge(values_saved[q], 16 * (BLOCKS // SLOTS))
            sp.wait_ge(weights_done, 4)

            sp.dma_start(b_o_sb[:], b_o.to_broadcast([2 * SHARES, HID])).then_inc(ow_in, 16)
            for i in range(2):
                sp.dma_start(ln1_sb[:, i, :], ln1[i:i + 1, :].to_broadcast([P, HID])).then_inc(ow_in, 16)
            def load_values(k, slot):
                pair = RING * k + slot
                after(sp, weighted_done, 2 * (pair - RING + 1))
                sp.dma_start(values[:, slot, :, :], block_values[ds(pair, 1), :, :, :].rearrange("o p j f -> (o p) j f")).then_inc(values_in[slot], 16)

            pipeline(sp, [(load_values, 0)], BLOCKS // 2, RING)

            for w in range(WINDOWS):
                q = w % 2
                after(sp, mix_done, w - 1)
                sp.dma_start(v_in[:, q, :], kv_tab[w * P:(w + 1) * P, HID:]).then_inc(v_arrived[q], 16)
            for w in range(WINDOWS):
                rows = min(P, NODES - w * P)
                if w < EARLY:
                    sp.wait_ge(y_early_done, w + 1)
                else:
                    sp.wait_ge(y_late_done, w - EARLY + 1)
                sp.dma_start(out[w * P:w * P + rows, :], hs[0:rows, w, :]).then_inc(y_stored, 16)
            sp.wait_ge(y_stored, 16 * WINDOWS)

        @block.gpsimd
        def _(pool):
            steps = [0]

            def step(ins):
                steps[0] += 1
                ins.then_inc(pool_step, 1)
                pool.wait_ge(pool_step, steps[0])

            g = nc.gpsimd
            g.iota(iota_b[:], pattern=[[1, BLOCKS]], base=0, channel_multiplier=0, allow_small_or_imprecise_dtypes=True)
            g.iota(iota_node[:], pattern=[[1, P]], base=0, channel_multiplier=0, allow_small_or_imprecise_dtypes=True)
            g.iota(iota_part[:], pattern=[[0, 1]], base=0, channel_multiplier=1, allow_small_or_imprecise_dtypes=True)
            g.memset(eps_col[:], EPS)
            g.memset(one_col[:], 1.0)
            g.memset(ones_c[:], 1.0)
            step(g.memset(ident[:], 0.0))
            step(g.affine_select(out=ident[:], in_=ident[:], compare_op=ALU.not_equal, fill=1.0, base=0,
                                 pattern=[[-1, P]], channel_multiplier=1))
            step(g.memset(upto[:], 1.0))
            g.affine_select(out=upto[:], in_=upto[:], compare_op=ALU.is_ge, fill=0.0, base=0,
                            pattern=[[1, HALF_C]], channel_multiplier=-1).then_inc(consts, 1)

            def gather_blocks(table, arrived, idx_signal, freed, saved=None):
                def one(first, u, half, turn=0):
                    b, q = first + u, u % SLOTS
                    if q == 0:
                        g.tensor_copy(idx[:, half, :, :], src_col[:, ds(b, SLOTS), :]).then_inc(idx_signal, 1)
                    after(pool, freed, b - SLOTS + 1)
                    if saved and not (isinstance(b, int) and b < SLOTS):
                        pool.wait_ge(saved[q], 16 * turn)
                    if q == 0:
                        pool.wait_ge(idx_signal, turn + 1)
                    pool.sem_inc(idx_seen, 1)
                    for i in range(2):
                        g.indirect_dma_start(gath[:, q, i, :], None, table,
                                             bass.IndirectOffsetOnAxis(ap=idx[:, half, q, i:i + 1], axis=0)).then_inc(arrived[q], 16)

                for u in range(SLOTS):
                    one(0, u, 0)
                with pool.Fori(0, (BLOCKS - SLOTS) // (2 * SLOTS)) as k:
                    for u in range(2 * SLOTS):
                        one(2 * SLOTS * k + SLOTS, u, 1 - u // SLOTS, 2 * k + 1 + u // SLOTS)

            pool.wait_ge(meta_ready, 1)
            for q in range(2):
                pool.wait_ge(row_stored[q], 16 * (WPAD // 2))
            gather_blocks(edge_in_tab, gath_in, idx_done, gate_added)
            pool.wait_ge(lw_in, 3 * 16)
            g.tensor_tensor(xs[:], xs[:], ln0_sb[:, 1:2, :].to_broadcast([P, WPAD, HID]), ALU.add).then_inc(beta_added, 1)

            pool.wait_ge(sum_added, BLOCKS)
            step(g.memset(spread[:], 1.0))
            step(g.affine_select(out=spread[:], in_=spread[:], compare_op=ALU.is_equal, fill=float(RELS), base=0,
                                 pattern=[[0, P]], channel_multiplier=1))
            step(g.affine_select(out=spread[:], in_=spread[:], compare_op=ALU.is_ge, fill=0.0, base=0,
                                 pattern=[[1, P]], channel_multiplier=-RELS))
            step(g.memset(block_row[:], 0.0))
            g.affine_select(out=block_row[:], in_=block_row[:], compare_op=ALU.is_ge, fill=1.0, base=1,
                            pattern=[[0, SLOTS], [-1, 2], [0, CHUNK]], channel_multiplier=-1).then_inc(consts, 1)

            pool.wait_ge(wqkv_hi_done, 2)
            g.tensor_tensor(wqkv_lo[:], wqkv_sb, wqkv_hi[:], ALU.subtract)
            g.tensor_tensor(wo_lo[:], wo_sb, wo_hi[:], ALU.subtract).then_inc(wqkv_lo_done, 1)

            def residual(k, q):
                w = 2 * k + q
                pool.wait_ge(scaled_done, w + 1)
                hrow, xrow = (t[:, ds(w, 1), :].rearrange("p o f -> p (o f)") for t in (hs, xs))
                g.tensor_tensor(xrow, xrow, hrow, ALU.add).then_inc(x1_done, 1)

            pool.wait_ge(beta_added, 1)
            pipeline(pool, [(residual, 0)], WPAD, 2, straight=True)

            pool.wait_ge(wqkv_lo_done, 1)
            step(g.tensor_scalar(outside[:], dst_row[:], 0.0, BIG, ALU.is_ge, ALU.mult))
            step(g.tensor_scalar(tmp_row[:], dst_row[:], float(P - 1), BIG, ALU.is_le, ALU.mult))
            step(g.tensor_tensor(outside[:], outside[:], tmp_row[:], ALU.add))
            step(g.tensor_scalar(outside[:], outside[:], 2 * BIG, None, ALU.subtract))
            step(g.memset(reset[:], -BIG))
            step(g.tensor_tensor(tmp_row[:, :, 1:], dst_row[:, :, 1:], dst_row[:, :, 0:CHUNK - 1], ALU.subtract))
            step(g.tensor_scalar(tmp_row[:, :, 1:], tmp_row[:, :, 1:], 0.0, None, ALU.is_equal))
            for r in range(2):
                for h in range(HEADS):
                    last = g.tensor_scalar(reset[:, r, h * CHUNK + 1:(h + 1) * CHUNK], tmp_row[:, r, 1:], BIG, BIG, ALU.mult, ALU.subtract)
            step(last)
            for r in range(2):
                for i, e in enumerate((0, CHUNK - 1)):
                    step(g.tensor_scalar(same[:, r, i, :], dst_row[:, r, :], dst_row[:, r, e:e + 1], BIG, ALU.is_equal, ALU.mult))
            step(g.tensor_scalar(same[:], same[:], BIG, None, ALU.subtract))
            step(g.memset(follows[:], 0.0))
            step(g.tensor_tensor(follows[:, 1:], ends_row[:, 0, 1:], ends_row[:, 1, 0:BLOCKS - 1], ALU.subtract))
            step(g.tensor_scalar(follows[:, 1:], follows[:, 1:], 0.0, None, ALU.is_equal))
            step(g.tensor_tensor(whole[:], ends_row[:, 0, :], ends_row[:, 1, :], ALU.subtract))
            step(g.tensor_scalar(whole[:], whole[:], 0.0, None, ALU.is_equal))
            step(g.memset(into[:], 0.0))
            step(g.tensor_copy(into[:, 0, :], follows[:]))
            step(g.tensor_copy(into[:, 1, 0:BLOCKS - 1], follows[:, 1:]))
            for i in range(2):
                step(g.tensor_tensor(through[:, i, :], into[:, i, :], whole[:], ALU.mult))
            step(g.tensor_scalar(into[:], into[:], BIG, BIG, ALU.mult, ALU.subtract))
            g.tensor_scalar(through[:], through[:], BIG, BIG, ALU.mult, ALU.subtract).then_inc(segments_known, 1)

            node_phase_over(pool)
            gather_blocks(kv_tab, gath1_in, idx1_done, key_ready, values_saved)
            pool.wait_ge(max_done, 1)
            g.memset(agg[:], 0.0).then_inc(agg_zero, 1)

            pool.wait_ge(ow_in, 3 * 16)
            g.tensor_tensor(xs[:], xs[:], ln1_sb[:, 1:2, :].to_broadcast([P, WPAD, HID]), ALU.add).then_inc(beta1_added, 1)
            pool.wait_ge(inv_done, 1)
            for w in range(WINDOWS):
                heads = agg[:, w, 0:HID].rearrange("p (h d) -> p h d", h=HEADS)
                g.tensor_tensor(heads, heads, inv[:, w, :].unsqueeze(2).to_broadcast([P, HEADS, HEAD]), ALU.mult).then_inc(mean_done, 1)
            pool.wait_ge(beta1_added, 1)
            for w in range(EARLY + 1):
                if w < EARLY:
                    pool.wait_ge(x2_normed, w + 1)
                    g.tensor_tensor(hs[:, w, :], hs[:, w, :], ln1_sb[:, 0, :], ALU.mult).then_inc(x2_scaled_early, 1)
                if w >= 1:
                    pool.wait_ge(x2_scaled_early, w)
                    g.tensor_tensor(hs[:, w - 1, :], hs[:, w - 1, :], xs[:, w - 1, :], ALU.add).then_inc(y_early_done, 1)

        @block.scalar
        def _(act):
            s = nc.scalar
            act.wait_ge(consts, 1)
            s.mul(share[:], ones_c[0:2 * SHARES, 0:P], 1 / SHARES).then_inc(share_done, 1)
            act.wait_ge(w_in, 9 * 16)
            s.copy(w_node_hi[:], w_node[:]).then_inc(w_hi_done, 1)
            s.copy(w_edge_hi[:], w_edge[:]).then_inc(w_hi_done, 1)
            s.copy(w2_hi[:], w2_sb[:]).then_inc(w_hi_done, 1)
            s.copy(b2_parts[:], b2_sb[:]).then_inc(w_hi_done, 1)

            def normed(done):
                def stage(k, q):
                    w = 2 * k + q
                    s.activation(hs[:, ds(w, 1), :].rearrange("p o f -> p (o f)"),
                                 xs[:, ds(w, 1), :].rearrange("p o f -> p (o f)"), ACT.Relu,
                                 bias=shift[:, ds(w, 1)], scale=rstd[:, ds(w, 1)]).then_inc(done, 1)
                return stage

            def high_rows(k, q):
                w = 2 * k + q
                act.wait_ge(ht_ready, w + 1)
                after(act, proj_ready, w - 1)
                s.copy(ht_hi[:, q, :, :], bank[q][:, 0:HID].rearrange("p (c n) -> p c n", c=2)).then_inc(ht_hi_done, 1)

            act.wait_ge(var_done, 1)
            s.activation(std[:], mean_var[:, :, 1], ACT.Sqrt, bias=eps_col[:]).then_inc(std_done, 1)
            act.wait_ge(norm_done, 1)
            pipeline(act, [(normed(h_done), 0), (high_rows, 1)], WPAD, 2)

            def split_edges(k, q):
                b = SLOTS * k + q
                act.wait_ge(ea_arrived[q], 32 * (k + 1))
                after(act, z_ready, b - SLOTS + 1)
                s.copy(ea_parts[:, q, :], ea_in[:, q, :]).then_inc(ea_hi_done, 1)

            def relu_inner(k, q):
                b = SLOTS * k + q
                act.wait_ge(z_ready, b + 1)
                after(act, core_ready, b - 1)
                s.activation(relu_hi[:, q % 2, :], bank[q % 2][:], ACT.Relu).then_inc(relu_hi_done, 1)

            def gates(k, q):
                b = SLOTS * k + q
                act.wait_ge(gate_added, b + 1)
                after(act, msg_done, b - 1)
                s.activation(gate[:, q % 2, :], gate_in[:, q % 2, :], ACT.Sigmoid).then_inc(gate_done, 1)

            def high_message(k, q):
                b = SLOTS * k + q
                act.wait_ge(msg_done, b + 1)
                after(act, sum_ready, b - 1)
                s.copy(msg_hi[:, q % 2, :, :].rearrange("p i f -> p (i f)"), msg[:, q % 2, :]).then_inc(msg_hi_done, 1)

            def distances(k, q):
                b = SLOTS * k + q
                after(act, hot_done, b - 1)
                for i in range(2):
                    last = s.activation(dist[:, q % 2, i, :], iota_node[:], ACT.Square, bias=rel_col[:, ds(b, 1), i], scale=-1.0)
                last.then_inc(dist_done, 1)

            def one_hot(k, q):
                b = SLOTS * k + q
                act.wait_ge(dist_done, b + 1)
                after(act, sum_ready, b - 1)
                s.activation(hot[:, q % 2, :, :], dist[:, q % 2, :, :], ACT.Relu, bias=one_col[:], scale=-1.0).then_inc(hot_done, 1)

            pipeline(act, [(split_edges, 0), (one_hot, 4), (distances, 3), (relu_inner, 2), (high_message, 4), (gates, 3)], BLOCKS, SLOTS)

            act.wait_ge(rel_in, 5 * 16)
            s.copy(wqkv_hi[:], wqkv_sb).then_inc(wqkv_hi_done, 1)
            s.copy(wo_hi[:], wo_sb).then_inc(wqkv_hi_done, 1)
            act.wait_ge(var_done, 2)
            s.activation(std[:], mean_var[:, :, 1], ACT.Sqrt, bias=eps_col[:]).then_inc(std_done, 1)
            act.wait_ge(norm_done, 2)

            def norm_messages(k, q):
                w = 2 * k + q
                rows = hs[:, ds(w, 1), :].rearrange("p o f -> p (o f)")
                s.activation(rows, rows, ACT.Identity, bias=shift[:, ds(w, 1)], scale=rstd[:, ds(w, 1)]).then_inc(n1_done, 1)

            pipeline(act, [(norm_messages, 0)], WPAD, 2, straight=True)
            act.wait_ge(var_done, 3)
            s.activation(std[:], mean_var[:, :, 1], ACT.Sqrt, bias=eps_col[:]).then_inc(std_done, 1)
            act.wait_ge(norm_done, 3)
            act.wait_ge(lw_in, 3 * 16)
            for h in range(HEADS):
                last = s.mul(rel_parts[:, h * HEAD:(h + 1) * HEAD], rel_sb[:], 0.2)
            last.then_inc(rel_done, 1)
            s.mul(query_sb[:], query_sb[:], 0.1).then_inc(a_step, 1)
            act.wait_ge(a_step, 1)

            def enhance(k, q):
                w = 2 * k + q
                act.wait_ge(ht2_ready, w + 1)
                after(act, qkv_ready, w - 1)
                for c in range(2):
                    last = s.activation(ht_hi[:, q, c, :], bank[q][:, c * P:(c + 1) * P], ACT.Identity, bias=query_sb[:, c:c + 1])
                last.then_inc(ht2_hi_done, 1)

            def high_parts(k, q):
                w = 2 * k + q
                act.wait_ge(qkv_done, w + 1)
                s.mul(q_hi[:, ds(w, 1), :].rearrange("p o f -> p (o f)"), qkv_row[:, q, 2 * HID:], 1 / HEAD ** 0.5).then_inc(q_hi_done, 1)

            pipeline(act, [(enhance, 1), (normed(h2_done), 0), (high_parts, 3)], WPAD, 2)

            def copy_keys(k, q):
                b = SLOTS * k + q
                act.wait_ge(key_ready, b + 1)
                after(act, prod_done, b - 1)
                s.copy(key_sb[:, q % 2, :, :].rearrange("p i f -> p (i f)"), bank[2 + q % 2][:]).then_inc(key_copied, 1)

            node_phase_over(act)
            pipeline(act, [(copy_keys, 0)], BLOCKS, SLOTS)

            act.wait_ge(max_done, 1)
            flat = m_row[:].rearrange("p r h e -> p (r h e)")
            s.activation(flat, flat, ACT.Exp).then_inc(exp_done, 1)

            def weight_sums(k, q):
                b = 2 * RING * k + q
                after(act, agg_ready, b - RING + 1)
                s.copy(weighted[:, q % RING, :, HID:], exp_col[:, ds(b, 1), :, :].rearrange("p o i h -> p (o i) h"))

            def distances1(k, q):
                b = 2 * RING * k + q
                for i in range(2):
                    last = s.activation(dist1[:, q % RING, i, :], iota_node[:], ACT.Square, bias=rel_col[:, ds(b, 1), i], scale=-1.0)
                last.then_inc(dist1_done, 1)

            def one_hot1(k, q):
                b = 2 * RING * k + q
                act.wait_ge(dist1_done, b + 1)
                s.activation(hot1[:, q % RING, :, :], dist1[:, q % RING, :, :], ACT.Relu, bias=one_col[:], scale=-1.0).then_inc(hot1_done, 1)

            act.wait_ge(weights_done, 4)
            pipeline(act, [(weight_sums, 2), (one_hot1, 2), (distances1, 0)], BLOCKS, 2 * RING)

            act.wait_ge(ow_in, 3 * 16)
            s.copy(b_o_parts[:], b_o_sb[:]).then_inc(bo_hi_done, 1)

            def deviation(n, some):
                act.wait_ge(var_done, n)
                s.activation(std[:, some], mean_var[:, some, 1], ACT.Sqrt, bias=eps_col[:]).then_inc(std_done, 1)

            def norm_output(w):
                s.activation(hs[:, w, :], hs[:, w, :], ACT.Identity, bias=shift[:, w:w + 1], scale=rstd[:, w:w + 1]).then_inc(x2_normed, 1)

            for w in range(WINDOWS):
                act.wait_ge(mt_ready, w + 1)
                after(act, o_ready, w - 1)
                s.copy(ht_hi[:, w % 2, :, :], bank[w % 2][:, 0:HID].rearrange("p (c n) -> p c n", c=2)).then_inc(mt_hi_done, 1)
                if w == EARLY + 4:
                    deviation(4, slice(0, EARLY))
                if w == EARLY + 6:
                    act.wait_ge(norm_done, 4)
                if w >= EARLY + 6:
                    for early in range(2 * (w - EARLY - 6), min(EARLY, 2 * (w - EARLY - 5))):
                        norm_output(early)
            for early in range(2 * (WINDOWS - EARLY - 6), EARLY):
                norm_output(early)
            deviation(5, slice(EARLY, WINDOWS))
            act.wait_ge(norm_done, 5)
            for w in range(EARLY, WINDOWS):
                norm_output(w)

        @block.vector
        def _(dve):
            v = nc.vector
            steps = [0]

            def step(ins):
                steps[0] += 1
                ins.then_inc(d_step, 1)
                dve.wait_ge(d_step, steps[0])

            dve.wait_ge(nat_in, 4 * 16)
            dve.wait_ge(consts, 1)
            v.tensor_copy(ends_i[:, 0, :], nat_i[:, 1, :, 0])
            step(v.tensor_copy(ends_i[:, 1, :], nat_i[:, 1, :, CHUNK - 1]))
            step(v.tensor_scalar(ends_i[:], ends_i[:], P.bit_length() - 1, None, ALU.arith_shift_right))
            step(v.tensor_copy(nat_f[:], nat_i[:]))
            step(v.tensor_scalar(ends_w[:], ends_i[:], float(WINDOWS - 1), None, ALU.min))
            v.scalar_tensor_tensor(count[:], in0=ends_w[:, 1, :], scalar=1.0, in1=ends_w[:, 0, :], op0=ALU.add, op1=ALU.subtract).then_inc(counted, 1)
            v.scalar_tensor_tensor(jump[:], in0=ends_w[:, 2, :], scalar=-1.0, in1=ends_w[:, 1, :], op0=ALU.add, op1=ALU.subtract).then_inc(counted, 1)
            dve.wait_ge(cumulated, 1)
            step(v.tensor_copy(last_b[:], bank[0][0:HALF_C, 0:2]))
            step(v.tensor_tensor(first_b[:], last_b[:], count[:], ALU.subtract))
            for c in range(2):
                v.tensor_scalar(passed[:, c, :], iota_b[:], last_b[:, c:c + 1], None, ALU.is_ge)
                step(v.tensor_scalar(chosen[:, c, :], iota_b[:], first_b[:, c:c + 1], None, ALU.is_ge))
            v.tensor_tensor(chosen[:], chosen[:], passed[:], ALU.subtract).then_inc(sel_ready, 1)
            dve.wait_ge(rows_ready, 1)
            v.tensor_scalar(chunk_i[:], bank[0][0:1, 0:BLOCKS], float(CHUNKS - 1), None, ALU.min)
            step(v.tensor_tensor(win_f[:], bank[1][0:1, 0:BLOCKS], iota_b[0:1, :], ALU.add))
            step(v.tensor_scalar(win_f[:], win_f[:], ends_w[0:1, 0, 0:1], None, ALU.add))
            step(v.tensor_tensor(win_f[:], win_f[:], bank[2][0:1, 0:BLOCKS], ALU.mult))
            v.tensor_copy(win_i[:], win_f[:])
            step(v.tensor_scalar(neg_off[:], bank[2][0:1, 0:BLOCKS], -FAR, FAR, ALU.mult, ALU.add))
            v.scalar_tensor_tensor(neg_off[:], in0=win_f[:], scalar=-float(P), in1=neg_off[:], op0=ALU.mult, op1=ALU.add).then_inc(off_ready, 1)
            dve.wait_ge(w_hi_done, 4)
            v.tensor_tensor(w_node_lo[:], w_node[:], w_node_hi[:], ALU.subtract).then_inc(w_lo_done, 1)
            v.tensor_tensor(w_edge_lo[:], w_edge[:], w_edge_hi[:], ALU.subtract)
            v.tensor_tensor(b2_parts[SHARES:, :], b2_sb[SHARES:, :], b2_parts[SHARES:, :], ALU.subtract)
            v.tensor_tensor(w2_lo[:], w2_sb[:], w2_hi[:], ALU.subtract).then_inc(w_lo_done, 1)

            def row_statistics(rows, w):
                return v.bn_stats(stats[:, ds(w, 1), :].rearrange("p o s -> p (o s)"), rows[:, ds(w, 1), :].rearrange("p o f -> p (o f)"))

            def aggregate_statistics(first, end):
                step(v.engine_nop())
                for w in range(first, end):
                    last = v.bn_aggr(mean_var[:, w, :], stats[:, w, :])
                last.then_inc(var_done, 1)

            def statistics(rows):
                for w in range(WPAD):
                    row_statistics(rows, w)
                aggregate_statistics(0, WPAD)

            def scale_and_shift(n, some=slice(0, WPAD)):
                dve.wait_ge(std_done, n)
                step(v.reciprocal(rstd[:, some], std[:, some]))
                v.scalar_tensor_tensor(shift[:, some], in0=mean_var[:, some, 0], scalar=-1.0, in1=rstd[:, some], op0=ALU.mult, op1=ALU.mult).then_inc(norm_done, 1)

            dve.wait_ge(x_in, 16)
            statistics(xs)
            scale_and_shift(1)

            dve.wait_ge(cols_ready, 1)
            v.tensor_copy(src_col[:].rearrange("p b i -> p i b"), bank[0][:, 0:2 * BLOCKS].rearrange("p (i b) -> p i b", i=2))
            v.tensor_copy(rel_col[:].rearrange("p b i -> p i b"), bank[1][:, 0:2 * BLOCKS].rearrange("p (i b) -> p i b", i=2))
            v.tensor_copy(ends_row[:], bank[4][0:HEADS, 0:2 * BLOCKS].rearrange("p (i b) -> p i b", i=2))
            step(v.tensor_scalar(dst_row[:], bank[2][0:HALF_B, :].rearrange("p (r e) -> p r e", r=2), 255.0, -1.0, ALU.min, ALU.max))
            v.tensor_copy(row_b[:, :, 1, :], bank[3][0:HALF_B, :].rearrange("p (r e) -> p r e", r=2))
            v.tensor_copy(row_b[:, :, 0, :], dst_row[:]).then_inc(meta_ready, 1)

            def low_rows(k, q):
                w = 2 * k + q
                dve.wait_ge(ht_hi_done, w + 1)
                v.tensor_tensor(ht_lo[:, q, :, :], bank[q][:, 0:HID].rearrange("p (c n) -> p c n", c=2), ht_hi[:, q, :, :],
                                ALU.subtract).then_inc(ht_lo_done, 1)

            def add_bias(k, q):
                w = 2 * k + q
                dve.wait_ge(proj_ready, w + 1)
                if not isinstance(w, int) or w >= 2:
                    dve.wait_ge(row_stored[q], 16 * k)
                v.tensor_tensor(node_row[:, q, :], bank[2 + q][:], b_cat_sb[:], ALU.add).then_inc(row_ready, 1)

            pipeline(dve, [(low_rows, 0), (add_bias, 1)], WPAD, 2)

            def low_edges(k, q):
                b = SLOTS * k + q
                dve.wait_ge(ea_hi_done, b + 1)
                rows = slice(EDGE_DIM, 2 * EDGE_DIM)
                v.tensor_tensor(ea_parts[rows, q, :], ea_in[rows, q, :], ea_parts[rows, q, :], ALU.subtract).then_inc(ea_lo_done, 1)

            def low_relu(k, q):
                b = SLOTS * k + q
                dve.wait_ge(relu_hi_done, b + 1)
                v.scalar_tensor_tensor(relu_lo[:, q % 2, :], in0=bank[q % 2][:], scalar=0.0, in1=relu_hi[:, q % 2, :],
                                       op0=ALU.max, op1=ALU.subtract).then_inc(relu_lo_done, 1)

            def add_gate(k, q):
                b = SLOTS * k + q
                dve.wait_ge(gate_ready, b + 1)
                v.tensor_tensor(gate_in[:, q % 2, :].rearrange("p (i f) -> p i f", i=2),
                                bank[2 + q % 2][:].rearrange("p (i f) -> p i f", i=2), gath[:, q, :, HID:],
                                ALU.add).then_inc(gate_added, 1)

            def message(k, q):
                b = SLOTS * k + q
                dve.wait_ge(core_ready, b + 1)
                dve.wait_ge(gate_done, b + 1)
                after(dve, msg_lo_done, b - 1)
                v.tensor_tensor(msg[:, q % 2, :], bank[4 + q % 2][:], gate[:, q % 2, :], ALU.mult).then_inc(msg_done, 1)

            def low_message(k, q):
                b = SLOTS * k + q
                dve.wait_ge(msg_hi_done, b + 1)
                v.tensor_tensor(msg_lo[:, q % 2, :, :].rearrange("p i f -> p (i f)"), msg[:, q % 2, :],
                                msg_hi[:, q % 2, :, :].rearrange("p i f -> p (i f)"), ALU.subtract).then_inc(msg_lo_done, 1)

            def add_sums(k, q):
                b = SLOTS * k + q
                w = dve.value_load(win_i[0:1, ds(b, 1)], min_val=0, max_val=WINDOWS - 1)
                dve.wait_ge(sum_ready, b + 1)
                after(dve, sum_added, b)
                rows = hs[:, ds(w, 1), :].rearrange("p o f -> p (o f)")
                v.tensor_tensor(rows, rows, bank[6 + q % 2][:, 0:HID], ALU.add).then_inc(sum_added, 1)

            pipeline(dve, [(message, 3), (low_relu, 2), (add_gate, 2), (low_edges, 0), (low_message, 3), (add_sums, 4)],
                     BLOCKS, SLOTS)
            dve.wait_ge(sum_added, BLOCKS)

            statistics(hs)
            scale_and_shift(2)

            def scale(k, q):
                w = 2 * k + q
                dve.wait_ge(n1_done, w + 1)
                rows = hs[:, ds(w, 1), :].rearrange("p o f -> p (o f)")
                v.tensor_tensor(rows, rows, ln0_sb[:, 0, :], ALU.mult).then_inc(scaled_done, 1)

            def x1_stats(k, q):
                w = 2 * k + q
                dve.wait_ge(x1_done, w + 1)
                row_statistics(xs, w)

            pipeline(dve, [(scale, 0), (x1_stats, 3)], WPAD, 2, straight=True)
            aggregate_statistics(0, WPAD)
            scale_and_shift(3)

            dve.wait_ge(rel_done, 1)
            for h in range(HEADS):
                last = v.scalar_tensor_tensor(rel_parts[RELS:, h * HEAD:(h + 1) * HEAD], in0=rel_sb[RELS:, :], scalar=0.2,
                                              in1=rel_parts[RELS:, h * HEAD:(h + 1) * HEAD], op0=ALU.mult, op1=ALU.subtract)
            last.then_inc(rel_done, 1)

            def low_enhanced(k, q):
                w = 2 * k + q
                dve.wait_ge(ht2_hi_done, w + 1)
                for c in range(2):
                    last = v.scalar_tensor_tensor(ht_lo[:, q, c, :], in0=bank[q][:, c * P:(c + 1) * P], scalar=query_sb[:, c:c + 1],
                                                  in1=ht_hi[:, q, c, :], op0=ALU.add, op1=ALU.subtract)
                last.then_inc(ht2_lo_done, 1)

            def qkv_bias(k, q):
                w = 2 * k + q
                dve.wait_ge(qkv_ready, w + 1)
                if not isinstance(w, int) or w >= 2:
                    dve.wait_ge(kv_stored[q], 16 * k)
                after(dve, q_hi_done, w - 1)
                after(dve, q_lo_done, w - 1)
                v.tensor_tensor(qkv_row[:, q, 0:2 * HID], bank[2 + q][:], b_qkv_sb[:, 0:2 * HID], ALU.add)
                v.tensor_tensor(qkv_row[:, q, 2 * HID:], bank[4 + q][:, 0:HID], b_qkv_sb[:, 2 * HID:], ALU.add).then_inc(qkv_done, 1)

            def low_parts(k, q):
                w = 2 * k + q
                dve.wait_ge(q_hi_done, w + 1)
                hi, lo = (t[:, ds(w, 1), :].rearrange("p o f -> p (o f)") for t in (q_hi, q_lo))
                v.scalar_tensor_tensor(lo, in0=qkv_row[:, q, 2 * HID:], scalar=1 / HEAD ** 0.5, in1=hi,
                                       op0=ALU.mult, op1=ALU.subtract).then_inc(q_lo_done, 1)

            pipeline(dve, [(low_enhanced, 0), (qkv_bias, 1), (low_parts, 2)], WPAD, 2)

            def one_hot_t(k, q):
                b = SLOTS * k + q
                dve.wait_ge(spread_ready, b + 1)
                after(dve, query_ready, b - 1)
                v.tensor_scalar(hot_t[:, q % 2, :, :].rearrange("p k e -> p (k e)"), bank[q % 2][:], iota_part[:], None,
                                ALU.is_equal).then_inc(hot_t_done, 1)

            def products(k, q):
                b = SLOTS * k + q
                dve.wait_ge(key_copied, b + 1)
                dve.wait_ge(query_ready, b + 1)
                after(dve, score_done, b - 1)
                v.tensor_tensor(prod[:, q % 2, :], bank[4 + q % 2][:], key_sb[:, q % 2, :, :].rearrange("p i f -> p (i f)"),
                                ALU.mult).then_inc(prod_done, 1)

            def scores(k, q):
                b = SLOTS * k + q
                dve.wait_ge(prod_done, b + 1)
                v.tensor_reduce(out=exp_col[:, ds(b, 1), :, :].rearrange("p o i h -> p (o i h)"),
                                in_=prod[:, q % 2, :].rearrange("p (j d) -> p j d", d=HEAD), axis=AX.X, op=ALU.add).then_inc(score_done, 1)

            node_phase_over(dve)
            dve.wait_ge(consts, 2)
            pipeline(dve, [(scores, 2), (one_hot_t, 0), (products, 1)], BLOCKS, SLOTS)
            dve.wait_ge(score_done, BLOCKS)
            dve.wait_ge(key_ready, BLOCKS)

            dve.wait_ge(segments_known, 1)
            dve.wait_ge(srow_ready, 1)
            for r in range(2):
                for hp in range(2):
                    for j in range(2):
                        last = v.tensor_tensor(s_row[:, r, 2 * hp + j, :], bank[2 * r + hp][0:HALF_B, j * CHUNK:(j + 1) * CHUNK],
                                               outside[:, r, :], ALU.add)
            step(last)
            for r in range(2):
                rows = m_row[:, r, :, :].rearrange("p h e -> p (h e)")
                step(v.tensor_tensor_scan(rows, reset[:, r, 0:HEADS * CHUNK], s_row[:, r, :, :].rearrange("p h e -> p (h e)"), -BIG, ALU.add, ALU.max))
            for r in range(2):
                rows = m_row[:, r, :, :].rearrange("p h e -> p (h e)")
                last = v.tensor_tensor_scan(rows[:, ::-1], reset[:, r, HEADS * CHUNK:0:-1], rows[:, ::-1], -BIG, ALU.add, ALU.max)
            last.then_inc(local_done, 1)
            dve.wait_ge(lends_ready, 1)
            for i in range(2):
                last = v.tensor_copy(edge_max[:, i, :], bank[4 + i][0:HEADS, 0:BLOCKS])
            step(last)
            v.tensor_tensor_scan(run_max[:, 0, :], through[:, 0, :], edge_max[:, 1, :], -BIG, ALU.add, ALU.max)
            step(v.tensor_tensor_scan(run_max[:, 1, ::-1], through[:, 1, ::-1], edge_max[:, 0, ::-1], -BIG, ALU.add, ALU.max))
            step(v.memset(carry[:], -BIG))
            v.tensor_tensor(carry[:, 0, 1:], run_max[:, 0, 0:BLOCKS - 1], into[:, 0, 1:], ALU.add)
            v.tensor_tensor(carry[:, 1, 0:BLOCKS - 1], run_max[:, 1, 1:], into[:, 1, 0:BLOCKS - 1], ALU.add).then_inc(carried, 1)
            dve.wait_ge(carry_ready, 1)
            step(v.tensor_copy(carry_col[:], bank[6][0:HALF_B, 0:4 * HEADS].rearrange("p (r i h) -> p r i h", r=2, i=2)))
            for i in range(2):
                for r in range(2):
                    for h in range(HEADS):
                        last = v.scalar_tensor_tensor(m_row[:, r, h, :], in0=same[:, r, i, :], scalar=carry_col[:, r, i, h:h + 1],
                                                      in1=m_row[:, r, h, :], op0=ALU.add, op1=ALU.max)
                step(last)
            v.tensor_tensor(m_row[:], s_row[:], m_row[:], ALU.subtract).then_inc(max_done, 1)
            for r in range(2):
                for i in range(2):
                    dve.wait_ge(expt_ready, 2 * r + i + 1)
                    v.tensor_copy(exp_col[:, r * HALF_B:(r + 1) * HALF_B, i, :].rearrange("p b h -> p h b"),
                                  bank[2 * r + i][:, 0:HEADS * HALF_B].rearrange("p (h b) -> p h b", h=HEADS)).then_inc(weights_done, 1)
            dve.wait_ge(weights_done, 4)

            def weight_values(k, q):
                b = 2 * RING * k + q
                if q % 2 == 0:
                    dve.wait_ge(values_in[q // 2], 16 * (k + 1))
                last = v.tensor_tensor(
                    weighted[:, q % RING, :, 0:HID].rearrange("p i (h d) -> p i h d", h=HEADS),
                    values[:, q // 2, q % 2, :].rearrange("p (i h d) -> p i h d", i=2, h=HEADS),
                    exp_col[:, ds(b, 1), :, :].rearrange("p o i h -> p i h o").to_broadcast([P, 2, HEADS, HEAD]), ALU.mult)
                last.then_inc(weighted_done, 1)

            def add_agg(k, q):
                b = 2 * RING * k + q
                w = dve.value_load(win_i[0:1, ds(b, 1)], min_val=0, max_val=WINDOWS - 1)
                dve.wait_ge(agg_ready, b + 1)
                after(dve, agg_added, b)
                rows = agg[:, ds(w, 1), :].rearrange("p o f -> p (o f)")
                v.tensor_tensor(rows, rows, bank[q % RING][:, 0:AGGW], ALU.add).then_inc(agg_added, 1)

            dve.wait_ge(agg_zero, 1)
            pipeline(dve, [(weight_values, 0), (add_agg, 3)], BLOCKS, 2 * RING)
            dve.wait_ge(agg_added, BLOCKS)

            step(v.tensor_scalar(empty[:], agg[:, :, HID:], 0.0, None, ALU.is_equal))
            step(v.tensor_tensor(denom[:], agg[:, :, HID:], empty[:], ALU.add))
            v.reciprocal(inv[:], denom[:]).then_inc(inv_done, 1)
            dve.wait_ge(bo_hi_done, 1)
            v.tensor_tensor(b_o_parts[SHARES:, :], b_o_sb[SHARES:, :], b_o_parts[SHARES:, :], ALU.subtract).then_inc(bo_lo_done, 1)

            def mix(w):
                dve.wait_ge(v_arrived[w % 2], 16 * (w // 2 + 1))
                dve.wait_ge(mean_done, w + 1)
                v.scalar_tensor_tensor(agg[:, w, 0:HID], in0=v_in[:, w % 2, :], scalar=empty[:, w, 0:1], in1=agg[:, w, 0:HID],
                                       op0=ALU.mult, op1=ALU.add).then_inc(mix_done, 1)

            def low_mixed(w):
                dve.wait_ge(mt_hi_done, w + 1)
                v.tensor_tensor(ht_lo[:, w % 2, :, :], bank[w % 2][:, 0:HID].rearrange("p (c n) -> p c n", c=2),
                                ht_hi[:, w % 2, :, :], ALU.subtract).then_inc(mt_lo_done, 1)

            def add_h(w):
                dve.wait_ge(o_ready, w + 1)
                v.tensor_tensor(hs[:, w, :], hs[:, w, :], bank[2 + w % 2][:, 0:HID], ALU.add).then_inc(o_done, 1)

            def out_stats(w):
                dve.wait_ge(o_done, w + 1)
                row_statistics(hs, w)

            for w in range(WINDOWS + 4):
                for stage, lag in ((mix, 0), (low_mixed, 1), (add_h, 3), (out_stats, 4)):
                    if 0 <= w - lag < WINDOWS:
                        stage(w - lag)
                if w == EARLY + 3:
                    aggregate_statistics(0, EARLY)
                if w == EARLY + 5:
                    scale_and_shift(4, slice(0, EARLY))
            aggregate_statistics(EARLY, WINDOWS)
            scale_and_shift(5, slice(EARLY, WINDOWS))
            dve.wait_ge(beta1_added, 1)
            for w in range(EARLY, WINDOWS + 1):
                if w < WINDOWS:
                    dve.wait_ge(x2_normed, w + 1)
                    v.tensor_tensor(hs[:, w, :], hs[:, w, :], ln1_sb[:, 0, :], ALU.mult).then_inc(x2_scaled, 1)
                if w > EARLY:
                    dve.wait_ge(x2_scaled, w - EARLY)
                    v.tensor_tensor(hs[:, w - 1, :], hs[:, w - 1, :], xs[:, w - 1, :], ALU.add).then_inc(y_late_done, 1)

        @block.tensor
        def _(pe):
            def mm(out_, lhs, rhs, start, stop):
                return nc.tensor.matmul(out_, lhsT=lhs, rhs=rhs, start=start, stop=stop)

            def tr(out_, in_, start=True, stop=True):
                return nc.tensor.matmul(out_, lhsT=in_, rhs=ident[:], is_transpose=True, start=start, stop=stop)

            pe.wait_ge(consts, 1)
            pe.wait_ge(counted, 2)
            mm(bank[0][0:HALF_C, 0:2], upto[:], count[:], True, False)
            mm(bank[0][0:HALF_C, 1:2], ones_c[:, 0:HALF_C], count[:, 0:1], False, True).then_inc(cumulated, 1)
            pe.wait_ge(sel_ready, 1)
            for c in range(2):
                mm(bank[0][0:1, 0:BLOCKS], ones_c[:, 0:1], passed[:, c, :], c == 0, c == 1)
            for c in range(2):
                mm(bank[1][0:1, 0:BLOCKS], jump[:, c:c + 1], passed[:, c, :], c == 0, c == 1)
            for c in range(2):
                last = mm(bank[2][0:1, 0:BLOCKS], ones_c[:, 0:1], chosen[:, c, :], c == 0, c == 1)
            last.then_inc(rows_ready, 1)
            pe.wait_ge(off_ready, 1)
            for i in range(2):
                cols = slice(i * BLOCKS, (i + 1) * BLOCKS)
                for c in range(2):
                    mm(bank[0][:, cols], nat_f[:, 0, c, i * P:(i + 1) * P], chosen[:, c, :], c == 0, c == 1)
                for c in range(2):
                    mm(bank[1][:, cols], nat_f[:, 1, c, i * P:(i + 1) * P], chosen[:, c, :], c == 0, False)
                mm(bank[1][:, cols], ones_c[0:1, 0:P], neg_off[:], False, True)
                e = i * (CHUNK - 1)
                for c in range(2):
                    mm(bank[4][0:HEADS, cols], nat_f[:, 1, c, e:e + 1].to_broadcast([HALF_C, HEADS]), chosen[:, c, :], c == 0, c == 1)
            for r in range(2):
                some = slice(r * HALF_B, (r + 1) * HALF_B)
                cols = slice(r * CHUNK, (r + 1) * CHUNK)
                for c in range(2):
                    mm(bank[2][0:HALF_B, cols], chosen[:, c, some], nat_f[:, 1, c, :], c == 0, False)
                mm(bank[2][0:HALF_B, cols], neg_off[0:1, some], ones_c[0:1, :], False, True)
                for c in range(2):
                    last = mm(bank[3][0:HALF_B, cols], chosen[:, c, some], nat_f[:, 2, c, :], c == 0, c == 1)
            last.then_inc(cols_ready, 1)
            pe.wait_ge(meta_ready, 1)
            pe.wait_ge(w_in, 9 * 16)

            def transpose_rows(rows, source_done, freed, ready):
                def stage(k, q):
                    w = 2 * k + q
                    pe.wait_ge(source_done, w + 1)
                    after(pe, freed, w - 1)
                    for c in range(2):
                        last = tr(bank[q][:, c * P:(c + 1) * P], rows[:, w, c * P:(c + 1) * P], c == 0, c == 1)
                    last.then_inc(ready, 1)
                return stage

            def three_products(to, q, hi, lo, cols, stop=True):
                for c in range(2):
                    mm(to, ht_hi[:, q, c, :], hi[:, c, cols], c == 0, False)
                    mm(to, ht_hi[:, q, c, :], lo[:, c, cols], False, False)
                    last = mm(to, ht_lo[:, q, c, :], hi[:, c, cols], False, stop and c == 1)
                return last

            def project_nodes(k, q):
                w = 2 * k + q
                pe.wait_ge(ht_lo_done, w + 1)
                after(pe, row_ready, w - 1)
                three_products(bank[2 + q][:], q, w_node_hi, w_node_lo, slice(0, 2 * HID)).then_inc(proj_ready, 1)

            pe.wait_ge(w_lo_done, 2)
            pipeline(pe, [(transpose_rows(hs, h_done, ht_lo_done, ht_ready), 0), (project_nodes, 1)], WPAD, 2, straight=True)
            pe.wait_ge(row_ready, WPAD)
            pe.wait_ge(share_done, 1)

            def edge_inputs(k, q):
                b = SLOTS * k + q
                pe.wait_ge(gath_in[q], 32 * (k + 1))
                pe.wait_ge(ea_lo_done, b + 1)
                for m in range(2):
                    to = bank[q % 2][:, m * CHUNK:(m + 1) * CHUNK]
                    for i in range(2):
                        tr(to[:, i * P:(i + 1) * P], gath[:, q, i, m * P:(m + 1) * P], i == 0, False)
                    mm(to, w_edge_hi[:, m * P:(m + 1) * P], ea_parts[:, q, :], False, False)
                    last = mm(to, w_edge_lo[:, m * P:(m + 1) * P], ea_parts[:, q, :], False, True)
                last.then_inc(z_ready, 1)
                for i in range(2):
                    to = bank[2 + q % 2][:, i * HID:(i + 1) * HID]
                    mm(to, ea_parts[:, q, i * P:(i + 1) * P], w_edge_hi[:, HID:], True, False)
                    last = mm(to, ea_parts[:, q, i * P:(i + 1) * P], w_edge_lo[:, HID:], False, True)
                last.then_inc(gate_ready, 1)

            def core(k, q):
                b = SLOTS * k + q
                pe.wait_ge(relu_lo_done, b + 1)
                for i in range(2):
                    to = bank[4 + q % 2][:, i * HID:(i + 1) * HID]
                    mm(to, share[:], b2_parts[:], True, False)
                    for c in range(2):
                        tile = slice(c * CHUNK + i * P, c * CHUNK + (i + 1) * P)
                        mm(to, relu_hi[:, q % 2, tile], w2_hi[:, c, :], False, False)
                        mm(to, relu_hi[:, q % 2, tile], w2_lo[:, c, :], False, False)
                        last = mm(to, relu_lo[:, q % 2, tile], w2_hi[:, c, :], False, c == 1)
                last.then_inc(core_ready, 1)

            def sum_messages(k, q):
                b = SLOTS * k + q
                pe.wait_ge(msg_lo_done, b + 1)
                pe.wait_ge(hot_done, b + 1)
                to = bank[6 + q % 2][:, 0:HID]
                for i in range(2):
                    mm(to, hot[:, q % 2, i, :], msg_hi[:, q % 2, i, :], i == 0, False)
                    last = mm(to, hot[:, q % 2, i, :], msg_lo[:, q % 2, i, :], False, i == 1)
                last.then_inc(sum_ready, 1)

            pipeline(pe, [(edge_inputs, 0), (sum_messages, 3), (core, 1)], BLOCKS, SLOTS)
            pe.wait_ge(sum_added, BLOCKS)
            pe.wait_ge(rel_in, 5 * 16)

            def project_qkv(k, q):
                w = 2 * k + q
                pe.wait_ge(ht2_lo_done, w + 1)
                after(pe, qkv_done, w - 1)
                three_products(bank[2 + q][:], q, wqkv_hi, wqkv_lo, slice(0, 2 * HID))
                three_products(bank[4 + q][:, 0:HID], q, wqkv_hi, wqkv_lo, slice(2 * HID, 3 * HID)).then_inc(qkv_ready, 1)

            pe.wait_ge(wqkv_lo_done, 1)
            pipeline(pe, [(transpose_rows(hs, h2_done, ht2_lo_done, ht2_ready), 0), (project_qkv, 1)], WPAD, 2, straight=True)
            pe.wait_ge(qkv_done, WPAD)
            pe.wait_ge(q_lo_done, WPAD)
            pe.wait_ge(rel_done, 2)
            pe.wait_ge(consts, 2)

            def spread_row(k, q):
                b = SLOTS * k + q
                pe.wait_ge(brow_in[q], 16 * (k + 1))
                after(pe, hot_t_done, b - 1)
                mm(bank[q % 2][:], spread[:], block_row[:, q, :, :].rearrange("p k e -> p (k e)"), True, True).then_inc(spread_ready, 1)

            def keys_and_queries(k, q):
                b = SLOTS * k + q
                pe.wait_ge(gath1_in[q], 32 * (k + 1))
                pe.wait_ge(hot_t_done, b + 1)
                after(pe, key_copied, b - 1)
                for i in range(2):
                    to = bank[2 + q % 2][:, i * HID:(i + 1) * HID]
                    mm(to, ident[:], gath[:, q, i, 0:HID], True, False)
                    last = mm(to, hot_t[:, q % 2, 1, i * P:(i + 1) * P], rel_parts[:], False, True)
                last.then_inc(key_ready, 1)
                after(pe, prod_done, b - 1)
                w = pe.value_load(win_i[0:1, ds(b, 1)], min_val=0, max_val=WINDOWS - 1)
                for i in range(2):
                    to = bank[4 + q % 2][:, i * HID:(i + 1) * HID]
                    for table in (q_hi, q_lo):
                        last = mm(to, hot_t[:, q % 2, 0, i * P:(i + 1) * P], table[:, ds(w, 1), :].rearrange("p o f -> p (o f)"),
                                  table is q_hi, table is q_lo)
                last.then_inc(query_ready, 1)

            pipeline(pe, [(spread_row, 0), (keys_and_queries, 1)], BLOCKS, SLOTS)

            pe.wait_ge(score_done, BLOCKS)
            for r in range(2):
                for h in range(HEADS):
                    for i in range(2):
                        at = (h % 2) * CHUNK + i * P
                        last = tr(bank[2 * r + h // 2][0:HALF_B, at:at + P], exp_col[:, r * HALF_B:(r + 1) * HALF_B, i, h])
            last.then_inc(srow_ready, 1)
            pe.wait_ge(local_done, 1)
            for i, e in enumerate((0, CHUNK - 1)):
                for r in range(2):
                    last = mm(bank[4 + i][0:HEADS, r * HALF_B:(r + 1) * HALF_B], m_row[:, r, :, e], ident[0:HALF_B, 0:HALF_B], True, True)
            last.then_inc(lends_ready, 1)
            pe.wait_ge(carried, 1)
            for r in range(2):
                for i in range(2):
                    at = (2 * r + i) * HEADS
                    last = mm(bank[6][0:HALF_B, at:at + HEADS], carry[:, i, r * HALF_B:(r + 1) * HALF_B], ident[0:HEADS, 0:HEADS], True, True)
            last.then_inc(carry_ready, 1)
            pe.wait_ge(exp_done, 1)
            for r in range(2):
                for i in range(2):
                    for h in range(HEADS):
                        last = nc.tensor.matmul(bank[2 * r + i][:, h * HALF_B:(h + 1) * HALF_B], lhsT=m_row[:, r, h, i * P:(i + 1) * P],
                                                rhs=ident[0:HALF_B, 0:HALF_B], is_transpose=True, start=True, stop=True)
                    last.then_inc(expt_ready, 1)
            pe.wait_ge(weights_done, 4)

            def aggregate(k, q):
                b = 2 * RING * k + q
                pe.wait_ge(hot1_done, b + 1)
                pe.wait_ge(weighted_done, b + 1)
                for i in range(2):
                    last = mm(bank[q % RING][:, 0:AGGW], hot1[:, q % RING, i, :], weighted[:, q % RING, i, :], i == 0, i == 1)
                last.then_inc(agg_ready, 1)

            pipeline(pe, [(aggregate, 0)], BLOCKS, 2 * RING)
            pe.wait_ge(agg_added, BLOCKS)

            pe.wait_ge(bo_lo_done, 1)
            for w in range(WINDOWS + 2):
                if w < WINDOWS:
                    q = w % 2
                    pe.wait_ge(mix_done, w + 1)
                    after(pe, mt_lo_done, w - 1)
                    for c in range(2):
                        last = tr(bank[q][:, c * P:(c + 1) * P], agg[:, w, c * P:(c + 1) * P], c == 0, c == 1)
                    last.then_inc(mt_ready, 1)
                if w >= 2:
                    q = w % 2
                    pe.wait_ge(mt_lo_done, w - 1)
                    after(pe, o_done, w - 3)
                    to = bank[2 + q][:, 0:HID]
                    three_products(to, q, wo_hi, wo_lo, slice(0, HID), stop=False)
                    mm(to, share[:], b_o_parts[:], False, True).then_inc(o_ready, 1)


def kernel(x, src, dst, edge_attr_64, edge_type_64, L0_gnn_W1, L0_gnn_b1, L0_gnn_W2, L0_gnn_b2, L0_gnn_Wg, L0_gnn_bg,
           L0_gnn_gamma, L0_gnn_beta, L1_gnn_query_emb, L1_gnn_Wq, L1_gnn_bq, L1_gnn_Wk, L1_gnn_bk, L1_gnn_Wv,
           L1_gnn_bv, L1_gnn_rel_w, L1_gnn_Wo, L1_gnn_bo, L1_gnn_gamma, L1_gnn_beta):
    import numpy as np
    import concourse.bacc as bacc
    from concourse import mybir as mb
    from concourse.bass_utils import run_bass_kernel_spmd

    def rows(a, n, fill):
        a = np.asarray(a)
        full = np.full((n * CHUNK,) + a.shape[1:], fill, a.dtype)
        full[:a.shape[0]] = a
        return full.reshape((n, CHUNK) + a.shape[1:])

    def col(a):
        return np.ascontiguousarray(np.asarray(a).reshape(2, P).T)

    x = np.asarray(x)
    x_pad = np.zeros((WPAD * P, HID), x.dtype)
    x_pad[:NODES] = x
    arrays = {
        "x": x_pad,
        "src": rows(src, CHUNKS + 1, 0),
        "dst": rows(dst, CHUNKS + 1, NO_NODE),
        "etype": rows(edge_type_64, CHUNKS + 1, 0),
        "ea": np.ascontiguousarray(rows(edge_attr_64, CHUNKS, 0).transpose(0, 2, 1)),
        "w1": np.asarray(L0_gnn_W1),
        "wg": np.asarray(L0_gnn_Wg),
        "b_cat": np.concatenate([np.asarray(L0_gnn_b1), np.asarray(L0_gnn_bg)])[None, :],
        "w2": np.asarray(L0_gnn_W2),
        "b2": np.asarray(L0_gnn_b2)[None, :],
        "ln0": np.stack([np.asarray(L0_gnn_gamma), np.asarray(L0_gnn_beta)]),
        "query_col": col(L1_gnn_query_emb),
        "wqkv": np.concatenate([np.asarray(a) for a in (L1_gnn_Wk, L1_gnn_Wv, L1_gnn_Wq)], axis=1),
        "b_qkv": np.concatenate([np.asarray(a) for a in (L1_gnn_bk, L1_gnn_bv, L1_gnn_bq)])[None, :],
        "rel": np.asarray(L1_gnn_rel_w),
        "wo": np.asarray(L1_gnn_Wo),
        "b_o": np.asarray(L1_gnn_bo)[None, :],
        "ln1": np.stack([np.asarray(L1_gnn_gamma), np.asarray(L1_gnn_beta)]),
    }
    nc = bacc.Bacc("TRN2", target_bir_lowering=False, num_devices=1)
    args = [nc.dram_tensor(f"in_{name}", a.shape, mb.dt.from_np(a.dtype), kind="ExternalInput").ap() for name, a in arrays.items()]
    result = nc.dram_tensor("out_x", (NODES, HID), mb.dt.float32, kind="ExternalOutput").ap()
    build(nc, *args, result)
    got = run_bass_kernel_spmd(nc, [{f"in_{name}": a for name, a in arrays.items()}], core_ids=[0])
    return got.results[0]["out_x"]
```
